# Optimizing a Trainium2 kernel written in Bass

```python
import numpy as np
import jax
import jax.numpy as jnp

def _softmax(x, axis=-1):
    return jax.nn.softmax(x, axis=axis)

def _gelu(x):
    return jax.nn.gelu(x, approximate=True)

def _silu(x):
    return jax.nn.silu(x)

def _sigmoid(x):
    return jax.nn.sigmoid(x)

def _layernorm(x, axis=-1, eps=1e-05):
    m = jnp.mean(x, axis=axis, keepdims=True)
    v = jnp.var(x, axis=axis, keepdims=True)
    return (x - m) / jnp.sqrt(v + eps)

def _scatter_add(tgt, idx, src, axis=0):
    return tgt.at[idx].add(src)

def _segment_sum(src, seg, n):
    return jax.ops.segment_sum(src, seg, n)
kernel_name = 'mk_macaron_d2_jaxref_r8_ae9e1a'

def setup_inputs(seed: int=0):
    np.random.seed(seed)
    _w = jnp.asarray

    def _L0_attn_setup():
        import jax, jax.numpy as jnp
        import numpy as np
        N_HEAD = 16
        key = jax.random.key(seed)
        ks = jax.random.split(key, 9)
        H = 256

        def w(k, shape, scale=0.02):
            return jax.random.normal(k, shape, dtype=jnp.float32) * scale
        return {'h': jax.random.normal(ks[0], (4, 256, H), dtype=jnp.float32), 'Wq': w(ks[1], (H, H)), 'bq': w(ks[2], (H,)), 'Wk': w(ks[3], (H, H)), 'bk': w(ks[4], (H,)), 'Wv': w(ks[5], (H, H)), 'bv': w(ks[6], (H,)), 'Wo': w(ks[7], (H, H)), 'bo': w(ks[8], (H,))}
    _L0_attn_in = _L0_attn_setup()

    def _L0_ffn_setup():
        import jax, jax.numpy as jnp
        import numpy as np
        D_MODEL = 256
        D_FF = 1024

        def absmean_quant(w):
            scale = jnp.mean(jnp.abs(w))
            mask = (jnp.abs(w) >= scale * 0.7).astype(w.dtype)
            return jnp.sign(w) * mask
        key = jax.random.key(seed)
        k_x, k_w1, k_w2 = jax.random.split(key, 3)
        x = jax.random.normal(k_x, (4, 512, D_MODEL), dtype=jnp.float32)
        w1 = jax.random.normal(k_w1, (D_FF, D_MODEL), dtype=jnp.float32)
        b1 = jnp.zeros((D_FF,), dtype=jnp.float32)
        w2 = jax.random.normal(k_w2, (D_MODEL, D_FF), dtype=jnp.float32)
        b2 = jnp.zeros((D_MODEL,), dtype=jnp.float32)
        return {'x': x, 'w1': w1, 'b1': b1, 'w2': w2, 'b2': b2}
    _L0_ffn_in = _L0_ffn_setup()

    def _L1_attn_setup():
        import jax, jax.numpy as jnp
        import numpy as np
        NHEADS = 16
        SCALE_BASE = 512.0
        EPS = 1e-05

        def _rotate_every_two(x):
            x1 = x[..., ::2]
            x2 = x[..., 1::2]
            return jnp.stack([-x2, x1], axis=-1).reshape(x.shape)

        def _xpos(x, offset=0):
            B, T, C = x.shape
            dim_scale = (jnp.arange(0, C, 2, dtype=jnp.float32) + 0.4 * C) / (1.4 * C)
            pos = jnp.arange(offset, offset + T, dtype=jnp.float32)
            scale = dim_scale[None, :] ** (pos[:, None] / SCALE_BASE)
            inv_freq = 1.0 / 10000.0 ** (jnp.arange(0, C, 2, dtype=jnp.float32) / C)
            sinusoid = pos[:, None] * inv_freq[None, :]
            sin = jnp.repeat(jnp.sin(sinusoid) * scale, 2, axis=-1)
            cos = jnp.repeat(jnp.cos(sinusoid) * scale, 2, axis=-1)
            return x * cos[None] + _rotate_every_two(x) * sin[None]

        def _decay_mask(H, T, dtype):
            gamma = 1.0 - 2.0 ** (-5.0 - jnp.arange(H, dtype=jnp.float32))
            idx = jnp.arange(T)
            diff = idx[:, None] - idx[None, :]
            exp = jnp.where(diff >= 0, diff, 0).astype(jnp.float32)
            mask = jnp.where(diff[None] >= 0, gamma[:, None, None] ** exp[None], 0.0)
            return (mask.astype(dtype), gamma)
        key = jax.random.key(seed)
        ks = jax.random.split(key, 4)
        B, T, C = (4, 128, 256)
        s = 0.02
        return {'x': jax.random.normal(ks[0], (B, T, C), dtype=jnp.float32), 'w_qkv': jax.random.normal(ks[1], (C, 3 * C), dtype=jnp.float32) * s, 'w_g': jax.random.normal(ks[2], (C, C), dtype=jnp.float32) * s, 'w_proj': jax.random.normal(ks[3], (C, C), dtype=jnp.float32) * s, 'gn_weight': jnp.ones((C,), dtype=jnp.float32), 'gn_bias': jnp.zeros((C,), dtype=jnp.float32)}
    _L1_attn_in = _L1_attn_setup()

    def _L1_ffn_setup():
        import jax, jax.numpy as jnp
        import numpy as np
        B, S, D = (4, 128, 256)
        H = 512
        NE = 8
        TOPK = 2
        key = jax.random.key(seed)
        ks = jax.random.split(key, 9)
        s = lambda fan_in: 1.0 / np.sqrt(fan_in)
        return {'x': jax.random.normal(ks[0], (B, S, D), dtype=jnp.float32), 'W1': jax.random.normal(ks[1], (NE, D, H), dtype=jnp.float32) * s(D), 'b1': jnp.zeros((NE, H), dtype=jnp.float32), 'W2': jax.random.normal(ks[2], (NE, H, H), dtype=jnp.float32) * s(H), 'b2': jnp.zeros((NE, H), dtype=jnp.float32), 'W3': jax.random.normal(ks[3], (NE, H, D), dtype=jnp.float32) * s(H), 'b3': jnp.zeros((NE, D), dtype=jnp.float32), 'Wg': jax.random.normal(ks[4], (D, NE), dtype=jnp.float32) * s(D), 'bg': jnp.zeros((NE,), dtype=jnp.float32)}
    _L1_ffn_in = _L1_ffn_setup()
    _d = {'L0_attn_h': _L0_attn_in['h'], 'L0_attn_Wq': _L0_attn_in['Wq'], 'L0_attn_bq': _L0_attn_in['bq'], 'L0_attn_Wk': _L0_attn_in['Wk'], 'L0_attn_bk': _L0_attn_in['bk'], 'L0_attn_Wv': _L0_attn_in['Wv'], 'L0_attn_bv': _L0_attn_in['bv'], 'L0_attn_Wo': _L0_attn_in['Wo'], 'L0_attn_bo': _L0_attn_in['bo'], 'L0_ffn_w1': _L0_ffn_in['w1'], 'L0_ffn_b1': _L0_ffn_in['b1'], 'L0_ffn_w2': _L0_ffn_in['w2'], 'L0_ffn_b2': _L0_ffn_in['b2'], 'L1_attn_w_qkv': _L1_attn_in['w_qkv'], 'L1_attn_w_g': _L1_attn_in['w_g'], 'L1_attn_w_proj': _L1_attn_in['w_proj'], 'L1_attn_gn_weight': _L1_attn_in['gn_weight'], 'L1_attn_gn_bias': _L1_attn_in['gn_bias'], 'L1_ffn_W1': _L1_ffn_in['W1'], 'L1_ffn_b1': _L1_ffn_in['b1'], 'L1_ffn_W2': _L1_ffn_in['W2'], 'L1_ffn_b2': _L1_ffn_in['b2'], 'L1_ffn_W3': _L1_ffn_in['W3'], 'L1_ffn_b3': _L1_ffn_in['b3'], 'L1_ffn_Wg': _L1_ffn_in['Wg'], 'L1_ffn_bg': _L1_ffn_in['bg']}
    _x0 = _d['L0_attn_h']
    _d['L0_attn_h'] = jax.random.normal(jax.random.fold_in(jax.random.key(seed), 1), (2, 1024, 256), dtype=_x0.dtype)
    del _x0
    return _d

def reference(L0_attn_h, L0_attn_Wq, L0_attn_bq, L0_attn_Wk, L0_attn_bk, L0_attn_Wv, L0_attn_bv, L0_attn_Wo, L0_attn_bo, L0_ffn_w1, L0_ffn_b1, L0_ffn_w2, L0_ffn_b2, L1_attn_w_qkv, L1_attn_w_g, L1_attn_w_proj, L1_attn_gn_weight, L1_attn_gn_bias, L1_ffn_W1, L1_ffn_b1, L1_ffn_W2, L1_ffn_b2, L1_ffn_W3, L1_ffn_b3, L1_ffn_Wg, L1_ffn_bg):

    def _L0_attn_ref(h, Wq, bq, Wk, bk, Wv, bv, Wo, bo):
        import jax, jax.numpy as jnp
        import numpy as np
        N_HEAD = 16
        B, S, H = h.shape
        nh = N_HEAD
        hd = H // nh
        q = (h @ Wq.T + bq).reshape(B, S, nh, hd)
        k = (h @ Wk.T + bk).reshape(B, S, nh, hd)
        v = (h @ Wv.T + bv).reshape(B, S, nh, hd)
        scale = 1.0 / jnp.sqrt(jnp.float32(hd))
        scores = jnp.einsum('bqhd,bkhd->bhqk', q, k) * scale
        causal = jnp.tril(jnp.ones((S, S), dtype=bool))
        scores = jnp.where(causal, scores, jnp.finfo(scores.dtype).min)
        attn = jax.nn.softmax(scores, axis=-1)
        o = jnp.einsum('bhqk,bkhd->bqhd', attn, v).reshape(B, S, H)
        return o @ Wo.T + bo

    def _L0_ffn_ref(x, w1, b1, w2, b2):
        import jax, jax.numpy as jnp
        import numpy as np
        D_MODEL = 256
        D_FF = 1024

        def absmean_quant(w):
            scale = jnp.mean(jnp.abs(w))
            mask = (jnp.abs(w) >= scale * 0.7).astype(w.dtype)
            return jnp.sign(w) * mask
        w1_q = absmean_quant(w1)
        w2_q = absmean_quant(w2)
        h = jnp.einsum('bsd,fd->bsf', x, w1_q) + b1
        h = jax.nn.gelu(h, approximate=False)
        out = jnp.einsum('bsf,df->bsd', h, w2_q) + b2
        return out

    def _L1_attn_ref(x, w_qkv, w_g, w_proj, gn_weight, gn_bias):
        import jax, jax.numpy as jnp
        import numpy as np
        NHEADS = 16
        SCALE_BASE = 512.0
        EPS = 1e-05

        def _rotate_every_two(x):
            x1 = x[..., ::2]
            x2 = x[..., 1::2]
            return jnp.stack([-x2, x1], axis=-1).reshape(x.shape)

        def _xpos(x, offset=0):
            B, T, C = x.shape
            dim_scale = (jnp.arange(0, C, 2, dtype=jnp.float32) + 0.4 * C) / (1.4 * C)
            pos = jnp.arange(offset, offset + T, dtype=jnp.float32)
            scale = dim_scale[None, :] ** (pos[:, None] / SCALE_BASE)
            inv_freq = 1.0 / 10000.0 ** (jnp.arange(0, C, 2, dtype=jnp.float32) / C)
            sinusoid = pos[:, None] * inv_freq[None, :]
            sin = jnp.repeat(jnp.sin(sinusoid) * scale, 2, axis=-1)
            cos = jnp.repeat(jnp.cos(sinusoid) * scale, 2, axis=-1)
            return x * cos[None] + _rotate_every_two(x) * sin[None]

        def _decay_mask(H, T, dtype):
            gamma = 1.0 - 2.0 ** (-5.0 - jnp.arange(H, dtype=jnp.float32))
            idx = jnp.arange(T)
            diff = idx[:, None] - idx[None, :]
            exp = jnp.where(diff >= 0, diff, 0).astype(jnp.float32)
            mask = jnp.where(diff[None] >= 0, gamma[:, None, None] ** exp[None], 0.0)
            return (mask.astype(dtype), gamma)
        B, T, C = x.shape
        H = NHEADS
        D = C // H
        qkv = x @ w_qkv
        q, k, v = jnp.split(qkv, 3, axis=-1)
        q = _xpos(q, offset=0)
        k = _xpos(k, offset=0)
        q = q.reshape(B, T, H, D).transpose(0, 2, 1, 3)
        k = k.reshape(B, T, H, D).transpose(0, 2, 1, 3)
        v = v.reshape(B, T, H, D).transpose(0, 2, 1, 3)
        mask, _ = _decay_mask(H, T, x.dtype)
        scores = jnp.einsum('bhtd,bhsd->bhts', q, k) * D ** (-0.5)
        scores = scores * mask[None]
        y = jnp.einsum('bhts,bhsd->bhtd', scores, v)
        yg = y.transpose(0, 2, 1, 3).reshape(B * T, H, D)
        mu = jnp.mean(yg, axis=-1, keepdims=True)
        var = jnp.var(yg, axis=-1, keepdims=True)
        yn = (yg - mu) / jnp.sqrt(var + EPS)
        yn = yn.reshape(B * T, C) * gn_weight[None] + gn_bias[None]
        yn = yn.reshape(B, T, C)
        out = jax.nn.silu(x @ w_g) * yn
        return out @ w_proj

    def _L1_ffn_ref(x, W1, b1, W2, b2, W3, b3, Wg, bg):
        import jax, jax.numpy as jnp
        import numpy as np
        B, S, D = (4, 128, 256)
        H = 512
        NE = 8
        TOPK = 2
        gate_logits = jnp.einsum('bsd,dn->bsn', x, Wg) + bg
        gate_weights = jax.nn.softmax(gate_logits, axis=-1)
        topv, topi = jax.lax.top_k(gate_weights, TOPK)
        h = jax.nn.gelu(jnp.einsum('bsd,ndh->nbsh', x, W1) + b1[:, None, None, :], approximate=False)
        h = jax.nn.gelu(jnp.einsum('nbsh,nhf->nbsf', h, W2) + b2[:, None, None, :], approximate=False)
        eo = jnp.einsum('nbsf,nfd->nbsd', h, W3) + b3[:, None, None, :]
        comb = jnp.sum(jax.nn.one_hot(topi, NE, dtype=x.dtype) * topv[..., None], axis=-2)
        out = jnp.einsum('nbsd,bsn->bsd', eo, comb)
        return out
    x = L0_attn_h
    x = x + 0.5 * _L0_ffn_ref(_layernorm(x, axis=-1), L0_ffn_w1, L0_ffn_b1, L0_ffn_w2, L0_ffn_b2)
    x = x + _L0_attn_ref(_layernorm(x, axis=-1), L0_attn_Wq, L0_attn_bq, L0_attn_Wk, L0_attn_bk, L0_attn_Wv, L0_attn_bv, L0_attn_Wo, L0_attn_bo)
    x = x + 0.5 * _L0_ffn_ref(_layernorm(x, axis=-1), L0_ffn_w1, L0_ffn_b1, L0_ffn_w2, L0_ffn_b2)
    x = x + 0.5 * _L1_ffn_ref(_layernorm(x, axis=-1), L1_ffn_W1, L1_ffn_b1, L1_ffn_W2, L1_ffn_b2, L1_ffn_W3, L1_ffn_b3, L1_ffn_Wg, L1_ffn_bg)
    x = x + _L1_attn_ref(_layernorm(x, axis=-1), L1_attn_w_qkv, L1_attn_w_g, L1_attn_w_proj, L1_attn_gn_weight, L1_attn_gn_bias)
    x = x + 0.5 * _L1_ffn_ref(_layernorm(x, axis=-1), L1_ffn_W1, L1_ffn_b1, L1_ffn_W2, L1_ffn_b2, L1_ffn_W3, L1_ffn_b3, L1_ffn_Wg, L1_ffn_bg)
    return x

_drawn_inputs = setup_inputs


def setup_inputs(seed=0):
    import zlib

    import numpy as np

    out = dict(_drawn_inputs(seed))
    spreads = {'L0_ffn_b1': (0.0, 0.8),
     'L0_ffn_b2': (0.0, 2.0),
     'L1_attn_gn_weight': (1.0, 0.6),
     'L1_attn_gn_bias': (0.0, 2.0),
     'L1_ffn_b1': (0.0, 0.8),
     'L1_ffn_b2': (0.0, 2.0),
     'L1_ffn_b3': (0.0, 2.0),
     'L1_ffn_bg': (0.0, 0.8)}
    factors = {'L0_attn_Wq': 8.0,
     'L0_attn_bq': 35.493,
     'L0_attn_Wk': 8.0,
     'L0_attn_bk': 64.0,
     'L0_attn_Wv': 8.0,
     'L0_attn_bv': 38.892,
     'L0_attn_Wo': 8.0,
     'L0_attn_bo': 64.0,
     'L1_attn_w_qkv': 8.0,
     'L1_attn_w_g': 8.0,
     'L1_attn_w_proj': 8.0,
     'L1_ffn_W1': 8.0,
     'L1_ffn_W2': 8.0,
     'L1_ffn_W3': 8.0,
     'L1_ffn_Wg': 8.0}
    for name, (base, spread) in spreads.items():
        noise = np.random.default_rng([zlib.crc32(name.encode()), seed]).standard_normal(out[name].shape)
        drawn = base * np.exp(spread * noise) if base else spread * noise
        out[name] = jnp.asarray(drawn.astype(out[name].dtype))
    for name, factor in factors.items():
        out[name] = (out[name] * factor).astype(out[name].dtype)
    return out
```

```python
from contextlib import ExitStack

import numpy as np

import concourse.bass as bass
from concourse import mybir

P = 128
F32 = mybir.dt.float32
F16 = mybir.dt.float16
BF16 = mybir.dt.bfloat16
I32 = mybir.dt.int32
ALU = mybir.AluOpType
ACT = mybir.ActivationFunctionType
AX = mybir.AxisListType

B, S, D = 2, 1024, 256
T = B * S
NT = T // P
KD = D // P
F0 = 1024
NF = F0 // P
GT = 4
NG = NT // GT
EPS = 1e-5
YS = 256.0


class Signal:

    def __init__(self, sem):
        self.sem, self.past, self.links = sem, 0, 0

    def at(self, n):
        return n + self.past

    def phase_over(self, n):
        self.past += n


def buffers(nc, ctx):
    def sb(name, shape, dt):
        used = sb.used[name] = sb.used.get(name, 0) + 1
        return ctx.enter_context(nc.sbuf_tensor(name if used == 1 else f"{name}_{used}", shape, dt))
    sb.used = USED
    return sb


USED = {}


def due(n):
    return not isinstance(n, int) or n > 0


class Memory:
    pass


def layer_norm_steps(nc, dve, m, link, x, y, n, scale):
    def stats():
        for i in range(n):
            ins = nc.vector.bn_stats(m.bn[:, i, :], x[:, i, :])
        link(ins)

    def aggregate():
        for i in range(n):
            ins = nc.vector.bn_aggr(m.mv[:, i, :], m.bn[:, i, :])
        link(ins)
        v, r = m.var[:, 0:n], m.rstd[:, 0:n]
        link(nc.vector.tensor_scalar(v, m.mv[:, 0:n, 1], EPS, 1.0 / (scale * scale), ALU.add, ALU.mult))
        return guess_root(nc, link, v, r)

    def apply():
        for i in range(n):
            ins = nc.vector.tensor_scalar(y[:, i, :], x[:, i, :], m.mv[:, i, 0:1], m.rstd[:, i:i + 1],
                                          ALU.subtract, ALU.mult)
        return ins
    return stats, aggregate, apply


def guess_root(nc, link, v, r):
    link(nc.vector.tensor_scalar(r.bitcast(I32), v.bitcast(I32), 1, None, ALU.arith_shift_right))
    return nc.vector.tensor_scalar(r.bitcast(I32), r.bitcast(I32), -1.0, float(0x5f3759df), ALU.mult, ALU.add)


def refine_root(nc, link, v, r, t):
    for step in range(3):
        link(nc.gpsimd.tensor_tensor(t, r, r, ALU.mult))
        link(nc.gpsimd.tensor_tensor(t, t, v, ALU.mult))
        link(nc.gpsimd.tensor_scalar(t, t, -0.5, 1.5, ALU.mult, ALU.add))
        ins = nc.gpsimd.tensor_tensor(r, r, t, ALU.mult)
        if step < 2:
            link(ins)
    return ins


def linker(eng, signal):
    signal.links = 0

    def link(ins):
        signal.links += 1
        ins.then_inc(signal.sem, 1)
        eng.wait_ge(signal.sem, signal.at(signal.links))
    return link


def quantize_phase(nc, m, a, sig):
    with ExitStack() as ctx:
        sb = buffers(nc, ctx)

        w1n = sb("w1_natural", [P, NF, D], F32)
        w2n = sb("w2_natural", [P, KD, F0], F32)
        below = sb("below", [P, NF * D], F16)
        q1 = sb("w1_quantized", [P, NF, D], F16)
        q2 = sb("w2_quantized", [P, KD, F0], F16)
        absw = sb("abs_w", [P, NF * D], F32)
        rows = sb("row_sums", [P, 2], F32)
        thr = sb("threshold", [P, 4], F32)
        loaded, xs = sig("q_loaded"), sig("x_loaded")
        summed, total, chain = sig("q_summed"), sig("q_total"), sig("q_chain")
        quant, tdone, tcopied = sig("q_quantized"), sig("q_transposed"), sig("q_copied")
        ps = m.ps
        block = ctx.enter_context(nc.Block())

        @block.sync
        def _(sp):
            sp.dma_start(m.ident[:], a["c_ident"]).then_inc(loaded.sem, 16)
            sp.dma_start(w1n[:], a["L0_ffn_w1"].rearrange("(c p) d -> p c d", p=P)).then_inc(loaded.sem, 16)
            sp.dma_start(w2n[:], a["L0_ffn_w2"].rearrange("(c p) f -> p c f", p=P)).then_inc(loaded.sem, 16)
            sp.dma_start(m.b1T[:], a["L0_ffn_b1"].rearrange("(c p) -> p c", p=P), allow_slow_non_contiguous=True).then_inc(loaded.sem, 16)
            sp.dma_start(m.b2h[:], a["L0_ffn_b2"].rearrange("(a d) -> a d", a=1).broadcast_to([P, D])).then_inc(loaded.sem, 16)
            h = a["L0_attn_h"].rearrange("b s d -> (b s) d").rearrange("(i p) d -> p i d", p=P)
            sp.dma_start(m.x[:], h).then_inc(xs.sem, 16)
            sp.wait_ge(xs.sem, 16)

        @block.scalar
        def _(act):
            act.wait_ge(loaded.sem, loaded.at(80))
            nc.scalar.activation(absw[:], w1n[:].rearrange("p c d -> p (c d)"), ACT.Abs,
                                 accum_out=rows[:, 0:1]).then_inc(summed.sem, 1)
            act.wait_ge(summed.sem, summed.at(1))
            nc.scalar.activation(absw[:], w2n[:].rearrange("p c d -> p (c d)"), ACT.Abs,
                                 accum_out=rows[:, 1:2]).then_inc(summed.sem, 1)

        @block.tensor
        def _(pe):
            pe.wait_ge(summed.sem, summed.at(2))
            pe.wait_ge(chain.sem, chain.at(1))
            pe.matmul(ps[:, 0, 0:2], m.ones[:], rows[:], start=True, stop=True).then_inc(total.sem, 1)
            for n in range(4):
                pe.wait_ge(quant.sem, quant.at(n // 2 + 1))
                if n >= 2:
                    pe.wait_ge(tcopied.sem, tcopied.at(n - 1))
                bank = ps[:, 1 + n % 2, :].bitcast(F16)
                for j in range(8):
                    if n < 2:
                        src = q1[:, j, n * P:(n + 1) * P]
                    else:
                        src = q2[:, n - 2, j * P:(j + 1) * P]
                    last = pe.transpose(bank[:, j * P:(j + 1) * P], src, m.ident16[:])
                last.then_inc(tdone.sem, 1)

        @block.vector
        def _(dve):
            link = linker(dve, chain)

            link(nc.vector.memset(m.ones[:], 1.0))
            dve.wait_ge(loaded.sem, loaded.at(80))
            link(nc.vector.tensor_copy(m.ident16[:], m.ident[:]))
            link(nc.vector.tensor_scalar(m.b2h[:], m.b2h[:], 0.5, None, ALU.mult))
            dve.wait_ge(total.sem, total.at(1))
            link(nc.vector.tensor_scalar(thr[:, 0:2], ps[:, 0, 0:2], 1.0 / (F0 * D), 0.7, ALU.mult, ALU.mult))
            link(nc.vector.tensor_scalar(thr[:, 2:4], thr[:, 0:2], -1.0, None, ALU.mult))
            for n, (w, q) in enumerate(((w1n, q1), (w2n, q2))):
                w_, q_ = w[:].rearrange("p c d -> p (c d)"), q[:].rearrange("p c d -> p (c d)")
                link(nc.vector.tensor_scalar(below[:], w_, thr[:, 2 + n:3 + n], None, ALU.is_le))
                ins = nc.vector.scalar_tensor_tensor(out=q_, in0=w_, scalar=thr[:, n:n + 1], in1=below[:],
                                                     op0=ALU.is_ge, op1=ALU.subtract)
                if n == 1:
                    link(ins)
                    ins = nc.vector.tensor_scalar(q_, q_, 0.5, None, ALU.mult)
                ins.then_inc(quant.sem, 1)
                dve.wait_ge(quant.sem, quant.at(n + 1))
            for n in range(4):
                dve.wait_ge(tdone.sem, tdone.at(n + 1))
                bank = ps[:, 1 + n % 2, :].bitcast(F16)
                if n < 2:
                    ins = nc.vector.tensor_copy(m.w1qT[:, n, :], bank)
                else:
                    ins = nc.vector.tensor_copy(m.w2qT[:, :, (n - 2) * P:(n - 1) * P],
                                                bank.rearrange("p (f q) -> p f q", f=NF))
                ins.then_inc(tcopied.sem, 1)


def ffn_phase(nc, m, a, sig):
    with ExitStack() as ctx:
        sb = buffers(nc, ctx)

        GW = GT * P
        y = sb("ffn_y", [P, GT, D], F32)
        yp = sb("ffn_y_parts", [P, 2, GT, D], F16)
        yT = sb("ffn_yT", [P, 2, 2, KD, GW], F16)
        g32 = sb("ffn_g", [P, 2, GW], F32)
        gp = sb("ffn_g_parts", [P, 4, 2, GW], F16)
        split, tdone, tcopied = sig("ffn_y_split"), sig("ffn_transposed"), sig("ffn_yT_ready")
        var, rstd = sig("ffn_var_ready"), sig("ffn_rstd_ready")
        normed, biased = sig("ffn_normed"), sig("ffn_bias_added")
        up, gelu, hi, lo = sig("ffn_up_done"), sig("ffn_gelu_done"), sig("ffn_hi_ready"), sig("ffn_lo_ready")
        down, added, chain = sig("ffn_down_done"), sig("ffn_added"), sig("ffn_chain")
        pchain = sig("ffn_pool_chain")
        ps = m.ps
        TB = 6
        steps = NG * NF
        block = ctx.enter_context(nc.Block())

        @block.gpsimd
        def _(pool):
            link = linker(pool, pchain)
            for g in range(NG):
                pool.wait_ge(var.sem, var.at(g + 1))
                refine_root(nc, link, m.var[:, 0:GT], m.rstd[:, 0:GT], m.nt[:, 0:GT]).then_inc(rstd.sem, 1)
                pool.wait_ge(normed.sem, normed.at(g + 1))
                xg = m.x[:, g * GT:(g + 1) * GT, :]
                nc.gpsimd.tensor_tensor(xg, xg, m.b2h[:, None, :].broadcast_to([P, GT, D]), ALU.add).then_inc(biased.sem, 1)

        @block.tensor
        def _(pe):
            def transposes(g):
                for part in range(2):
                    pe.wait_ge(split.sem, split.at(2 * g + part + 1))
                    if 2 * g + part > 0:
                        pe.wait_ge(tcopied.sem, tcopied.at(2 * g + part))
                    bank = ps[:, TB, :].bitcast(F16)
                    for k in range(KD):
                        for i in range(GT):
                            j = k * GT + i
                            last = pe.transpose(bank[:, j * P:(j + 1) * P], yp[:, part, i, k * P:(k + 1) * P], m.ident16[:])
                    last.then_inc(tdone.sem, 1)

            def up_chunk(n):
                g, f = divmod(n, NF)
                if f == 0:
                    pe.wait_ge(tcopied.sem, tcopied.at(2 * g + 2))
                if n >= 2:
                    pe.wait_ge(gelu.sem, gelu.at(n - 1))
                for k in range(KD):
                    for part in range(2):
                        last = pe.matmul(ps[:, n % 2, :], m.w1qT[:, k, f * P:(f + 1) * P], yT[:, g % 2, part, k, :],
                                         start=(k + part == 0), stop=(k == KD - 1 and part == 1))
                last.then_inc(up.sem, 1)

            def down_chunk(n):
                g, f = divmod(n, NF)
                pe.wait_ge(lo.sem, lo.at(n + 1))
                if f == 0 and g >= 2:
                    pe.wait_ge(added.sem, added.at(g - 1))
                for i in range(GT):
                    acc = ps[:, 2 + 2 * (g % 2) + i // 2, (i % 2) * D:(i % 2 + 1) * D]
                    for part in range(2):
                        last = pe.matmul(acc, gp[:, n % 4, part, i * P:(i + 1) * P], m.w2qT[:, f, :],
                                         start=(f == 0 and part == 0 and i % 2 == 0),
                                         stop=(f == NF - 1 and part == 1), skip_group_check=True)
                last.then_inc(down.sem, 1)

            transposes(0)
            for n in range(steps + 2):
                if n < steps:
                    up_chunk(n)
                    if n % NF == 6 and n // NF + 1 < NG:
                        transposes(n // NF + 1)
                if n >= 2:
                    down_chunk(n - 2)

        @block.scalar
        def _(act):
            for n in range(steps):
                f = n % NF
                act.wait_ge(up.sem, up.at(n + 1))
                if n >= 2:
                    act.wait_ge(lo.sem, lo.at(n - 1))
                nc.scalar.activation(g32[:, n % 2, :], ps[:, n % 2, :], ACT.Gelu, bias=m.b1T[:, f:f + 1],
                                     scale=1.0 / YS).then_inc(gelu.sem, 1)
                act.wait_ge(gelu.sem, gelu.at(n + 1))
                if n >= 4:
                    act.wait_ge(down.sem, down.at(n - 3))
                nc.scalar.copy(gp[:, n % 4, 0, :], g32[:, n % 2, :]).then_inc(hi.sem, 1)

        @block.vector
        def _(dve):
            link = linker(dve, chain)

            def norm(g):
                stats, aggregate, apply = layer_norm_steps(nc, dve, m, link, m.x[:, g * GT:(g + 1) * GT, :], y, GT, YS)

                def first():
                    if g >= 1:
                        dve.wait_ge(normed.sem, normed.at(g))
                    stats()

                def variances():
                    aggregate().then_inc(var.sem, 1)

                def scaled():
                    if g >= 1:
                        dve.wait_ge(split.sem, split.at(2 * g))
                    dve.wait_ge(rstd.sem, rstd.at(g + 1))
                    ins = apply()
                    ins.then_inc(normed.sem, 1)
                    dve.wait_ge(normed.sem, normed.at(g + 1))

                def high():
                    if g >= 1:
                        dve.wait_ge(tdone.sem, tdone.at(2 * g))
                    nc.vector.tensor_copy(yp[:, 0], y[:]).then_inc(split.sem, 1)
                    dve.wait_ge(split.sem, split.at(2 * g + 1))

                def low():
                    nc.vector.tensor_tensor(yp[:, 1], y[:], yp[:, 0], ALU.subtract).then_inc(split.sem, 1)
                return first, variances, scaled, high, low

            def copy_yT(g):
                for part in range(2):
                    dve.wait_ge(tdone.sem, tdone.at(2 * g + part + 1))
                    if g >= 2:
                        dve.wait_ge(up.sem, up.at(NF * (g - 1)))
                    nc.vector.tensor_copy(yT[:, g % 2, part].rearrange("p k t -> p (k t)"),
                                          ps[:, TB, :].bitcast(F16)).then_inc(tcopied.sem, 1)

            def add_out(g):
                dve.wait_ge(down.sem, down.at(NF * (g + 1)))
                dve.wait_ge(biased.sem, biased.at(g + 1))
                for j in range(2):
                    xg = m.x[:, g * GT + 2 * j:g * GT + 2 * j + 2, :]
                    acc = ps[:, 2 + 2 * (g % 2) + j, :].rearrange("p (i d) -> p i d", i=2)
                    ins = nc.vector.tensor_tensor(xg, acc, xg, ALU.add)
                ins.then_inc(added.sem, 1)

            for step in norm(0):
                step()
            copy_yT(0)
            for n in range(steps):
                g, f = divmod(n, NF)
                if g + 1 < NG:
                    if f == 0:
                        ahead = norm(g + 1)
                    if f < 5:
                        ahead[f]()
                    if f == 6:
                        copy_yT(g + 1)
                if f == 2 and g >= 1:
                    add_out(g - 1)
                dve.wait_ge(hi.sem, hi.at(n + 1))
                nc.vector.tensor_tensor(gp[:, n % 4, 1, :], g32[:, n % 2, :], gp[:, n % 4, 0, :],
                                        ALU.subtract).then_inc(lo.sem, 1)
            add_out(NG - 1)
        for s, n in ((split, 2 * NG), (tdone, 2 * NG), (tcopied, 2 * NG), (normed, NG), (var, NG), (rstd, NG), (biased, NG), (up, steps),
                     (gelu, steps), (hi, steps), (lo, steps), (down, steps), (added, NG), (chain, chain.links), (pchain, pchain.links)):
            s.phase_over(n)


NH = 16
HD = D // NH
BT = S // P
HP = 32
PARTS = 3
Q_PARTS = (0, 0, 0, 1, 1, 2)
K_PARTS = (0, 1, 2, 0, 1, 0)
QK = HD * len(Q_PARTS)
NEG = -1e30


def transpose_weights_phase(nc, m, a, sig):
    with ExitStack() as ctx:
        wn = ctx.enter_context(nc.sbuf_tensor("w_natural", [P, 4, KD, D], F32))
        cm = ctx.enter_context(nc.sbuf_tensor("mask_loaded", [P, 2, P], F32))
        loaded, tdone, copied = sig("aw_loaded"), sig("aw_transposed"), sig("aw_copied")
        chain = sig("aw_chain")
        block = ctx.enter_context(nc.Block())

        @block.sync
        def _(sp):
            for n, w in enumerate((a["L0_attn_Wq"], a["L0_attn_Wk"], a["L0_attn_Wv"], a["L0_attn_Wo"])):
                sp.dma_start(wn[:, n], w.rearrange("(c p) d -> p c d", p=P)).then_inc(loaded.sem, 16)
            for n, v in enumerate((a["L0_attn_bq"], a["L0_attn_bk"])):
                sp.dma_start(m.bqkT[:, n, :], v.rearrange("(c p) -> p c", p=P), allow_slow_non_contiguous=True).then_inc(loaded.sem, 16)
            for n, v in enumerate((a["L0_attn_bv"], a["L0_attn_bo"])):
                sp.dma_start(m.bvo[:, n, :], v.rearrange("(a d) -> a d", a=1).broadcast_to([P, D])).then_inc(loaded.sem, 16)
            sp.dma_start(cm[:], a["c_mask"]).then_inc(loaded.sem, 16)

        @block.tensor
        def _(pe):
            pe.wait_ge(loaded.sem, loaded.at(16 * 9))
            for n in range(4):
                if n >= 2:
                    pe.wait_ge(copied.sem, copied.at(n - 1))
                for ko in range(KD):
                    for ki in range(KD):
                        last = pe.transpose(m.ps[:, n % 2, (ki * KD + ko) * P:(ki * KD + ko + 1) * P],
                                            wn[:, n, ko, ki * P:(ki + 1) * P], m.ident[:])
                last.then_inc(tdone.sem, 1)

        @block.vector
        def _(dve):
            for n in range(4):
                dve.wait_ge(tdone.sem, tdone.at(n + 1))
                nc.vector.tensor_copy(m.awT[:, n].rearrange("p k d -> p (k d)"), m.ps[:, n % 2, :]).then_inc(copied.sem, 1)
            nc.vector.tensor_copy(m.mask16[:], cm[:])
            nc.vector.tensor_copy(m.identb[:], m.ident[:])


def project_phase(nc, m, a, sig, b, Qp, Kp, V):
    with ExitStack() as ctx:
        sb = buffers(nc, ctx)

        GW = GT * P
        groups = BT // GT
        y = sb("pr_y", [P, GT, D], F32)
        yT = sb("pr_yT", [P, KD, GW], F32)
        full = sb("pr_full", [P, 2, GW], F32)
        rest = sb("pr_rest", [P, 2, GW], F32)
        parts = sb("pr_parts", [P, 2, PARTS, GW], BF16)
        var, rstd, normed, biased = sig("pr_var"), sig("pr_rstd"), sig("pr_normed"), sig("pr_biased")
        tdone, yready = sig("pr_transposed"), sig("pr_yT_ready")
        proj, evac, high = sig("pr_projected"), sig("pr_full_ready"), sig("pr_high_ready")
        restr, mid, low = sig("pr_rest_ready"), sig("pr_mid_ready"), sig("pr_low_ready")
        sent = [sig("pr_parts_sent_even"), sig("pr_parts_sent_odd")]
        vdone, vready, chain, pchain = sig("pr_v_done"), sig("pr_v_ready"), sig("pr_chain"), sig("pr_pool_chain")
        spread, cleared = sig("pr_spread"), sig("pr_v_cleared")
        ps = m.ps
        units = groups * 4
        block = ctx.enter_context(nc.Block())

        @block.gpsimd
        def _(pool):
            link = linker(pool, pchain)
            if b == 0:
                nc.gpsimd.memset(V[:, :, :, HD:HP], 0.0).then_inc(cleared.sem, 1)
                pool.wait_ge(cleared.sem, cleared.at(1))
                nc.gpsimd.memset(V[:, :, :, HD:HD + 1], 1.0).then_inc(cleared.sem, 1)
                pool.wait_ge(cleared.sem, cleared.at(2))
                nc.gpsimd.memset(Kp[QK:QK + PARTS, :, :], 1.0).then_inc(cleared.sem, 1)
                pool.wait_ge(cleared.sem, cleared.at(3))
            for n in range(units):
                g = n // 4
                if n % 4 == 0:
                    pool.wait_ge(var.sem, var.at(g + 1))
                    refine_root(nc, link, m.var[:, 0:GT], m.rstd[:, 0:GT], m.nt[:, 0:GT]).then_inc(rstd.sem, 1)
                    pool.wait_ge(normed.sem, normed.at(g + 1))
                    xg = m.x[:, b * BT + g * GT:b * BT + (g + 1) * GT, :]
                    nc.gpsimd.tensor_tensor(xg, xg, m.bvo[:, 1:2, :].broadcast_to([P, GT, D]), ALU.add).then_inc(biased.sem, 1)
                pool.wait_ge(mid.sem, mid.at(n + 1))
                nc.gpsimd.tensor_tensor(parts[:, n % 2, 2, :], rest[:, n % 2, :], parts[:, n % 2, 1, :],
                                        ALU.subtract).then_inc(low.sem, 1)

        @block.tensor
        def _(pe):
            n = 0
            for g in range(groups):
                pe.wait_ge(normed.sem, normed.at(g + 1))
                if g >= 1:
                    pe.wait_ge(yready.sem, yready.at(g))
                for k in range(KD):
                    for i in range(GT):
                        last = pe.transpose(ps[:, k, i * P:(i + 1) * P], y[:, i, k * P:(k + 1) * P], m.ident[:])
                last.then_inc(tdone.sem, 1)
                pe.wait_ge(yready.sem, yready.at(g + 1))
                for w in range(2):
                    for c in range(KD):
                        if n >= 2:
                            pe.wait_ge(evac.sem, evac.at(n - 1))
                        for k in range(KD):
                            last = pe.matmul(ps[:, 2 + n % 2, :], m.awT[:, w, k, c * P:(c + 1) * P], yT[:, k, :],
                                             start=(k == 0), stop=(k == KD - 1))
                        last.then_inc(proj.sem, 1)
                        n += 1
                for i in range(GT):
                    t = g * GT + i
                    if t >= 2:
                        pe.wait_ge(vready.sem, vready.at(t - 1))
                    for k in range(KD):
                        last = pe.matmul(ps[:, 4 + t % 2, 0:D], yT[:, k, i * P:(i + 1) * P], m.awT[:, 2, k, :],
                                         start=(k == 0), stop=(k == KD - 1))
                    last.then_inc(vdone.sem, 1)

        @block.scalar
        def _(act):
            for n in range(units):
                w, c = n // 2 % 2, n % 2
                act.wait_ge(proj.sem, proj.at(n + 1))
                if n >= 2:
                    act.wait_ge(restr.sem, restr.at(n - 1))
                nc.scalar.activation(full[:, n % 2, :], ps[:, 2 + n % 2, :], ACT.Identity,
                                     bias=m.bqkT[:, w, c:c + 1]).then_inc(evac.sem, 1)
                act.wait_ge(evac.sem, evac.at(n + 1))
                if n >= 2:
                    act.wait_ge(sent[n % 2].sem, sent[n % 2].at(16 * (n // 2)))
                nc.scalar.copy(parts[:, n % 2, 0, :], full[:, n % 2, :]).then_inc(high.sem, 1)

        @block.vector
        def _(dve):
            link = linker(dve, chain)
            for g in range(groups):
                t0 = b * BT + g * GT
                stats, aggregate, apply = layer_norm_steps(nc, dve, m, link, m.x[:, t0:t0 + GT, :], y, GT, 1.0)
                if g >= 1:
                    dve.wait_ge(tdone.sem, tdone.at(g))
                stats()
                aggregate().then_inc(var.sem, 1)
                dve.wait_ge(rstd.sem, rstd.at(g + 1))
                apply().then_inc(normed.sem, 1)
                dve.wait_ge(tdone.sem, tdone.at(g + 1))
                if g >= 1:
                    dve.wait_ge(vdone.sem, vdone.at(g * GT))
                nc.vector.tensor_copy(yT[:], ps[:, 0:2, :]).then_inc(yready.sem, 1)
                for n in range(g * 4, g * 4 + 4):
                    dve.wait_ge(high.sem, high.at(n + 1))
                    if n >= 2:
                        dve.wait_ge(low.sem, low.at(n - 1))
                    nc.vector.tensor_tensor(rest[:, n % 2, :], full[:, n % 2, :], parts[:, n % 2, 0, :],
                                            ALU.subtract).then_inc(restr.sem, 1)
                    dve.wait_ge(restr.sem, restr.at(n + 1))
                    nc.vector.tensor_copy(parts[:, n % 2, 1, :], rest[:, n % 2, :]).then_inc(mid.sem, 1)
                for i in range(GT):
                    t = g * GT + i
                    dve.wait_ge(vdone.sem, vdone.at(t + 1))
                    nc.vector.tensor_tensor(V[:, t, :, 0:HD], ps[:, 4 + t % 2, 0:D].rearrange("p (h d) -> p h d", h=NH),
                                            m.bvo[:, 0, :].rearrange("p (h d) -> p h d", h=NH), ALU.add).then_inc(vready.sem, 1)

        @block.sync
        def _(sp):
            for n in range(units):
                g, w, c = n // 4, n // 2 % 2, n % 2
                sp.wait_ge(low.sem, low.at(n + 1))
                dst = a["qk_parts"][w, :, c * P:(c + 1) * P, g * GW:(g + 1) * GW].rearrange("s c t -> c s t")
                sp.dma_start(dst, parts[:, n % 2]).then_inc(sent[n % 2].sem, 16)
            for s in sent:
                sp.wait_ge(s.sem, s.at(8 * units))
            for w, (dst, order) in enumerate(((Qp, Q_PARTS), (Kp, K_PARTS))):
                for j, part in enumerate(order):
                    src = a["qk_parts"][w, part].rearrange("(h d) t -> d h t", d=HD)
                    (sp if j % 2 == 0 else sp).dma_start(dst[j * HD:(j + 1) * HD], src).then_inc(spread.sem, 16)
            sp.wait_ge(spread.sem, spread.at(16 * 12))
        for s, n in ((var, groups), (rstd, groups), (normed, groups), (biased, groups), (tdone, groups), (yready, groups),
                     (proj, units), (evac, units), (high, units), (restr, units), (mid, units), (low, units),
                     (sent[0], 8 * units), (sent[1], 8 * units), (vdone, BT), (vready, BT), (chain, chain.links), (pchain, pchain.links),
                     (spread, 16 * 12), (cleared, 3 * (b == 0))):
            s.phase_over(n)


def attend_phase(nc, m, a, sig, b, Qp, Kp, V, O):
    with ExitStack() as ctx:
        sb = buffers(nc, ctx)

        HG, QG = 4, BT // 4
        GW = 4 * P
        E = sb("at_probs", [P, 2, HG, GW], F32)
        mx = sb("at_max", [P, 2, HG * BT], F32)
        nm = sb("at_neg_max", [HG * BT, 2, P], F32)
        mp = sb("at_max_parts", [HG * BT, PARTS, P], BF16)
        oT = sb("at_oT", [P, GW], F32)
        rec = sb("at_rec", [P, 4, HG], F32)
        qk, mxd, mtd, mpr, mset = sig("at_qk_done"), sig("at_max_done"), sig("at_maxT_done"), sig("at_max_parts"), sig("at_max_rows")
        st, ex, pv = sig("at_st_done"), sig("at_exp_done"), sig("at_pv_done")
        oev, otd, ord_, chain = sig("at_oT_ready"), sig("at_o_transposed"), sig("at_o_ready"), sig("at_chain")
        ps = m.ps
        groups = NH // HG
        units = [(G, kb) for G in range(QG) for kb in range(4 * G + 4)]
        NU = len(units)
        items = [(hh, i) for i in range(BT) for hh in range(HG)]
        NI = len(items)
        cost = [i + 1 for _, i in items]
        share = [[] for _ in units]
        spent, u = 0, 0
        per = sum(cost) / (NU - 2)
        for n, c in enumerate(cost):
            share[min(NU - 3, int(spent / per))].append(n)
            spent += c
        block = ctx.enter_context(nc.Block())

        @block.tensor
        def _(pe):
            def max_item(gr, n):
                hh, i = items[n]
                h = gr * HG + hh
                c = gr * NI + n
                if c >= 2:
                    pe.wait_ge(mxd.sem, mxd.at(c - 1))
                q = Qp[0:QK, h, i * P:(i + 1) * P]
                for bk in range((i + 4) // 4):
                    w = min(GW, (i + 1) * P - bk * GW)
                    out = ps[:, 2 * (c % 2) + bk, 0:w]
                    diag = bk == i // 4
                    last = pe.matmul(out, q, Kp[0:QK, h, bk * GW:bk * GW + w], start=True, stop=not diag)
                    if diag:
                        last = pe.matmul(out[:, w - P:w], m.identb[:], m.mask16[:, 0, :], start=False, stop=True)
                last.then_inc(qk.sem, 1)

            def scores(gr, u):
                G, kb = units[u]
                j = max(0, kb - 4 * G)
                for hh in range(HG):
                    h = gr * HG + hh
                    n = (gr * NU + u) * HG + hh
                    if n >= 2:
                        pe.wait_ge(ex.sem, ex.at(n - 1))
                    bank = ps[:, 4 + n % 2, :]
                    last = pe.matmul(bank[:, j * P:GW], Kp[0:QK + PARTS, h, kb * P:(kb + 1) * P],
                                     Qp[0:QK + PARTS, h, G * GW + j * P:(G + 1) * GW], start=True, stop=kb < 4 * G)
                    if kb >= 4 * G:
                        last = pe.matmul(bank[:, j * P:(j + 1) * P], m.identb[:], m.mask16[:, 1, :], start=False, stop=True)
                    last.then_inc(st.sem, 1)

            def weigh(gr, u):
                G, kb = units[u]
                j = max(0, kb - 4 * G)
                pe.wait_ge(ex.sem, ex.at((gr * NU + u + 1) * HG))
                if kb == 0 and gr * QG + G >= 1:
                    pe.wait_ge(oev.sem, oev.at(gr * QG + G))
                for hh in range(HG):
                    last = pe.matmul(ps[hh * HP:(hh + 1) * HP, 6, j * P:GW], V[:, kb, gr * HG + hh, :],
                                     E[:, (gr * NU + u) % 2, hh, j * P:GW], start=(kb == 0), stop=(kb == 4 * G + 3),
                                     skip_group_check=True)
                last.then_inc(pv.sem, 1)
                if kb == 4 * G + 3:
                    turn(gr, G)

            def turn(gr, G):
                n = gr * QG + G
                pe.wait_ge(oev.sem, oev.at(n + 1))
                if n >= 1:
                    pe.wait_ge(ord_.sem, ord_.at(n))
                for i in range(4):
                    last = pe.transpose(ps[:, 7, i * P:(i + 1) * P], oT[:, i * P:(i + 1) * P], m.ident[:])
                last.then_inc(otd.sem, 1)

            def max_rows(gr):
                pe.wait_ge(mxd.sem, mxd.at(NI * (gr + 1)))
                if gr >= 1:
                    pe.wait_ge(ord_.sem, ord_.at(QG * gr - 1))
                pe.transpose(ps[0:HG * BT, 7, 0:P], mx[:, gr % 2, :], m.ident[:]).then_inc(mtd.sem, 1)
                pe.wait_ge(mpr.sem, mpr.at(gr + 1))

            for n in range(NI):
                max_item(0, n)
            max_rows(0)
            for gr in range(groups):
                pe.wait_ge(mset.sem, mset.at(16 * PARTS * (gr + 1)))
                for u in range(NU):
                    scores(gr, u)
                    if u >= 1:
                        weigh(gr, u - 1)
                    if gr + 1 < groups:
                        for n in share[u]:
                            max_item(gr + 1, n)
                        if u == NU - 2:
                            max_rows(gr + 1)
                weigh(gr, NU - 1)

        @block.scalar
        def _(act):
            for gr in range(groups):
                for u, (G, kb) in enumerate(units):
                    j = max(0, kb - 4 * G)
                    if gr * NU + u >= 2:
                        act.wait_ge(pv.sem, pv.at(gr * NU + u - 1))
                    for hh in range(HG):
                        n = (gr * NU + u) * HG + hh
                        act.wait_ge(st.sem, st.at(n + 1))
                        nc.scalar.activation(E[:, (gr * NU + u) % 2, hh, j * P:GW], ps[:, 4 + n % 2, j * P:GW],
                                             ACT.Exp, scale=HD ** -0.5).then_inc(ex.sem, 1)

        @block.vector
        def _(dve):
            link = linker(dve, chain)

            def max_item(gr, n):
                hh, i = items[n]
                c = gr * NI + n
                dve.wait_ge(qk.sem, qk.at(c + 1))
                flat = ps[:, 2 * (c % 2):2 * (c % 2) + 2, :].rearrange("p a b -> p (a b)")
                nc.vector.tensor_reduce(mx[:, gr % 2, hh * BT + i:hh * BT + i + 1], flat[:, 0:(i + 1) * P], AX.X,
                                        ALU.max).then_inc(mxd.sem, 1)

            def max_parts(gr):
                dve.wait_ge(mtd.sem, mtd.at(gr + 1))
                if gr >= 1:
                    dve.wait_ge(mset.sem, mset.at(16 * PARTS * gr))
                link(nc.vector.tensor_scalar(nm[:, 0, :], ps[0:HG * BT, 7, 0:P], -1.0, None, ALU.mult))
                link(nc.vector.tensor_copy(mp[:, 0, :], nm[:, 0, :]))
                link(nc.vector.tensor_tensor(nm[:, 1, :], nm[:, 0, :], mp[:, 0, :], ALU.subtract))
                link(nc.vector.tensor_copy(mp[:, 1, :], nm[:, 1, :]))
                nc.vector.tensor_tensor(mp[:, 2, :], nm[:, 1, :], mp[:, 1, :], ALU.subtract).then_inc(mpr.sem, 1)

            def outputs(gr, G):
                n = gr * QG + G
                dve.wait_ge(pv.sem, pv.at(gr * NU + units.index((G, 4 * G + 3)) + 1))
                if n >= 1:
                    dve.wait_ge(otd.sem, otd.at(n))
                nc.vector.tensor_copy(oT[:], ps[:, 6, :]).then_inc(oev.sem, 1)
                dve.wait_ge(otd.sem, otd.at(n + 1))
                o = ps[:, 7, :].rearrange("p (i h d) -> p i h d", i=4, h=HG)
                link(nc.vector.reciprocal(rec[:], o[:, :, :, HD]))
                for i in range(4):
                    out = O[:, 4 * G + i, gr * HG * HD:(gr + 1) * HG * HD].rearrange("p (h d) -> p h d", h=HG)
                    ins = nc.vector.tensor_tensor(out, o[:, i, :, 0:HD], rec[:, i, :, None].broadcast_to([P, HG, HD]), ALU.mult)
                link(ins) if i == 99 else ins.then_inc(ord_.sem, 1)

            for n in range(NI):
                max_item(0, n)
            max_parts(0)
            for gr in range(groups):
                for u in range(NU):
                    if u >= 1 and units[u - 1][1] == 4 * units[u - 1][0] + 3:
                        outputs(gr, units[u - 1][0])
                    if gr + 1 < groups:
                        for n in share[u]:
                            max_item(gr + 1, n)
                        if u == NU - 2:
                            max_parts(gr + 1)
                outputs(gr, QG - 1)

        @block.sync
        def _(sp):
            for gr in range(groups):
                sp.wait_ge(mpr.sem, mpr.at(gr + 1))
                for p in range(PARTS):
                    dst = Qp[QK + p:QK + p + 1, gr * HG:(gr + 1) * HG, :].rearrange("p h t -> p (h t)")
                    sp.dma_start(dst.rearrange("p (j t) -> p j t", t=P), mp[:, p, :]).then_inc(mset.sem, 16)
            sp.wait_ge(mset.sem, mset.at(16 * PARTS * groups))
        for s, n in ((qk, NI * groups), (mxd, NI * groups), (mtd, groups), (mpr, groups), (mset, 16 * PARTS * groups),
                     (st, NU * groups * HG), (ex, NU * groups * HG), (pv, NU * groups), (oev, QG * groups),
                     (otd, QG * groups), (ord_, QG * groups), (chain, chain.links)):
            s.phase_over(n)


def out_projection_phase(nc, m, a, sig, b, O):
    with ExitStack() as ctx:
        sb = buffers(nc, ctx)
        OT = sb("op_OT", [P, 2, KD, P], F32)
        tdone, tcop, done, added = sig("op_transposed"), sig("op_copied"), sig("op_done"), sig("op_added")
        ps = m.ps
        block = ctx.enter_context(nc.Block())

        @block.tensor
        def _(pe):
            def turn(i):
                if i >= 2:
                    pe.wait_ge(tcop.sem, tcop.at(i - 1))
                for k in range(KD):
                    last = pe.transpose(ps[:, i % 2, k * P:(k + 1) * P], O[:, i, k * P:(k + 1) * P], m.ident[:])
                last.then_inc(tdone.sem, 1)
            turn(0)
            for i in range(BT):
                if i + 1 < BT:
                    turn(i + 1)
                pe.wait_ge(tcop.sem, tcop.at(i + 1))
                if i >= 2:
                    pe.wait_ge(added.sem, added.at(i - 1))
                for k in range(KD):
                    last = pe.matmul(ps[:, 2 + i % 2, 0:D], OT[:, i % 2, k, :], m.awT[:, 3, k, :], start=(k == 0),
                                     stop=(k == KD - 1))
                last.then_inc(done.sem, 1)

        @block.scalar
        def _(act):
            for i in range(BT):
                act.wait_ge(tdone.sem, tdone.at(i + 1))
                if i >= 2:
                    act.wait_ge(done.sem, done.at(i - 1))
                nc.scalar.copy(OT[:, i % 2].rearrange("p k t -> p (k t)"), ps[:, i % 2, 0:D]).then_inc(tcop.sem, 1)

        @block.vector
        def _(dve):
            for i in range(BT):
                dve.wait_ge(done.sem, done.at(i + 1))
                xt = m.x[:, b * BT + i, :]
                nc.vector.tensor_tensor(xt, ps[:, 2 + i % 2, 0:D], xt, ALU.add).then_inc(added.sem, 1)
        for s in (tdone, tcop, done, added):
            s.phase_over(BT)


def attention_phases(nc, m, a, sig):
    with ExitStack() as ctx:
        Qp = ctx.enter_context(nc.sbuf_tensor("q_parts", [QK + PARTS, NH, S], BF16))
        Kp = ctx.enter_context(nc.sbuf_tensor("k_parts", [QK + PARTS, NH, S], BF16))
        V = ctx.enter_context(nc.sbuf_tensor("v_padded", [P, BT, NH, HP], F32))
        O = ctx.enter_context(nc.sbuf_tensor("attn_out", [P, BT, D], F32))
        for b in range(B):
            project_phase(nc, m, a, sig, b, Qp, Kp, V)
            attend_phase(nc, m, a, sig, b, Qp, Kp, V, O)
            out_projection_phase(nc, m, a, sig, b, O)


NE, HE = 8, 512
KH = HE // P
TOPK = 2
SLOT_TILES = (T * TOPK + NE * (P - 1)) // P
SLOTS = SLOT_TILES * P
W1_COLS, W2_COLS, W3_COLS = KD * HE, KH * HE, KH * D
EXPERT_COLS = 2 * (W1_COLS + W2_COLS + W3_COLS)
WS = 256.0


def expert_views(flat):
    out, at = [], 0
    for cols, n in ((W1_COLS, HE), (W2_COLS, HE), (W3_COLS, D)):
        out.append(flat[:, at:at + 2 * cols].rearrange("p (s k n) -> p s k n", s=2, n=n))
        at += 2 * cols
    return out


def expert_weights_phase(nc, m, a, sig):
    with ExitStack() as ctx:
        sb = buffers(nc, ctx)
        raw = sb("expert_raw", [P, 2, EXPERT_COLS // 2], F32)
        bn = sb("expert_bias_natural", [NE * KH, 2, P], F32)
        zero = sb("zero_rows", [P, 2 * D], F16)
        loaded = [sig("ew_loaded_even"), sig("ew_loaded_odd")]
        biases, hi, lo = sig("ew_biases_loaded"), sig("ew_hi"), sig("ew_lo")
        tdone, zeroed, cleared = sig("ew_bias_transposed"), sig("ew_zeroed"), sig("ew_cleared")
        chain = sig("ew_chain")
        block = ctx.enter_context(nc.Block())
        stages = ((a["L1_ffn_W1"], 0, W1_COLS), (a["L1_ffn_W2"], W1_COLS, W2_COLS), (a["L1_ffn_W3"], W1_COLS + W2_COLS, W3_COLS))

        @block.sync
        def _(sp):
            for e in range(NE):
                if e >= 2:
                    sp.wait_ge(lo.sem, lo.at(3 * (e - 1)))
                for w, at, cols in stages:
                    sp.dma_start(raw[:, e % 2, at:at + cols].rearrange("p (k n) -> p k n", n=w.shape[2]),
                                 w[e].rearrange("(k p) n -> p k n", p=P)).then_inc(loaded[e % 2].sem, 16)
                if e == 0:
                    for n, v in enumerate((a["L1_ffn_b1"], a["L1_ffn_b2"])):
                        sp.dma_start(bn[:, n, :], v.rearrange("e (m p) -> (e m) p", p=P)).then_inc(biases.sem, 16)
                    sp.dma_start(m.wg[:], a["L1_ffn_Wg"].rearrange("(k p) n -> p k n", p=P)).then_inc(biases.sem, 16)
                    sp.dma_start(m.bg[:], a["L1_ffn_bg"].rearrange("(a n) -> a n", a=1).broadcast_to([P, NE])).then_inc(biases.sem, 16)
                    sp.dma_start(m.tri[:], a["c_before"]).then_inc(biases.sem, 16)
                    sp.dma_start(m.eiota[:], a["c_experts"]).then_inc(biases.sem, 16)
                    sp.dma_start(m.starts[:], a["c_tile_starts"]).then_inc(biases.sem, 16)
            sp.wait_ge(biases.sem, biases.at(16 * 7))

        @block.gpsimd
        def _(pool):
            nc.gpsimd.memset(zero[:], 0.0).then_inc(cleared.sem, 1)
            pool.wait_ge(cleared.sem, cleared.at(1))
            for t in range(SLOT_TILES):
                pool.dma_start(a["moe_rows"][t * P:(t + 1) * P, :], zero[:]).then_inc(zeroed.sem, 16)
            pool.wait_ge(zeroed.sem, zeroed.at(16 * SLOT_TILES))

        @block.tensor
        def _(pe):
            pe.wait_ge(biases.sem, biases.at(16 * 7))
            for n in range(2):
                last = pe.transpose(m.ps[:, 0, n * NE * KH:(n + 1) * NE * KH], bn[:, n, :], m.ident[0:NE * KH, 0:NE * KH])
            last.then_inc(tdone.sem, 1)

        @block.scalar
        def _(act):
            for e in range(NE):
                act.wait_ge(loaded[e % 2].sem, loaded[e % 2].at(48 * (e // 2 + 1)))
                views = expert_views(m.we[:, e, :])
                for n, (w, at, cols) in enumerate(stages):
                    src = raw[:, e % 2, at:at + cols].rearrange("p (k n) -> p k n", n=w.shape[2])
                    nc.scalar.mul(views[n][:, 0], src, WS).then_inc(hi.sem, 1)

        @block.vector
        def _(dve):
            dve.wait_ge(tdone.sem, tdone.at(1))
            nc.vector.tensor_copy(m.eb12[:], m.ps[:, 0, 0:2 * NE * KH].rearrange("p (n e c) -> p e n c", n=2, e=NE))
            for e in range(NE):
                dve.wait_ge(loaded[e % 2].sem, loaded[e % 2].at(48 * (e // 2 + 1)))
                views = expert_views(m.we[:, e, :])
                for n, (w, at, cols) in enumerate(stages):
                    src = raw[:, e % 2, at:at + cols].rearrange("p (k n) -> p k n", n=w.shape[2])
                    dve.wait_ge(hi.sem, hi.at(3 * e + n + 1))
                    nc.vector.scalar_tensor_tensor(out=views[n][:, 1], in0=src, scalar=WS, in1=views[n][:, 0],
                                                   op0=ALU.mult, op1=ALU.subtract).then_inc(lo.sem, 1)


def routing_phase(nc, m, a, sig):
    with ExitStack() as ctx:
        sb = buffers(nc, ctx)
        y = sb("rt_y", [P, GT, D], F32)
        yT = sb("rt_yT", [P, KD, GT * P], F32)
        rows = sb("rt_rows", [P, NT, 2 * D], F16)
        big = [sb(f"rt_big{n}", [P, NT, NE], F32) for n in range(8)]
        small = [sb(f"rt_small{n}", [P, NT], F32) for n in range(6)]
        ends = sb("rt_ends", [P, 6, NE], F32)
        te = sb("rt_tile_expert", [1, 2, SLOT_TILES + 1, NE], F32)
        tr = sb("rt_tile_sum", [1, 2, SLOT_TILES + 1], F32)
        one = sb("rt_one", [P, NT], F32)
        var, rstd, normed = sig("rt_var"), sig("rt_rstd"), sig("rt_normed")
        tdone, yready, gated = sig("rt_transposed"), sig("rt_yT_ready"), sig("rt_gated")
        shifted, expd, chosen, counted = sig("rt_shifted"), sig("rt_exp"), sig("rt_chosen"), sig("rt_counted")
        placed, sent, chain, pchain = sig("rt_placed"), sig("rt_rows_sent"), sig("rt_chain"), sig("rt_pool_chain")
        split = sig("rt_rows_split")
        ps = m.ps
        logits, prob, h1, h2, eq, cand, both, base = big
        mx, i1, i2, w1, w2, rs = small
        block = ctx.enter_context(nc.Block())

        @block.tensor
        def _(pe):
            for g in range(NG):
                pe.wait_ge(normed.sem, normed.at(g + 1))
                if g >= 1:
                    pe.wait_ge(yready.sem, yready.at(g))
                for k in range(KD):
                    for i in range(GT):
                        last = pe.transpose(ps[:, k, i * P:(i + 1) * P], y[:, i, k * P:(k + 1) * P], m.ident[:])
                last.then_inc(tdone.sem, 1)
                pe.wait_ge(yready.sem, yready.at(g + 1))
                for i in range(GT):
                    t = g * GT + i
                    for k in range(KD):
                        last = pe.matmul(ps[:, 2, t * NE:(t + 1) * NE], yT[:, k, i * P:(i + 1) * P], m.wg[:, k, :],
                                         start=(k == 0), stop=(k == KD - 1))
                last.then_inc(gated.sem, 1)
            pe.wait_ge(chosen.sem, chosen.at(1))
            flat = both[:].rearrange("p t e -> p (t e)")
            pe.matmul(ps[:, 3, 0:NT * NE], m.tri[:], flat, start=True, stop=True)
            pe.matmul(ps[:, 4, 0:NT * NE], m.ones[:], flat, start=True, stop=True).then_inc(counted.sem, 1)

        @block.scalar
        def _(act):
            act.wait_ge(shifted.sem, shifted.at(1))
            nc.scalar.activation(prob[:], logits[:], ACT.Exp).then_inc(expd.sem, 1)

        @block.vector
        def _(dve):
            link = linker(dve, chain)
            v = nc.vector
            link(v.memset(one[:], 1.0))
            for g in range(NG):
                x = m.x[:, g * GT:(g + 1) * GT, :]
                stats, aggregate, apply = layer_norm_steps(nc, dve, m, link, x, y, GT, YS)
                if g >= 1:
                    dve.wait_ge(tdone.sem, tdone.at(g))
                    dve.wait_ge(split.sem, split.at(2 * g))
                stats()
                aggregate().then_inc(var.sem, 1)
                dve.wait_ge(rstd.sem, rstd.at(g + 1))
                apply().then_inc(normed.sem, 1)
                dve.wait_ge(normed.sem, normed.at(g + 1))
                r = rows[:, g * GT:(g + 1) * GT, :]
                v.tensor_copy(r[:, :, 0:D], y[:]).then_inc(split.sem, 1)
                dve.wait_ge(split.sem, split.at(2 * g + 1))
                v.tensor_tensor(r[:, :, D:2 * D], y[:], r[:, :, 0:D], ALU.subtract).then_inc(split.sem, 1)
                dve.wait_ge(tdone.sem, tdone.at(g + 1))
                if g >= 1:
                    dve.wait_ge(gated.sem, gated.at(g))
                v.tensor_copy(yT[:], ps[:, 0:2, :]).then_inc(yready.sem, 1)

            def over(t, shape=(P, NT, NE)):
                return t[:, :, None].broadcast_to(list(shape))
            dve.wait_ge(gated.sem, gated.at(NG))
            iota = m.eiota[:]
            link(v.scalar_tensor_tensor(out=logits[:], in0=ps[:, 2, 0:NT * NE].rearrange("p (t e) -> p t e", e=NE),
                                        scalar=1.0 / YS, in1=m.bg[:, None, :].broadcast_to([P, NT, NE]),
                                        op0=ALU.mult, op1=ALU.add))
            link(v.tensor_reduce(mx[:], logits[:], AX.X, ALU.max))
            v.tensor_tensor(logits[:], logits[:], over(mx), ALU.subtract).then_inc(shifted.sem, 1)
            dve.wait_ge(expd.sem, expd.at(1))
            link(v.tensor_reduce(rs[:], prob[:], AX.X, ALU.add))
            link(v.reciprocal(rs[:], rs[:]))
            link(v.tensor_tensor(prob[:], prob[:], over(rs), ALU.mult))
            for n, (w, idx, hot) in enumerate(((w1, i1, h1), (w2, i2, h2))):
                link(v.tensor_reduce(w[:], prob[:], AX.X, ALU.max))
                link(v.tensor_tensor(eq[:], prob[:], over(w), ALU.is_equal))
                link(v.scalar_tensor_tensor(out=cand[:], in0=eq[:], scalar=-float(NE), in1=iota, op0=ALU.mult, op1=ALU.add))
                link(v.tensor_reduce(idx[:], cand[:], AX.X, ALU.min))
                link(v.tensor_scalar(idx[:], idx[:], float(NE), None, ALU.add))
                link(v.tensor_tensor(hot[:], iota, over(idx), ALU.is_equal))
                link(v.tensor_scalar(m.weight[:, :, n], w[:], 0.5, None, ALU.mult))
                if n == 0:
                    link(v.scalar_tensor_tensor(out=prob[:], in0=hot[:], scalar=-2.0, in1=prob[:], op0=ALU.mult, op1=ALU.add))
            v.tensor_tensor(both[:], h1[:], h2[:], ALU.add).then_inc(chosen.sem, 1)
            dve.wait_ge(counted.sem, counted.at(1))
            total = cand
            link(v.tensor_copy(total[:], ps[:, 4, 0:NT * NE].rearrange("p (t e) -> p t e", e=NE)))
            for e in range(NE):
                ins = v.tensor_tensor_scan(logits[:, :, e], one[:], total[:, :, e], 0.0, ALU.mult, ALU.add)
            link(ins)
            n_, pad, end, start, up, rem = (ends[:, k, :] for k in range(6))
            link(v.tensor_scalar(up, logits[:, NT - 1, :], float(P - 1), None, ALU.add))
            link(v.tensor_scalar(rem.bitcast(I32), up, 0.0, None, ALU.add))
            link(v.tensor_scalar(rem.bitcast(I32), rem.bitcast(I32), 7, None, ALU.arith_shift_right))
            link(v.tensor_scalar(pad, rem.bitcast(I32), float(P), None, ALU.mult))
            link(v.tensor_tensor_scan(end, one[:, 0:NE], pad, 0.0, ALU.mult, ALU.add))
            link(v.tensor_tensor(start, end, pad, ALU.subtract))
            link(v.tensor_tensor(base[:], logits[:], total[:], ALU.subtract))
            link(v.tensor_tensor(base[:], base[:], start[:, None, :].broadcast_to([P, NT, NE]), ALU.add))
            link(v.tensor_tensor(base[:], ps[:, 3, 0:NT * NE].rearrange("p (t e) -> p t e", e=NE), base[:], ALU.add))
            for n, hot in enumerate((h1, h2)):
                link(v.tensor_tensor(eq[:], hot[:], base[:], ALU.mult))
                link(v.tensor_reduce(mx[:], eq[:], AX.X, ALU.add))
                v.tensor_copy(m.slot[:, :, n], mx[:]).then_inc(placed.sem, 1)
                dve.wait_ge(placed.sem, placed.at(n + 1))
            nt = SLOT_TILES
            link(v.tensor_tensor(te[:, 0, 0:nt, :], end[0:1, None, :].broadcast_to([1, nt, NE]),
                                 m.starts[0:1, :, None].broadcast_to([1, nt, NE]), ALU.is_le))
            link(v.tensor_reduce(tr[:, 0, 0:nt], te[:, 0, 0:nt, :], AX.X, ALU.add))
            link(v.tensor_scalar(m.tile_expert[:], tr[:, 0, 0:nt], float(NE - 1), None, ALU.min))

        @block.gpsimd
        def _(pool):
            link = linker(pool, pchain)
            for g in range(NG):
                pool.wait_ge(var.sem, var.at(g + 1))
                refine_root(nc, link, m.var[:, 0:GT], m.rstd[:, 0:GT], m.nt[:, 0:GT]).then_inc(rstd.sem, 1)
            pool.wait_ge(placed.sem, placed.at(2))
            for t in range(NT):
                for n in range(TOPK):
                    pool.indirect_dma_start(out=a["moe_rows"][:, :], out_offset=bass.IndirectOffsetOnAxis(ap=m.slot[:, t, n:n + 1], axis=0),
                                            in_=rows[:, t, :], in_offset=None).then_inc(sent.sem, 16)
            pool.wait_ge(sent.sem, sent.at(16 * NT * TOPK))
        for s, n in ((var, NG), (rstd, NG), (normed, NG), (tdone, NG), (yready, NG), (gated, NG), (shifted, 1), (expd, 1),
                     (chosen, 1), (counted, 1), (placed, 2), (sent, 16 * NT * TOPK), (split, 2 * NG),
                     (chain, chain.links), (pchain, pchain.links)):
            s.phase_over(n)


def expert_phase(nc, m, a, sig):
    with ExitStack() as ctx:
        sb = buffers(nc, ctx)
        xt = sb("ex_rows", [P, 2, 2 * D], F16)
        yT = sb("ex_yT", [P, 2, 2, KD, P], F16)
        wr = sb("ex_weights", [P, 2, EXPERT_COLS], F16)
        bb = sb("ex_biases", [P, 2, 2, KH], F32)
        g32 = sb("ex_gelu", [P, 2, KH, P], F32)
        gp = sb("ex_gelu_parts", [P, 2, 2, 2, KH, P], F16)
        eo = sb("ex_out", [P, 2, D], F32)
        b3 = sb("ex_b3", [P, NE, D], F32)
        b3_loaded = sig("ex_b3_loaded")
        loaded = [sig("ex_rows_loaded_even"), sig("ex_rows_loaded_odd")]
        stored = [sig("ex_out_stored_even"), sig("ex_out_stored_odd")]
        tdone, yready, out_ready = sig("ex_transposed"), sig("ex_yT_ready"), sig("ex_out_ready")
        wready = [sig(f"ex_w{n}_ready") for n in (1, 2, 3)]
        layer = [sig(f"ex_layer{n}_done") for n in (1, 2, 3)]
        gelu = [sig(f"ex_gelu{n}_done") for n in (1, 2)]
        hi = [sig(f"ex_hi{n}_ready") for n in (1, 2)]
        lo = [sig(f"ex_lo{n}_ready") for n in (1, 2)]
        ps = m.ps
        views = [expert_views(wr[:, n, :]) for n in range(2)]
        block = ctx.enter_context(nc.Block())
        N = SLOT_TILES
        FIRST = 4
        OUTER = (N - 2 - FIRST) // 2
        AT = (0, 2 * W1_COLS, 2 * (W1_COLS + W2_COLS), EXPERT_COLS)

        def run(eng, body):
            def peeled(i):
                body(i, i % 2, i // 2, lambda o: 0 <= i + o < N)
            for i in range(FIRST):
                peeled(i)
            with eng.Fori(0, OUTER) as j:
                for u in range(2):
                    body(j * 2 + (FIRST + u), u, j + FIRST // 2, lambda o: True)
            for i in range(FIRST + 2 * OUTER, N + 2):
                peeled(i)

        def tile(i):
            return bass.ds(i * P, P)

        @block.sync
        def _(sp):
            for e in range(NE):
                sp.dma_start(b3[:, e, :], a["L1_ffn_b3"][e:e + 1, :].broadcast_to([P, D])).then_inc(b3_loaded.sem, 16)
            for t in range(2):
                sp.dma_start(xt[:, t, :], a["moe_rows"][t * P:(t + 1) * P, :]).then_inc(loaded[t].sem, 16)

            def body(i, par, half, stage):
                if stage(2) and (not isinstance(i, int) or i + 2 < N):
                    sp.wait_ge(tdone.sem, tdone.at(i + 1))
                    sp.dma_start(xt[:, par, :], a["moe_rows"][tile(i + 2), :]).then_inc(loaded[par].sem, 16)
                if stage(-2):
                    if due(i - 1):
                        sp.wait_ge(out_ready.sem, out_ready.at(i - 1))
                    sp.dma_start(a["moe_out"][tile(i - 2), :], eo[:, par, :]).then_inc(stored[par].sem, 16)
            run(sp, body)
            for par in range(2):
                sp.wait_ge(stored[par].sem, stored[par].at(16 * ((N + 1 - par) // 2)))

        @block.tensor
        def _(pe):
            def transposes(i, par, half):
                o = 1 - par
                if due((half + 1 + par) * 16):
                    pe.wait_ge(loaded[o].sem, loaded[o].at((half + 1 + par) * 16))
                if due(i):
                    pe.wait_ge(yready.sem, yready.at(i))
                bank = ps[:, o, :].bitcast(F16)
                for c in range(2 * KD):
                    last = pe.transpose(bank[:, c * P:(c + 1) * P], xt[:, o, c * P:(c + 1) * P], m.ident16[:])
                last.then_inc(tdone.sem, 1)

            def wide(bank, w, act, kn, done):
                for mo in range(KH):
                    for k in range(kn):
                        for n, (pw, pa) in enumerate(((0, 0), (0, 1), (1, 0))):
                            last = pe.matmul(bank[:, mo * P:(mo + 1) * P], w[:, pw, k, mo * P:(mo + 1) * P],
                                             act[:, pa, k, :], start=(k == 0 and n == 0), stop=(k == kn - 1 and n == 2))
                last.then_inc(done.sem, 1)

            def body(i, par, half, stage):
                if stage(0):
                    pe.wait_ge(yready.sem, yready.at(i + 1))
                    pe.wait_ge(wready[0].sem, wready[0].at(i + 1))
                    if due(i - 1):
                        pe.wait_ge(gelu[0].sem, gelu[0].at(i - 1))
                    wide(ps[:, 2 + par, :], views[par][0], yT[:, par], KD, layer[0])
                if stage(1):
                    transposes(i, par, half)
                if stage(-1):
                    if due(i):
                        pe.wait_ge(lo[0].sem, lo[0].at(i))
                    if due(i):
                        pe.wait_ge(wready[1].sem, wready[1].at(i))
                    if due(i - 2):
                        pe.wait_ge(gelu[1].sem, gelu[1].at(i - 2))
                    wide(ps[:, 5 - par, :], views[1 - par][1], gp[:, 0, 1 - par], KH, layer[1])
                if stage(-2):
                    if due(i - 1):
                        pe.wait_ge(lo[1].sem, lo[1].at(i - 1))
                    if due(i - 1):
                        pe.wait_ge(wready[2].sem, wready[2].at(i - 1))
                    if due(i - 3):
                        pe.wait_ge(out_ready.sem, out_ready.at(i - 3))
                    for k in range(KH):
                        for n, (pw, pa) in enumerate(((0, 0), (1, 0), (0, 1))):
                            last = pe.matmul(ps[:, 6 + par, 0:D], gp[:, 1, par, pa, k, :], views[par][2][:, pw, k, :],
                                             start=(k == 0 and n == 0), stop=(k == KH - 1 and n == 2))
                    last.then_inc(layer[2].sem, 1)
            transposes(-1, 1, -1)
            run(pe, body)

        @block.scalar
        def _(act):
            def layer_out(n, t, par, bank, scale, parts_free, freed):
                act.wait_ge(layer[n].sem, layer[n].at(t + 1))
                if due(t):
                    act.wait_ge(lo[n].sem, lo[n].at(t))
                for c in range(KH):
                    last = nc.scalar.activation(g32[:, n, c, :], bank[:, c * P:(c + 1) * P], ACT.Gelu,
                                                bias=bb[:, par, n, c:c + 1], scale=scale)
                last.then_inc(gelu[n].sem, 1)
                act.wait_ge(gelu[n].sem, gelu[n].at(t + 1))
                if due(t - 1):
                    act.wait_ge(parts_free.sem, parts_free.at(t - 1))
                nc.scalar.copy(gp[:, n, par, 0], g32[:, n]).then_inc(hi[n].sem, 1)

            def body(i, par, half, stage):
                if stage(0):
                    layer_out(0, i, par, ps[:, 2 + par, :], 1.0 / (YS * WS), layer[1], None)
                if stage(-1):
                    layer_out(1, i - 1, 1 - par, ps[:, 5 - par, :], 1.0 / WS, layer[2], None)
            run(act, body)

        @block.vector
        def _(dve):
            v = nc.vector

            def expert_of(t):
                if isinstance(t, int):
                    return dve.value_load(m.tile_expert[0:1, t:t + 1], min_val=0, max_val=NE - 1)
                return dve.value_load(m.tile_expert[0:1, bass.ds(t, 1)], min_val=0, max_val=NE - 1)

            def weights(n, t, par):
                e = expert_of(t)
                flat = m.we[:].rearrange("p e c -> p (e c)")
                if due(t - 1):
                    dve.wait_ge(layer[n].sem, layer[n].at(t - 1))
                if n < 2:
                    if due(t - 1):
                        dve.wait_ge(gelu[n].sem, gelu[n].at(t - 1))
                    v.tensor_copy(bb[:, par, n, :], m.eb12[:].rearrange("p e n c -> p (e n c)")[:, bass.ds(e * (2 * KH) + n * KH, KH)])
                c = AT[n + 1] - AT[n]
                v.tensor_copy(wr[:, par, AT[n]:AT[n + 1]], flat[:, bass.ds(e * EXPERT_COLS + AT[n], c)]).then_inc(wready[n].sem, 1)

            def low(n, t, par):
                dve.wait_ge(hi[n].sem, hi[n].at(t + 1))
                v.tensor_tensor(gp[:, n, par, 1], g32[:, n], gp[:, n, par, 0], ALU.subtract).then_inc(lo[n].sem, 1)

            def yT_copy(t, par):
                dve.wait_ge(tdone.sem, tdone.at(t + 1))
                if due(t - 1):
                    dve.wait_ge(layer[0].sem, layer[0].at(t - 1))
                v.tensor_copy(yT[:, par].rearrange("p s k t -> p (s k t)"), ps[:, par, 0:D].bitcast(F16)).then_inc(yready.sem, 1)

            weights(0, 0, 0)
            yT_copy(0, 0)
            dve.wait_ge(b3_loaded.sem, b3_loaded.at(16 * NE))

            def body(i, par, half, stage):
                if stage(1):
                    weights(0, i + 1, 1 - par)
                if stage(0):
                    weights(1, i, par)
                if stage(-1):
                    weights(2, i - 1, 1 - par)
                if stage(1):
                    yT_copy(i + 1, 1 - par)
                if stage(0):
                    low(0, i, par)
                if stage(-1):
                    low(1, i - 1, 1 - par)
                if stage(-2):
                    e = expert_of(i - 2)
                    if due(i - 1):
                        dve.wait_ge(layer[2].sem, layer[2].at(i - 1))
                    if not isinstance(half, int) or half > 1:
                        dve.wait_ge(stored[par].sem, stored[par].at((half - 1) * 16))
                    v.scalar_tensor_tensor(out=eo[:, par, :], in0=ps[:, 6 + par, 0:D], scalar=1.0 / WS,
                                           in1=b3[:].rearrange("p e d -> p (e d)")[:, bass.ds(e * D, D)],
                                           op0=ALU.mult, op1=ALU.add).then_inc(out_ready.sem, 1)
            run(dve, body)
        for s in [tdone, yready, out_ready] + wready + layer + gelu + hi + lo:
            s.phase_over(N)
        b3_loaded.phase_over(16 * NE)
        for par in range(2):
            loaded[par].phase_over(16 * ((N + 1 - par) // 2))
            stored[par].phase_over(16 * ((N + 1 - par) // 2))


def combine_phase(nc, m, a, sig):
    with ExitStack() as ctx:
        sb = buffers(nc, ctx)
        R = 4
        got = sb("co_rows", [P, R, TOPK, D], F32)
        here = [sig(f"co_rows_here{n}") for n in range(R)]
        added = sig("co_added")
        block = ctx.enter_context(nc.Block())

        @block.gpsimd
        def _(pool):
            for t in range(NT):
                if t >= R:
                    pool.wait_ge(added.sem, added.at(2 * (t - R + 1)))
                for n in range(TOPK):
                    pool.indirect_dma_start(out=got[:, t % R, n, :], out_offset=None, in_=a["moe_out"][:, :],
                                            in_offset=bass.IndirectOffsetOnAxis(ap=m.slot[:, t, n:n + 1], axis=0)
                                            ).then_inc(here[t % R].sem, 16)

        @block.vector
        def _(dve):
            for t in range(NT):
                dve.wait_ge(here[t % R].sem, here[t % R].at(16 * TOPK * (t // R + 1)))
                for n in range(TOPK):
                    nc.vector.scalar_tensor_tensor(out=m.x[:, t, :], in0=got[:, t % R, n, :], scalar=m.weight[:, t, n:n + 1],
                                                   in1=m.x[:, t, :], op0=ALU.mult, op1=ALU.add).then_inc(added.sem, 1)
                    dve.wait_ge(added.sem, added.at(2 * t + n + 1))
        added.phase_over(2 * NT)
        for s in here:
            s.phase_over(16 * TOPK * NT // R)


def moe_phases(nc, m, a, sig):
    routing_phase(nc, m, a, sig)
    expert_phase(nc, m, a, sig)
    combine_phase(nc, m, a, sig)


def retention_phase(nc, m, a, sig):
    with ExitStack() as ctx:
        sb = buffers(nc, ctx)
        HC = NH // KD
        wqkvg = sb("re_w_qkvg", [P, KD, 4 * D], F32)
        wproj = sb("re_w_proj", [P, KD, D], F32)
        gn = sb("re_gn", [P, 2, D], F32)
        decay = sb("re_decay", [P, NH, P], F32)
        qdec = sb("re_q_decay", [P, KD, P], F32)
        kdec = sb("re_k_decay", [P, D], F32)
        heads = sb("re_head_rows", [P, HC], F32)
        blocks = sb("re_state_blocks", [P, HC * HP], F32)
        sdec = sb("re_state_decay", [P, KD], F32)
        rot = sb("re_rotation", [P, 2, D], F32)
        y = sb("re_y", [P, 1, D], F32)
        yT = sb("re_yT", [P, KD, P], F32)
        qk = sb("re_qk", [P, 2, D], F32)
        t2 = sb("re_swapped", [P, 2, D], F32)
        V = sb("re_v", [P, 2, NH, HP], F32)
        gate = sb("re_gate", [P, 3, D], F32)
        qkT = sb("re_qkT", [P, 2, KD, P], F32)
        qdT = sb("re_q_decayed", [P, KD, P], F32)
        kd = sb("re_k_decayed", [P, D], F32)
        qx = sb("re_q_by_head", [P, HC, P], F32)
        pt = sb("re_weights", [P, HC, P], F32)
        state = sb("re_state", [P, KD, HC * HP], F32)
        upd = t2
        oT = sb("re_oT", [P, 4 * P], F32)
        cent = sb("re_centred", [P, NH, HD], F32)
        sq = t2[:, 0, :].rearrange("p (h d) -> p h d", h=NH)
        st = sb("re_stats", [P, 4, NH], F32)
        nT = sb("re_nT", [P, KD, P], F32)
        names = ("loaded rot cleared var rstd normed yturned yT qkproj vgproj rotated vready gated qkturned qkT qdT kd qx "
                 "scored weighed retained updated stated oT oturned gnvar gnrstd centred mixed nturned nT projected added "
                 "chain pchain heard").split()
        g = {n: sig("re_" + n) for n in names}
        ps = m.ps
        v, pl = nc.vector, nc.gpsimd
        N = NT
        block = ctx.enter_context(nc.Block())
        NLOAD = 11

        @block.sync
        def _(sp):
            kp = "(k p) n -> p k n"
            row = lambda w: w.rearrange("(a d) -> a d", a=1).broadcast_to([P, D])
            for dst, src in ((wqkvg[:, :, 0:3 * D], a["L1_attn_w_qkv"].rearrange(kp, p=P)),
                             (wqkvg[:, :, 3 * D:], a["L1_attn_w_g"].rearrange(kp, p=P)), (wproj[:], a["L1_attn_w_proj"].rearrange(kp, p=P)),
                             (gn[:, 0, :], row(a["L1_attn_gn_weight"])), (gn[:, 1, :], row(a["L1_attn_gn_bias"])),
                             (decay[:], a["c_decay"]), (qdec[:], a["c_q_decay"]), (kdec[:], a["c_k_decay"]),
                             (heads[:], a["c_head_rows"]), (blocks[:], a["c_state_blocks"]), (sdec[:], a["c_state_decay"])):
                sp.dma_start(dst, src).then_inc(g["loaded"].sem, 16)
            for i in range(N):
                if i > 0:
                    sp.wait_ge(g["rotated"].sem, i)
                sp.dma_start(rot[:], a["c_rotation"][i % BT]).then_inc(g["rot"].sem, 16)
            sp.wait_ge(g["loaded"].sem, 16 * NLOAD)

        @block.tensor
        def _(pe):
            pe.wait_ge(g["loaded"].sem, 16 * NLOAD)
            for i in range(N + 2):
                r, o = i - 1, i - 2
                if 0 <= o:
                    pe.wait_ge(g["oT"].sem, o + 1)
                    pe.wait_ge(g["stated"].sem, o + 1)
                    for n in range(4):
                        last = pe.transpose(ps[:, 7, n * P:(n + 1) * P], oT[:, n * P:(n + 1) * P], m.ident[:])
                    last.then_inc(g["oturned"].sem, 1)
                if i < N:
                    pe.wait_ge(g["normed"].sem, i + 1)
                    for k in range(KD):
                        last = pe.transpose(ps[:, 0, k * P:(k + 1) * P], y[:, 0, k * P:(k + 1) * P], m.ident[:])
                    last.then_inc(g["yturned"].sem, 1)
                if 0 <= r < N:
                    pe.wait_ge(g["rotated"].sem, r + 1)
                    if r - 1 > 0:
                        pe.wait_ge(g["added"].sem, r - 1)
                    for n in range(4):
                        last = pe.transpose(ps[:, 3, n * P:(n + 1) * P], qk[:, n // 2, (n % 2) * P:(n % 2 + 1) * P], m.ident[:])
                    last.then_inc(g["qkturned"].sem, 1)

                def scores(c):
                    pe.wait_ge(g["qx"].sem, 2 * r + c + 1)
                    if 2 * r + c > 0:
                        pe.wait_ge(g["weighed"].sem, 2 * r + c)
                    for n in range(2):
                        last = pe.matmul(ps[:, 4 + n, :], qkT[:, 1, c, :], qx[:, 4 * n:4 * n + 4, :], start=True, stop=True)
                    last.then_inc(g["scored"].sem, 1)

                def retain(c):
                    pe.wait_ge(g["weighed"].sem, 2 * r + c + 1)
                    if c == 0:
                        if r > 0:
                            pe.wait_ge(g["oT"].sem, r)
                        pe.wait_ge(g["qdT"].sem, r + 1)
                        if r > 0:
                            pe.wait_ge(g["stated"].sem, r)
                        pe.wait_ge(g["vready"].sem, r + 1)
                    for n in range(2):
                        at = (2 * c + n) * P
                        pe.matmul(ps[:, 6, at:at + P], state[:, c, n * P:(n + 1) * P], qdT[:, c, :], start=True, stop=False,
                                  skip_group_check=True)
                        for h in range(4):
                            last = pe.matmul(ps[h * HP:(h + 1) * HP, 6, at:at + P], V[:, r % 2, c * HC + n * 4 + h, :],
                                             pt[:, n * 4 + h, :], start=False, stop=True, skip_group_check=True)
                    last.then_inc(g["retained"].sem, 1)
                if 0 <= r < N:
                    scores(0)
                if i < N:
                    pe.wait_ge(g["yT"].sem, i + 1)
                    for n, projected in enumerate((g["qkproj"], g["vgproj"])):
                        if n == 0:
                            if i > 0:
                                pe.wait_ge(g["rotated"].sem, i)
                        else:
                            if i > 0:
                                pe.wait_ge(g["vready"].sem, i)
                            if i > 0:
                                pe.wait_ge(g["gated"].sem, i)
                        for k in range(KD):
                            last = pe.matmul(ps[:, 1 + n, :], yT[:, k, :], wqkvg[:, k, n * 512:(n + 1) * 512],
                                             start=(k == 0), stop=(k == KD - 1))
                        last.then_inc(projected.sem, 1)
                if 0 <= r < N:
                    retain(0)
                    scores(1)
                if 0 <= o:
                    pe.wait_ge(g["mixed"].sem, o + 1)
                    if min(N, i + 1) > 0:
                        pe.wait_ge(g["yT"].sem, min(N, i + 1))
                    for k in range(KD):
                        last = pe.transpose(ps[:, 0, k * P:(k + 1) * P], cent[:, k * 8:(k + 1) * 8, :].rearrange("p h d -> p (h d)"), m.ident[:])
                    last.then_inc(g["nturned"].sem, 1)
                if 0 <= r < N:
                    retain(1)
                    pe.wait_ge(g["kd"].sem, r + 1)
                    if r - 0 > 0:
                        pe.wait_ge(g["centred"].sem, r - 0)
                    for c in range(KD):
                        last = pe.matmul(ps[:, 7, c * HC * HP:(c + 1) * HC * HP], kd[:, c * P:(c + 1) * P],
                                         V[:, r % 2, c * HC:(c + 1) * HC, :].rearrange("p h d -> p (h d)"), start=True, stop=True)
                    last.then_inc(g["updated"].sem, 1)
                if 0 <= o:
                    pe.wait_ge(g["nT"].sem, o + 1)
                    if min(N, i) > 0:
                        pe.wait_ge(g["qkT"].sem, min(N, i))
                    if min(N, i) > 0:
                        pe.wait_ge(g["qdT"].sem, min(N, i))
                    for k in range(KD):
                        last = pe.matmul(ps[:, 3, 0:D], nT[:, k, :], wproj[:, k, :], start=(k == 0), stop=(k == KD - 1))
                    last.then_inc(g["projected"].sem, 1)

        @block.scalar
        def _(act):
            for i in range(N + 2):
                r, o = i - 1, i - 2
                if i < N:
                    act.wait_ge(g["yturned"].sem, i + 1)
                    if i > 0:
                        act.wait_ge(g["vgproj"].sem, i)
                    nc.scalar.copy(yT[:].rearrange("p k t -> p (k t)"), ps[:, 0, 0:D]).then_inc(g["yT"].sem, 1)
                if 0 <= r < N:
                    act.wait_ge(g["qkturned"].sem, r + 1)
                    if 2 * r > 0:
                        act.wait_ge(g["scored"].sem, 2 * r)
                    if 2 * r > 0:
                        act.wait_ge(g["qx"].sem, 2 * r)
                    nc.scalar.copy(qkT[:].rearrange("p n k t -> p (n k t)"), ps[:, 3, :]).then_inc(g["qkT"].sem, 1)
                if i < N:
                    act.wait_ge(g["vgproj"].sem, i + 1)
                    if i >= 2:
                        if i - 1 > 0:
                            act.wait_ge(g["updated"].sem, i - 1)
                    act.wait_ge(g["cleared"].sem, 2)
                    nc.scalar.copy(V[:, i % 2, :, 0:HD], ps[:, 2, 0:D].rearrange("p (h d) -> p h d", h=NH)).then_inc(g["vready"].sem, 1)
                    if i >= 3:
                        if i - 2 > 0:
                            act.wait_ge(g["mixed"].sem, i - 2)
                    nc.scalar.activation(gate[:, i % 3, :], ps[:, 2, D:2 * D], ACT.Silu).then_inc(g["gated"].sem, 1)
                if 0 <= r < N:
                    act.wait_ge(g["retained"].sem, 2 * r + 2)
                    if r > 0:
                        act.wait_ge(g["oturned"].sem, r)
                    nc.scalar.copy(oT[:], ps[:, 6, :]).then_inc(g["oT"].sem, 1)
                if 0 <= o:
                    act.wait_ge(g["nturned"].sem, o + 1)
                    if o > 0:
                        act.wait_ge(g["projected"].sem, o)
                    nc.scalar.copy(nT[:].rearrange("p k t -> p (k t)"), ps[:, 0, 0:D]).then_inc(g["nT"].sem, 1)

        @block.vector
        def _(dve):
            link = linker(dve, g["chain"])
            v.memset(state[:], 0.0).then_inc(g["cleared"].sem, 1)
            v.memset(V[:], 0.0).then_inc(g["cleared"].sem, 1)
            dve.wait_ge(g["cleared"].sem, 2)
            dve.wait_ge(g["loaded"].sem, 16 * NLOAD)

            def norm_start(t):
                stats, aggregate, _ = layer_norm_steps(nc, dve, m, link, m.x[:, t:t + 1, :], y, 1, 1.0)
                if t > 0:
                    dve.wait_ge(g["normed"].sem, t)
                stats()
                aggregate().then_inc(g["var"].sem, 1)

            def norm_end(t):
                _, _, apply = layer_norm_steps(nc, dve, m, link, m.x[:, t:t + 1, :], y, 1, 1.0)
                dve.wait_ge(g["rstd"].sem, t + 1)
                if t > 0:
                    dve.wait_ge(g["yturned"].sem, t)
                apply().then_inc(g["normed"].sem, 1)
            norm_start(0)
            norm_end(0)
            for i in range(N + 2):
                r, o = i - 1, i - 2
                if i + 1 < N:
                    norm_start(i + 1)
                if 0 <= r < N:
                    dve.wait_ge(g["qkturned"].sem, r + 1)
                    if 2 * r > 0:
                        dve.wait_ge(g["retained"].sem, 2 * r)
                    dve.wait_ge(g["qkT"].sem, r + 1)
                    v.tensor_tensor(qdT[:], ps[:, 3, 0:D].rearrange("p (k t) -> p k t", k=KD), qdec[:], ALU.mult).then_inc(g["qdT"].sem, 1)
                if 0 <= o:
                    dve.wait_ge(g["oturned"].sem, o + 1)
                    if o > 0:
                        dve.wait_ge(g["nturned"].sem, o)
                    ov = ps[:, 7, :].rearrange("p (h d) -> p h d", h=NH)[:, :, 0:HD]
                    link(v.tensor_reduce(st[:, 0, :], ov, AX.X, ALU.add))
                    link(v.tensor_scalar(st[:, 0, :], st[:, 0, :], 1.0 / HD, None, ALU.mult))
                    v.tensor_tensor(cent[:], ov, st[:, 0, :, None].broadcast_to([P, NH, HD]), ALU.subtract).then_inc(g["centred"].sem, 1)
                    dve.wait_ge(g["centred"].sem, o + 1)
                    link(v.tensor_tensor(sq, cent[:], cent[:], ALU.mult))
                    link(v.tensor_reduce(st[:, 1, :], sq, AX.X, ALU.add))
                    link(v.tensor_scalar(st[:, 1, :], st[:, 1, :], 1.0 / HD, EPS, ALU.mult, ALU.add))
                    guess_root(nc, link, st[:, 1, :], st[:, 2, :]).then_inc(g["gnvar"].sem, 1)
                if 0 <= r < N:
                    def weigh(c):
                        dve.wait_ge(g["scored"].sem, 2 * r + c + 1)
                        if 2 * r + c > 0:
                            dve.wait_ge(g["retained"].sem, 2 * r + c)
                        v.tensor_tensor(pt[:], ps[:, 4:6, :].rearrange("p a (h t) -> p (a h) t", t=P),
                                             decay[:, c * HC:(c + 1) * HC, :], ALU.mult).then_inc(g["weighed"].sem, 1)
                    weigh(0)
                if i + 1 < N:
                    norm_end(i + 1)
                if i < N:
                    rw = rot[:]
                    src = ps[:, 1, :].rearrange("p (n d) -> p n d", n=2)
                    pair = lambda t: t.rearrange("p n (d e) -> p n d e", e=2)
                    sin = rw[:, 1:2, :].rearrange("p n (d e) -> p n d e", e=2)
                    dve.wait_ge(g["qkproj"].sem, i + 1)
                    dve.wait_ge(g["rot"].sem, 16 * (i + 1))
                    if i > 0:
                        dve.wait_ge(g["qkturned"].sem, i)
                    if i > 0:
                        dve.wait_ge(g["kd"].sem, i)
                    v.tensor_tensor(qk[:], src, rw[:, 0:1, :].broadcast_to([P, 2, D]), ALU.mult)
                    for e in range(2):
                        ins = v.tensor_tensor(pair(t2[:])[:, :, :, e], pair(src)[:, :, :, 1 - e],
                                              sin[:, :, :, e].broadcast_to([P, 2, D // 2]), ALU.mult)
                    link(ins)
                    v.tensor_tensor(qk[:], qk[:], t2[:], ALU.add).then_inc(g["rotated"].sem, 1)
                if 0 <= r < N:
                    weigh(1)
                    dve.wait_ge(g["updated"].sem, r + 1)
                    dve.wait_ge(g["retained"].sem, 2 * r + 2)
                    if r % BT == BT - 1:
                        v.memset(state[:], 0.0).then_inc(g["stated"].sem, 1)
                    else:
                        link(v.tensor_tensor(upd[:], ps[:, 7, :].rearrange("p (k n) -> p k n", k=KD),
                                             blocks[:, None, :].broadcast_to([P, KD, HC * HP]), ALU.mult))
                        for c in range(KD):
                            ins = v.scalar_tensor_tensor(out=state[:, c, :], in0=state[:, c, :], scalar=sdec[:, c:c + 1],
                                                         in1=upd[:, c, :], op0=ALU.mult, op1=ALU.add)
                        ins.then_inc(g["stated"].sem, 1)
                    dve.wait_ge(g["stated"].sem, r + 1)
                if 0 <= o:
                    dve.wait_ge(g["projected"].sem, o + 1)
                    xt = m.x[:, o, :]
                    v.tensor_tensor(xt, ps[:, 3, 0:D], xt, ALU.add).then_inc(g["added"].sem, 1)

        @block.gpsimd
        def _(pool):
            link = linker(pool, g["pchain"])
            pool.wait_ge(g["loaded"].sem, 16 * NLOAD)
            pool.wait_ge(g["var"].sem, 1)
            refine_root(nc, link, m.var[:, 0:1], m.rstd[:, 0:1], m.nt[:, 0:1]).then_inc(g["rstd"].sem, 1)
            for i in range(N + 2):
                r, o = i - 1, i - 2
                if 0 <= r < N:
                    def by_head(c):
                        if 2 * r + c > 0:
                            pool.wait_ge(g["scored"].sem, 2 * r + c)
                        pl.tensor_tensor(qx[:], qkT[:, 0, c:c + 1, :].broadcast_to([P, HC, P]),
                                              heads[:, :, None].broadcast_to([P, HC, P]), ALU.mult).then_inc(g["qx"].sem, 1)
                    pool.wait_ge(g["qkT"].sem, r + 1)
                    by_head(0)
                if i + 1 < N:
                    pool.wait_ge(g["var"].sem, i + 2)
                    refine_root(nc, link, m.var[:, 0:1], m.rstd[:, 0:1], m.nt[:, 0:1]).then_inc(g["rstd"].sem, 1)
                if 0 <= r < N:
                    by_head(1)
                    pool.wait_ge(g["rotated"].sem, r + 1)
                    if r > 0:
                        pool.wait_ge(g["updated"].sem, r)
                    pl.tensor_tensor(kd[:], qk[:, 1, :], kdec[:], ALU.mult).then_inc(g["kd"].sem, 1)
                if 0 <= o:
                    pool.wait_ge(g["gnvar"].sem, o + 1)
                    link(refine_root(nc, link, st[:, 1, :], st[:, 2, :], st[:, 3, :]))
                    flat = cent[:].rearrange("p h d -> p (h d)")
                    link(pl.tensor_tensor(cent[:], cent[:], st[:, 2, :, None].broadcast_to([P, NH, HD]), ALU.mult))
                    link(pl.tensor_tensor(flat, flat, gn[:, 0, :], ALU.mult))
                    link(pl.tensor_tensor(flat, flat, gn[:, 1, :], ALU.add))
                    pool.wait_ge(g["gated"].sem, o + 1)
                    pl.tensor_tensor(flat, flat, gate[:, o % 3, :], ALU.mult).then_inc(g["mixed"].sem, 1)


def store_phase(nc, m, a, sig):
    with ExitStack() as ctx:
        stored = sig("out_stored")
        block = ctx.enter_context(nc.Block())

        @block.sync
        def _(sp):
            o = a["out"].rearrange("b s d -> (b s) d").rearrange("(i p) d -> p i d", p=P)
            sp.dma_start(o, m.x[:]).then_inc(stored.sem, 16)
            sp.wait_ge(stored.sem, stored.at(16))


def macaron(nc, a, stages=6, first=0):
    ctx = ExitStack()
    with ctx:
        sb = buffers(nc, ctx)

        USED.clear()
        sems = {}

        def sig(name):
            if name not in sems:
                sems[name] = Signal(ctx.enter_context(nc.semaphore(name)))
            return sems[name]

        m = Memory()
        m.x = sb("x", [P, NT, D], F32)
        m.ident = sb("ident", [P, P], F32)
        m.ident16 = sb("ident16", [P, P], F16)
        m.ones = sb("ones", [P, P], F32)
        m.bn = sb("bn_stats", [P, GT, 6], F32)
        m.mv = sb("bn_mean_var", [P, GT, 2], F32)
        m.var = sb("variance", [P, GT], F32)
        m.rstd = sb("rstd", [P, GT], F32)
        m.nt = sb("newton", [P, GT], F32)
        m.ps = ctx.enter_context(nc.psum_tensor("ps", [P, 8, 512], F32))
        a["qk_parts"] = nc.dram_tensor("qk_parts", (2, PARTS, D, S), BF16, kind="Internal").ap()
        a["moe_rows"] = nc.dram_tensor("moe_rows", (SLOTS, 2 * D), F16, kind="Internal").ap()
        a["moe_out"] = nc.dram_tensor("moe_out", (SLOTS, D), F32, kind="Internal").ap()
        with ExitStack() as inner:
            sb = buffers(nc, inner)
            m.b2h = sb("ffn_b2_half", [P, D], F32)
            m.b1T = sb("ffn_b1T", [P, NF], F32)
            m.w1qT = sb("w1qT", [P, KD, F0], F16)
            m.w2qT = sb("w2qT", [P, NF, D], F16)
            m.bqkT = sb("attn_bqkT", [P, 2, KD], F32)
            m.bvo = sb("attn_bvo", [P, 2, D], F32)
            m.awT = sb("attn_wT", [P, 4, KD, D], F32)
            m.mask16 = sb("causal_mask", [P, 2, P], BF16)
            m.identb = sb("ident_bf16", [P, P], BF16)
            quantize_phase(nc, m, a, sig)
            phases = [lambda: ffn_phase(nc, m, a, sig), lambda: attention_phases(nc, m, a, sig), lambda: ffn_phase(nc, m, a, sig)]
            if first <= 1 < stages:
                transpose_weights_phase(nc, m, a, sig)
            for ph in phases[first:stages]:
                ph()
        if stages > 3:
            sb = buffers(nc, ctx)
            m.we = sb("expert_weights", [P, NE, EXPERT_COLS], F16)
            m.eb12 = sb("expert_b12", [P, NE, 2, KH], F32)
            m.wg = sb("gate_w", [P, KD, NE], F32)
            m.bg = sb("gate_b", [P, NE], F32)
            m.tri = sb("before", [P, P], F32)
            m.eiota = sb("experts", [P, NT, NE], F32)
            m.starts = sb("tile_starts", [1, SLOT_TILES], F32)
            m.slot = sb("slots", [P, NT, TOPK], I32)
            m.weight = sb("mix_weights", [P, NT, TOPK], F32)
            m.tile_expert = sb("tile_expert", [1, SLOT_TILES], I32)
            expert_weights_phase(nc, m, a, sig)
            for ph in [moe_phases, retention_phase, moe_phases][max(0, first - 3):stages - 3]:
                ph(nc, m, a, sig)
        store_phase(nc, m, a, sig)


def retention_constants():
    c = {}
    f = np.float32
    gamma = 1.0 - 2.0 ** (-5.0 - np.arange(NH, dtype=np.float64))
    i = np.arange(P)
    scale = HD ** -0.5
    late = i[None, None, :] - i[:, None, None]
    c["c_decay"] = np.where(late >= 0, gamma[None, :, None] ** np.maximum(late, 0) * scale, 0).astype(f)
    head = np.arange(D) // HD
    by_channel = gamma[head].reshape(KD, P).T
    c["c_q_decay"] = (by_channel[:, :, None] ** (i + 1)[None, None, :] * scale).astype(f)
    c["c_k_decay"] = (gamma[head][None, :] ** (P - 1 - i)[:, None]).astype(f)
    c["c_state_decay"] = (by_channel ** P).astype(f)
    own = (i[:, None] // HD) == np.arange(NH // KD)[None, :]
    c["c_head_rows"] = own.astype(f)
    c["c_state_blocks"] = np.repeat(own, HP, axis=1).astype(f)
    pair = np.arange(0, D, 2, dtype=f)
    dim_scale = (pair + f(0.4 * D)) / f(1.4 * D)
    pos = np.arange(S, dtype=f)
    xs = dim_scale[None, :] ** (pos[:, None] / f(512.0))
    inv_freq = f(1.0) / f(10000.0) ** (pair / f(D))
    angle = pos[:, None] * inv_freq[None, :]
    sin, cos = np.sin(angle) * xs, np.cos(angle) * xs
    rotation = np.stack([np.repeat(cos, 2, axis=1), np.stack([-sin, sin], axis=-1).reshape(S, D)], axis=1)
    c["c_rotation"] = np.ascontiguousarray(rotation.reshape(BT, P, 2, D).astype(f))
    return c


def constants():
    c = {}
    c["c_ident"] = np.eye(P, dtype=np.float32)
    q, k = np.arange(P)[:, None], np.arange(P)[None, :]
    c["c_mask"] = np.stack([np.where(k > q, NEG, 0), np.where(q > k, NEG, 0)], axis=1).astype(np.float32)
    c["c_before"] = (q < k).astype(np.float32)
    c["c_experts"] = np.broadcast_to(np.arange(NE, dtype=np.float32), (P, NT, NE)).copy()
    c["c_tile_starts"] = (np.arange(SLOT_TILES, dtype=np.float32) * P)[None]
    c.update(retention_constants())
    return c


_INS = ['L0_attn_h', 'L0_attn_Wq', 'L0_attn_bq', 'L0_attn_Wk', 'L0_attn_bk', 'L0_attn_Wv', 'L0_attn_bv', 'L0_attn_Wo',
        'L0_attn_bo', 'L0_ffn_w1', 'L0_ffn_b1', 'L0_ffn_w2', 'L0_ffn_b2', 'L1_attn_w_qkv', 'L1_attn_w_g',
        'L1_attn_w_proj', 'L1_attn_gn_weight', 'L1_attn_gn_bias', 'L1_ffn_W1', 'L1_ffn_b1', 'L1_ffn_W2', 'L1_ffn_b2',
        'L1_ffn_W3', 'L1_ffn_b3', 'L1_ffn_Wg', 'L1_ffn_bg']


def kernel(**inputs):
    import concourse.bacc as _bacc
    from concourse import mybir as _mybir
    from concourse.bass_utils import run_bass_kernel_spmd as _run

    nc = _bacc.Bacc("TRN2", target_bir_lowering=False, num_devices=1)
    arrays, aps = {}, {}
    given = {name: np.ascontiguousarray(inputs[name]) for name in _INS}
    given.update(constants())
    for name, v in given.items():
        arrays[f"in_{name}"] = v
        aps[name] = nc.dram_tensor(f"in_{name}", v.shape, _mybir.dt.from_np(v.dtype), kind="ExternalInput").ap()
    aps["out"] = nc.dram_tensor("out_x", (B, S, D), F32, kind="ExternalOutput").ap()
    macaron(nc, aps)
    r = _run(nc, [arrays], core_ids=[0])
    return r.results[0]["out_x"]
```

```python
from contextlib import ExitStack

import numpy as np

import concourse.bass as bass
from concourse import mybir

P = 128
F32 = mybir.dt.float32
F16 = mybir.dt.float16
BF16 = mybir.dt.bfloat16
I32 = mybir.dt.int32
ALU = mybir.AluOpType
ACT = mybir.ActivationFunctionType
AX = mybir.AxisListType

B, S, D = 2, 1024, 256
T = B * S
NT = T // P
KD = D // P
F0 = 1024
NF = F0 // P
GT = 4
NG = NT // GT
EPS = 1e-5
YS = 256.0


NH = 16
HD = D // NH
BT = S // P
HP = 32
PARTS = 3
Q_PARTS = (0, 0, 0, 1, 1, 2)
K_PARTS = (0, 1, 2, 0, 1, 0)
QK = HD * len(Q_PARTS)
NEG = -1e30
HG = 4
STEP_BUFFERS = 3


class Signal:

    def __init__(self, sem):
        self.sem, self.past, self.links = sem, 0, 0

    def at(self, n):
        return n + self.past

    def phase_over(self, n):
        self.past += n


def buffers(nc, ctx):
    def sb(name, shape, dt):
        used = sb.used[name] = sb.used.get(name, 0) + 1
        return ctx.enter_context(nc.sbuf_tensor(name if used == 1 else f"{name}_{used}", shape, dt))
    sb.used = USED
    return sb


USED = {}


def due(n):
    return not isinstance(n, int) or n > 0


class Memory:
    pass


class Overlay:

    def __init__(self, whole):
        self.flat, self.at = whole[:].rearrange("p e c -> p (e c)"), 0
        self.V = self.place([NT, NH, HP], F32, "p (t h d) -> p t h d", t=NT, h=NH)
        self.O = self.place([NT, D], F32, "p (t d) -> p t d", t=NT)
        self.Qp = self.place([STEP_BUFFERS, HG, S], BF16, "p (r h t) -> p r h t", r=STEP_BUFFERS, h=HG)
        self.Kp = self.place([STEP_BUFFERS, HG, S], BF16, "p (r h t) -> p r h t", r=STEP_BUFFERS, h=HG)
        self.E = self.place([2, HG, 4 * P], F32, "p (n h t) -> p n h t", n=2, h=HG)
        self.wn = self.place([4, KD, D], F32, "p (n k d) -> p n k d", n=4, k=KD)

    def place(self, shape, dt, pattern=None, **sizes):
        cols = int(np.prod(shape)) * (2 if dt == F32 else 1)
        part = self.flat[:, self.at:self.at + cols]
        self.at += cols
        if dt != F16:
            part = part.bitcast(dt)
        return part.rearrange(pattern, **sizes) if pattern else part


def layer_norm_steps(nc, dve, m, link, x, y, n, scale):
    def stats():
        for i in range(n):
            ins = nc.vector.bn_stats(m.bn[:, i, :], x[:, i, :])
        link(ins)

    def aggregate():
        for i in range(n):
            ins = nc.vector.bn_aggr(m.mv[:, i, :], m.bn[:, i, :])
        link(ins)
        v, r = m.var[:, 0:n], m.rstd[:, 0:n]
        link(nc.vector.tensor_scalar(v, m.mv[:, 0:n, 1], EPS, 1.0 / (scale * scale), ALU.add, ALU.mult))
        return guess_root(nc, link, v, r)

    def apply():
        for i in range(n):
            ins = nc.vector.tensor_scalar(y[:, i, :], x[:, i, :], m.mv[:, i, 0:1], m.rstd[:, i:i + 1],
                                          ALU.subtract, ALU.mult)
        return ins
    return stats, aggregate, apply


def guess_root(nc, link, v, r):
    link(nc.vector.tensor_scalar(r.bitcast(I32), v.bitcast(I32), 1, None, ALU.arith_shift_right))
    return nc.vector.tensor_scalar(r.bitcast(I32), r.bitcast(I32), -1.0, float(0x5f3759df), ALU.mult, ALU.add)


def refine_root(nc, link, v, r, t):
    for step in range(3):
        link(nc.gpsimd.tensor_tensor(t, r, r, ALU.mult))
        link(nc.gpsimd.tensor_tensor(t, t, v, ALU.mult))
        link(nc.gpsimd.tensor_scalar(t, t, -0.5, 1.5, ALU.mult, ALU.add))
        ins = nc.gpsimd.tensor_tensor(r, r, t, ALU.mult)
        if step < 2:
            link(ins)
    return ins


def linker(eng, signal):
    signal.links = 0

    def link(ins):
        signal.links += 1
        ins.then_inc(signal.sem, 1)
        eng.wait_ge(signal.sem, signal.at(signal.links))
    return link


def quantize_phase(nc, m, a, sig):
    with ExitStack() as ctx:
        sb = buffers(nc, ctx)

        w1n = sb("w1_natural", [P, NF, D], F32)
        w2n = sb("w2_natural", [P, KD, F0], F32)
        below = sb("below", [P, NF * D], F16)
        q1 = sb("w1_quantized", [P, NF, D], F16)
        q2 = sb("w2_quantized", [P, KD, F0], F16)
        absw = sb("abs_w", [P, NF * D], F32)
        rows = sb("row_sums", [P, 2], F32)
        thr = sb("threshold", [P, 4], F32)
        loaded, xs, later, cleared = sig("q_loaded"), sig("x_loaded"), sig("aw_loaded"), sig("q_cleared")
        summed, total, chain = sig("q_summed"), sig("q_total"), sig("q_chain")
        quant, tdone, tcopied = sig("q_quantized"), sig("q_transposed"), sig("q_copied")
        ps = m.ps
        block = ctx.enter_context(nc.Block())

        @block.sync
        def _(sp):
            sp.dma_start(m.ident[:], a["c_ident"]).then_inc(loaded.sem, 16)
            sp.dma_start(w1n[:], a["L0_ffn_w1"].rearrange("(c p) d -> p c d", p=P)).then_inc(loaded.sem, 16)
            sp.dma_start(w2n[:], a["L0_ffn_w2"].rearrange("(c p) f -> p c f", p=P)).then_inc(loaded.sem, 16)
            sp.dma_start(m.b1T[:], a["L0_ffn_b1"].rearrange("(c p) -> p c", p=P), allow_slow_non_contiguous=True).then_inc(loaded.sem, 16)
            sp.dma_start(m.b2h[:], a["L0_ffn_b2"].rearrange("(a d) -> a d", a=1).broadcast_to([P, D])).then_inc(loaded.sem, 16)
            h = a["L0_attn_h"].rearrange("b s d -> (b s) d").rearrange("(i p) d -> p i d", p=P)
            sp.dma_start(m.x[:], h).then_inc(xs.sem, 16)
            for n, w in enumerate((a["L0_attn_Wq"], a["L0_attn_Wk"], a["L0_attn_Wv"], a["L0_attn_Wo"])):
                sp.dma_start(m.over.wn[:, n], w.rearrange("(c p) d -> p c d", p=P)).then_inc(later.sem, 16)
            for n, v in enumerate((a["L0_attn_bq"], a["L0_attn_bk"])):
                sp.dma_start(m.bqkT[:, n, :], v.rearrange("(c p) -> p c", p=P), allow_slow_non_contiguous=True).then_inc(later.sem, 16)
            for n, v in enumerate((a["L0_attn_bv"], a["L0_attn_bo"])):
                sp.dma_start(m.bvo[:, n, :], v.rearrange("(a d) -> a d", a=1).broadcast_to([P, D])).then_inc(later.sem, 16)
            sp.dma_start(m.mask_loaded[:], a["c_mask"]).then_inc(later.sem, 16)
            sp.wait_ge(xs.sem, 16)

        @block.gpsimd
        def _(pool):
            nc.gpsimd.memset(m.over.Kp[QK:QK + PARTS], 1.0).then_inc(cleared.sem, 1)
            pool.wait_ge(cleared.sem, 1)
            nc.gpsimd.memset(m.over.V[:, :, :, HD:HP], 0.0).then_inc(cleared.sem, 1)
            pool.wait_ge(cleared.sem, 2)
            nc.gpsimd.memset(m.over.V[:, :, :, HD:HD + 1], 1.0).then_inc(cleared.sem, 1)

        @block.scalar
        def _(act):
            act.wait_ge(loaded.sem, loaded.at(80))
            nc.scalar.activation(absw[:], w1n[:].rearrange("p c d -> p (c d)"), ACT.Abs,
                                 accum_out=rows[:, 0:1]).then_inc(summed.sem, 1)
            act.wait_ge(summed.sem, summed.at(1))
            nc.scalar.activation(absw[:], w2n[:].rearrange("p c d -> p (c d)"), ACT.Abs,
                                 accum_out=rows[:, 1:2]).then_inc(summed.sem, 1)

        @block.tensor
        def _(pe):
            pe.wait_ge(summed.sem, summed.at(2))
            pe.wait_ge(chain.sem, chain.at(1))
            pe.matmul(ps[:, 0, 0:2], m.ones[:], rows[:], start=True, stop=True).then_inc(total.sem, 1)
            for n in range(4):
                pe.wait_ge(quant.sem, quant.at(n // 2 + 1))
                if n >= 2:
                    pe.wait_ge(tcopied.sem, tcopied.at(n - 1))
                bank = ps[:, 1 + n % 2, :].bitcast(F16)
                for j in range(8):
                    if n < 2:
                        src = q1[:, j, n * P:(n + 1) * P]
                    else:
                        src = q2[:, n - 2, j * P:(j + 1) * P]
                    last = pe.transpose(bank[:, j * P:(j + 1) * P], src, m.ident16[:])
                last.then_inc(tdone.sem, 1)

        @block.vector
        def _(dve):
            link = linker(dve, chain)

            link(nc.vector.memset(m.ones[:], 1.0))
            dve.wait_ge(loaded.sem, loaded.at(80))
            link(nc.vector.tensor_copy(m.ident16[:], m.ident[:]))
            link(nc.vector.tensor_scalar(m.b2h[:], m.b2h[:], 0.5, None, ALU.mult))
            dve.wait_ge(total.sem, total.at(1))
            link(nc.vector.tensor_scalar(thr[:, 0:2], ps[:, 0, 0:2], 1.0 / (F0 * D), 0.7, ALU.mult, ALU.mult))
            link(nc.vector.tensor_scalar(thr[:, 2:4], thr[:, 0:2], -1.0, None, ALU.mult))
            for n, (w, q) in enumerate(((w1n, q1), (w2n, q2))):
                w_, q_ = w[:].rearrange("p c d -> p (c d)"), q[:].rearrange("p c d -> p (c d)")
                link(nc.vector.tensor_scalar(below[:], w_, thr[:, 2 + n:3 + n], None, ALU.is_le))
                ins = nc.vector.scalar_tensor_tensor(out=q_, in0=w_, scalar=thr[:, n:n + 1], in1=below[:],
                                                     op0=ALU.is_ge, op1=ALU.subtract)
                if n == 1:
                    link(ins)
                    ins = nc.vector.tensor_scalar(q_, q_, 0.5, None, ALU.mult)
                ins.then_inc(quant.sem, 1)
                dve.wait_ge(quant.sem, quant.at(n + 1))
            for n in range(4):
                dve.wait_ge(tdone.sem, tdone.at(n + 1))
                bank = ps[:, 1 + n % 2, :].bitcast(F16)
                if n < 2:
                    ins = nc.vector.tensor_copy(m.w1qT[:, n, :], bank)
                else:
                    ins = nc.vector.tensor_copy(m.w2qT[:, :, (n - 2) * P:(n - 1) * P],
                                                bank.rearrange("p (f q) -> p f q", f=NF))
                ins.then_inc(tcopied.sem, 1)
        xs.phase_over(16)


def ffn_phase(nc, m, a, sig, experts=False):
    with ExitStack() as ctx:
        sb = buffers(nc, ctx)

        GW = GT * P
        y = sb("ffn_y", [P, GT, D], F32)
        yp = sb("ffn_y_parts", [P, 2, GT, D], F16)
        yT = sb("ffn_yT", [P, 2, 2, KD, GW], F16)
        g32 = sb("ffn_g", [P, 2, GW], F32)
        gp = sb("ffn_g_parts", [P, 4, 2, GW], F16)
        split, tdone, tcopied = sig("ffn_y_split"), sig("ffn_transposed"), sig("ffn_yT_ready")
        var, rstd = sig("ffn_var_ready"), sig("ffn_rstd_ready")
        normed, biased = sig("ffn_normed"), sig("ffn_bias_added")
        up, gelu, hi, lo = sig("ffn_up_done"), sig("ffn_gelu_done"), sig("ffn_hi_ready"), sig("ffn_lo_ready")
        down, added, chain = sig("ffn_down_done"), sig("ffn_added"), sig("ffn_chain")
        pchain = sig("ffn_pool_chain")
        ps = m.ps
        TB = 6
        steps = NG * NF
        WC = 1024
        RAW = 4
        if experts:
            raw = sb("ew_raw", [P, RAW, WC], F32)
            bn = sb("ew_bias_natural", [NE * KH, 2, P], F32)
            zero = sb("ew_zero_rows", [P, 2 * D], F16)
            arrived = [sig(f"ew_arrived{n}") for n in range(RAW)]
            consts, whi, wlo = sig("ew_constants"), sig("ew_hi"), sig("ew_lo")
            bturned, cleared = sig("ew_bias_transposed"), sig("ew_cleared")
            zeroed = [sig("ew_zeroed_even"), sig("ew_zeroed_odd")]
            ZT = -(-SLOT_TILES * 2 // steps)
            ZN = -(-SLOT_TILES // ZT)
            chunks = [(w, e, k, v) for e in range(NE) for w, v, ks in ((a["L1_ffn_W1"], 0, (0,)), (a["L1_ffn_W2"], 1, (0, 2)),
                                                                       (a["L1_ffn_W3"], 2, (0,))) for k in ks]
            assert len(chunks) == steps

            def weights(n):
                w, e, k, v = chunks[n]
                cols = w.shape[2]
                ks = WC // cols
                view = expert_views(m.we[:, e, :])[v]
                return (raw[:, n % RAW, :].rearrange("p (k n) -> p k n", n=cols), view[:, 0, k:k + ks], view[:, 1, k:k + ks],
                        w[e].rearrange("(k p) n -> p k n", p=P)[:, k:k + ks])
        block = ctx.enter_context(nc.Block())

        @block.gpsimd
        def _(pool):
            link = linker(pool, pchain)
            if experts:
                nc.gpsimd.memset(zero[:], 0.0).then_inc(cleared.sem, 1)
            for g in range(NG):
                pool.wait_ge(var.sem, var.at(g + 1))
                refine_root(nc, link, m.var[:, 0:GT], m.rstd[:, 0:GT], m.nt[:, 0:GT]).then_inc(rstd.sem, 1)
                pool.wait_ge(normed.sem, normed.at(g + 1))
                xg = m.x[:, g * GT:(g + 1) * GT, :]
                nc.gpsimd.tensor_tensor(xg, xg, m.b2h[:, None, :].broadcast_to([P, GT, D]), ALU.add).then_inc(biased.sem, 1)

        @block.sync
        def _(sp):
            if experts:
                for n in range(steps):
                    if n >= RAW:
                        sp.wait_ge(wlo.sem, n - RAW + 1)
                    sp.dma_start(weights(n)[0], weights(n)[3]).then_inc(arrived[n % RAW].sem, 16)
                    if n == RAW:
                        for i, b in enumerate((a["L1_ffn_b1"], a["L1_ffn_b2"])):
                            sp.dma_start(bn[:, i, :], b.rearrange("e (m p) -> (e m) p", p=P)).then_inc(consts.sem, 16)
                        sp.dma_start(m.wg[:], a["L1_ffn_Wg"].rearrange("(k p) n -> p k n", p=P)).then_inc(consts.sem, 16)
                        sp.dma_start(m.bg[:], a["L1_ffn_bg"].rearrange("(a n) -> a n", a=1).broadcast_to([P, NE])).then_inc(consts.sem, 16)
                        sp.dma_start(m.tri[:], a["c_before"]).then_inc(consts.sem, 16)
                        sp.dma_start(m.eiota[:], a["c_experts"]).then_inc(consts.sem, 16)
                        sp.dma_start(m.starts[:], a["c_tile_starts"]).then_inc(consts.sem, 16)
                    if n == 0:
                        sp.wait_ge(cleared.sem, 1)
                    if n % 2 == 0 and n // 2 < ZN:
                        z = slice(n // 2 * ZT * P, min(SLOT_TILES, (n // 2 + 1) * ZT) * P)
                        rows = a["moe_rows"][z, :].rearrange("(t p) d -> p t d", p=P)
                        sp.dma_start(rows, zero[:, None, :].broadcast_to([P, rows.shape[1], 2 * D])).then_inc(zeroed[n // 2 % 2].sem, 16)
                sp.wait_ge(consts.sem, 16 * 7)
                for par, z in enumerate(zeroed):
                    sp.wait_ge(z.sem, 16 * ((ZN + 1 - par) // 2))

        @block.tensor
        def _(pe):
            def transposes(g):
                for part in range(2):
                    pe.wait_ge(split.sem, split.at(2 * g + part + 1))
                    if 2 * g + part > 0:
                        pe.wait_ge(tcopied.sem, tcopied.at(2 * g + part))
                    bank = ps[:, TB, :].bitcast(F16)
                    for k in range(KD):
                        for i in range(GT):
                            j = k * GT + i
                            last = pe.transpose(bank[:, j * P:(j + 1) * P], yp[:, part, i, k * P:(k + 1) * P], m.ident16[:])
                    last.then_inc(tdone.sem, 1)

            def up_chunk(n):
                g, f = divmod(n, NF)
                if f == 0:
                    pe.wait_ge(tcopied.sem, tcopied.at(2 * g + 2))
                if n >= 2:
                    pe.wait_ge(gelu.sem, gelu.at(n - 1))
                for k in range(KD):
                    for part in range(2):
                        last = pe.matmul(ps[:, n % 2, :], m.w1qT[:, k, f * P:(f + 1) * P], yT[:, g % 2, part, k, :],
                                         start=(k + part == 0), stop=(k == KD - 1 and part == 1))
                last.then_inc(up.sem, 1)

            def down_chunk(n):
                g, f = divmod(n, NF)
                pe.wait_ge(lo.sem, lo.at(n + 1))
                if f == 0 and g >= 2:
                    pe.wait_ge(added.sem, added.at(g - 1))
                for i in range(GT):
                    acc = ps[:, 2 + 2 * (g % 2) + i // 2, (i % 2) * D:(i % 2 + 1) * D]
                    for part in range(2):
                        last = pe.matmul(acc, gp[:, n % 4, part, i * P:(i + 1) * P], m.w2qT[:, f, :],
                                         start=(f == 0 and part == 0 and i % 2 == 0),
                                         stop=(f == NF - 1 and part == 1), skip_group_check=True)
                last.then_inc(down.sem, 1)

            transposes(0)
            for n in range(steps + 2):
                if n < steps:
                    up_chunk(n)
                    if n % NF == 6 and n // NF + 1 < NG:
                        transposes(n // NF + 1)
                if n >= 2:
                    down_chunk(n - 2)
            if experts:
                pe.wait_ge(consts.sem, 16 * 7)
                for n in range(2):
                    last = pe.transpose(ps[:, 7, n * NE * KH:(n + 1) * NE * KH], bn[:, n, :], m.ident[0:NE * KH, 0:NE * KH])
                last.then_inc(bturned.sem, 1)

        @block.scalar
        def _(act):
            for n in range(steps):
                f = n % NF
                act.wait_ge(up.sem, up.at(n + 1))
                if n >= 2:
                    act.wait_ge(lo.sem, lo.at(n - 1))
                nc.scalar.activation(g32[:, n % 2, :], ps[:, n % 2, :], ACT.Gelu, bias=m.b1T[:, f:f + 1],
                                     scale=1.0 / YS).then_inc(gelu.sem, 1)
                act.wait_ge(gelu.sem, gelu.at(n + 1))
                if n >= 4:
                    act.wait_ge(down.sem, down.at(n - 3))
                nc.scalar.copy(gp[:, n % 4, 0, :], g32[:, n % 2, :]).then_inc(hi.sem, 1)
                if experts:
                    src, high, _, _ = weights(n)
                    act.wait_ge(arrived[n % RAW].sem, 16 * (n // RAW + 1))
                    nc.scalar.mul(high, src, WS).then_inc(whi.sem, 1)

        @block.vector
        def _(dve):
            link = linker(dve, chain)

            def norm(g):
                stats, aggregate, apply = layer_norm_steps(nc, dve, m, link, m.x[:, g * GT:(g + 1) * GT, :], y, GT, YS)

                def first():
                    if g >= 1:
                        dve.wait_ge(normed.sem, normed.at(g))
                    stats()

                def variances():
                    aggregate().then_inc(var.sem, 1)

                def scaled():
                    if g >= 1:
                        dve.wait_ge(split.sem, split.at(2 * g))
                    dve.wait_ge(rstd.sem, rstd.at(g + 1))
                    ins = apply()
                    ins.then_inc(normed.sem, 1)
                    dve.wait_ge(normed.sem, normed.at(g + 1))

                def high():
                    if g >= 1:
                        dve.wait_ge(tdone.sem, tdone.at(2 * g))
                    nc.vector.tensor_copy(yp[:, 0], y[:]).then_inc(split.sem, 1)
                    dve.wait_ge(split.sem, split.at(2 * g + 1))

                def low():
                    nc.vector.tensor_tensor(yp[:, 1], y[:], yp[:, 0], ALU.subtract).then_inc(split.sem, 1)
                return first, variances, scaled, high, low

            def copy_yT(g):
                for part in range(2):
                    dve.wait_ge(tdone.sem, tdone.at(2 * g + part + 1))
                    if g >= 2:
                        dve.wait_ge(up.sem, up.at(NF * (g - 1)))
                    nc.vector.tensor_copy(yT[:, g % 2, part].rearrange("p k t -> p (k t)"),
                                          ps[:, TB, :].bitcast(F16)).then_inc(tcopied.sem, 1)

            def add_out(g):
                dve.wait_ge(down.sem, down.at(NF * (g + 1)))
                dve.wait_ge(biased.sem, biased.at(g + 1))
                for j in range(2):
                    xg = m.x[:, g * GT + 2 * j:g * GT + 2 * j + 2, :]
                    acc = ps[:, 2 + 2 * (g % 2) + j, :].rearrange("p (i d) -> p i d", i=2)
                    ins = nc.vector.tensor_tensor(xg, acc, xg, ALU.add)
                ins.then_inc(added.sem, 1)

            def weights_low(n):
                src, high, low, _ = weights(n)
                dve.wait_ge(whi.sem, n + 1)
                dve.wait_ge(arrived[n % RAW].sem, 16 * (n // RAW + 1))
                nc.vector.scalar_tensor_tensor(out=low, in0=src, scalar=WS, in1=high, op0=ALU.mult,
                                               op1=ALU.subtract).then_inc(wlo.sem, 1)

            for step in norm(0):
                step()
            copy_yT(0)
            for n in range(steps):
                g, f = divmod(n, NF)
                if g + 1 < NG:
                    if f == 0:
                        ahead = norm(g + 1)
                    if f < 5:
                        ahead[f]()
                    if f == 6:
                        copy_yT(g + 1)
                if f == 2 and g >= 1:
                    add_out(g - 1)
                dve.wait_ge(hi.sem, hi.at(n + 1))
                nc.vector.tensor_tensor(gp[:, n % 4, 1, :], g32[:, n % 2, :], gp[:, n % 4, 0, :],
                                        ALU.subtract).then_inc(lo.sem, 1)
                if experts and n >= 1:
                    weights_low(n - 1)
            if experts:
                weights_low(steps - 1)
            add_out(NG - 1)
            if experts:
                dve.wait_ge(bturned.sem, 1)
                nc.vector.tensor_copy(m.eb12[:], ps[:, 7, 0:2 * NE * KH].rearrange("p (n e c) -> p e n c", n=2, e=NE))
        for s, n in ((split, 2 * NG), (tdone, 2 * NG), (tcopied, 2 * NG), (normed, NG), (var, NG), (rstd, NG), (biased, NG), (up, steps),
                     (gelu, steps), (hi, steps), (lo, steps), (down, steps), (added, NG), (chain, chain.links), (pchain, pchain.links)):
            s.phase_over(n)


def transpose_weights_phase(nc, m, a, sig):
    with ExitStack() as ctx:
        wn, cm, loaded = m.over.wn, m.mask_loaded, sig("aw_loaded")
        tdone, copied = sig("aw_transposed"), sig("aw_copied")
        block = ctx.enter_context(nc.Block())

        @block.tensor
        def _(pe):
            pe.wait_ge(loaded.sem, loaded.at(16 * 9))
            for n in range(4):
                if n >= 2:
                    pe.wait_ge(copied.sem, copied.at(n - 1))
                for ko in range(KD):
                    for ki in range(KD):
                        last = pe.transpose(m.ps[:, n % 2, (ki * KD + ko) * P:(ki * KD + ko + 1) * P],
                                            wn[:, n, ko, ki * P:(ki + 1) * P], m.ident[:])
                last.then_inc(tdone.sem, 1)

        @block.vector
        def _(dve):
            for n in range(4):
                dve.wait_ge(tdone.sem, tdone.at(n + 1))
                nc.vector.tensor_copy(m.awT[:, n].rearrange("p k d -> p (k d)"), m.ps[:, n % 2, :]).then_inc(copied.sem, 1)
            dve.wait_ge(loaded.sem, loaded.at(16 * 9))
            nc.vector.tensor_copy(m.mask16[:], cm[:])
            nc.vector.tensor_copy(m.identb[:], m.ident[:])


def attend_phase(nc, m, a, sig):
    with ExitStack() as ctx:
        sb = buffers(nc, ctx)
        V, O, Qp, Kp, E = m.over.V, m.over.O, m.over.Qp, m.over.Kp, m.over.E
        TW = GT * P
        PR = 4
        y = sb("pr_y", [P, GT, D], F32)
        yT = sb("pr_yT", [P, 2, KD, TW], F32)
        full = sb("pr_full", [P, 2, TW], F32)
        rest = sb("pr_rest", [P, 2, TW], F32)
        parts = sb("pr_parts", [P, PR, PARTS, TW], BF16)
        var, rstd, normed = sig("pr_var"), sig("pr_rstd"), sig("pr_normed")
        tdone, yready = sig("pr_transposed"), sig("pr_yT_ready")
        proj, evac, high = sig("pr_projected"), sig("pr_full_ready"), sig("pr_high_ready")
        restr, mid, low = sig("pr_rest_ready"), sig("pr_mid_ready"), sig("pr_low_ready")
        sent = [sig(f"pr_parts_sent{n}") for n in range(PR)]
        vdone, vready, pchain = sig("pr_v_done"), sig("pr_v_ready"), sig("pr_pool_chain")
        biased = sig("pr_biased")
        PU = NG * 4
        QG = BT // 4
        GW = 4 * P
        R = STEP_BUFFERS
        STEPS = B * NH // HG
        LOADS = 2 * len(Q_PARTS)
        mx = sb("at_max_pieces", [P, 2, HG * BT, 2], F32)
        mc = sb("at_max", [P, HG * BT], F32)
        nm = sb("at_neg_max", [HG * BT, 2, P], F32)
        mp = sb("at_max_parts", [HG * BT, PARTS, P], BF16)
        oT = sb("at_oT", [P, GW], F32)
        rec = sb("at_rec", [P, 4, HG], F32)
        spread = [sig(f"at_qk_loaded{n}") for n in range(R)]
        qk, mxd, mcd, mtd, mpr = sig("at_qk_done"), sig("at_max_done"), sig("at_max_ready"), sig("at_maxT_done"), sig("at_max_parts")
        mset = sig("at_max_rows")
        st, ex, pv = sig("at_st_done"), sig("at_exp_done"), sig("at_pv_done")
        oev, otd, ord_, chain = sig("at_oT_ready"), sig("at_o_transposed"), sig("at_o_ready"), sig("at_chain")
        ps = m.ps
        SB, NSB = 3, 3
        units = [(G, kb) for G in range(QG) for kb in range(4 * G + 4)]
        NU = len(units)
        UL = [u for u, (G, kb) in enumerate(units) if kb == 4 * G + 3]
        pieces = [(hh, i, bk) for i in range(BT) for bk in range((i + 4) // 4) for hh in range(HG)]
        NP = len(pieces)

        def width(piece):
            _, i, bk = piece
            return min(GW, (i + 1) * P - bk * GW)
        total = sum(width(p) + 60 for p in pieces)
        spans = [GW - max(0, kb - 4 * G) * P + 60 for G, kb in units for _ in range(HG)]
        share, piece, passed, at = [[] for _ in spans], 0, 0, 0
        for n, w in enumerate(spans):
            at += w
            while piece < NP and passed < 1.25 * total * at / sum(spans):
                share[n].append(piece)
                passed += width(pieces[piece]) + 60
                piece += 1
        END = next(n for n, some in enumerate(share) if NP - 1 in some)
        ROWS, SPLIT = END + 2, END + 3
        assert SPLIT < NU * HG and (UL[-2] + 2) * HG <= ROWS

        LATE = 3
        SLOTS0 = NG // 2 * 8
        each = -(-NP // (SLOTS0 - LATE))
        PASS0 = [[p for p in range((n - LATE) * each, (n - LATE + 1) * each) if 0 <= p < NP] for n in range(SLOTS0)]

        def early(g, n):
            return PASS0[(g - NG // 2) * 8 + n] if g >= NG // 2 else []

        def max_bank(c):
            return 6 + c % 2 if c < NP else c % 3
        block = ctx.enter_context(nc.Block())

        @block.gpsimd
        def _(pool):
            link = linker(pool, pchain)

            def root(g):
                pool.wait_ge(var.sem, g + 1)
                refine_root(nc, link, m.var[:, 0:GT], m.rstd[:, 0:GT], m.nt[:, 0:GT]).then_inc(rstd.sem, 1)
            root(0)
            for g in range(NG):
                if g + 1 < NG:
                    root(g + 1)
                pool.wait_ge(normed.sem, g + 1)
                xg = m.x[:, g * GT:(g + 1) * GT, :]
                nc.gpsimd.tensor_tensor(xg, xg, m.bvo[:, 1:2, :].broadcast_to([P, GT, D]), ALU.add).then_inc(biased.sem, 1)
                for n in range(4 * g, 4 * g + 4):
                    pool.wait_ge(mid.sem, n + 1)
                    nc.gpsimd.tensor_tensor(parts[:, n % PR, 2, :], rest[:, n % 2, :], parts[:, n % PR, 1, :],
                                            ALU.subtract).then_inc(low.sem, 1)

        @block.tensor
        def _(pe):
            def max_piece(s, n):
                hh, i, bk = pieces[n]
                c = s * NP + n
                if n == 0:
                    pe.wait_ge(spread[s % R].sem, 16 * LOADS * (s // R + 1))
                if c >= 2:
                    pe.wait_ge(mxd.sem, c - 1 if c < NP + 3 else c - 2)
                w = width(pieces[n])
                diag = bk == i // 4
                last = pe.matmul(ps[:, max_bank(c), 0:w], Qp[0:QK, s % R, hh, i * P:(i + 1) * P],
                                 Kp[0:QK, s % R, hh, bk * GW:bk * GW + w], start=True, stop=not diag)
                if diag:
                    last = pe.matmul(ps[:, max_bank(c), w - P:w], m.identb[:], m.mask16[:, 0, :], start=False, stop=True)
                last.then_inc(qk.sem, 1)

            def scores(s, u, hh):
                G, kb = units[u]
                j = max(0, kb - 4 * G)
                n = (s * NU + u) * HG + hh
                if n >= NSB:
                    pe.wait_ge(ex.sem, n - NSB + 1)
                bank = ps[:, SB + n % NSB, :]
                last = pe.matmul(bank[:, j * P:GW], Kp[0:QK + PARTS, s % R, hh, kb * P:(kb + 1) * P],
                                 Qp[0:QK + PARTS, s % R, hh, G * GW + j * P:(G + 1) * GW], start=True, stop=kb < 4 * G)
                if kb >= 4 * G:
                    last = pe.matmul(bank[:, j * P:(j + 1) * P], m.identb[:], m.mask16[:, 1, :], start=False, stop=True)
                last.then_inc(st.sem, 1)

            def weigh(s, u):
                G, kb = units[u]
                j = max(0, kb - 4 * G)
                pe.wait_ge(ex.sem, (s * NU + u + 1) * HG)
                if kb == 0 and s * QG + G >= 1:
                    pe.wait_ge(oev.sem, s * QG + G)
                b, gr = divmod(s, NH // HG)
                for hh in range(HG):
                    last = pe.matmul(ps[hh * HP:(hh + 1) * HP, 6, j * P:GW], V[:, b * BT + kb, gr * HG + hh, :],
                                     E[:, (s * NU + u) % 2, hh, j * P:GW], start=(kb == 0), stop=(kb == 4 * G + 3),
                                     skip_group_check=True)
                last.then_inc(pv.sem, 1)

            def turn(s, G):
                n = s * QG + G
                pe.wait_ge(oev.sem, n + 1)
                if n >= 1:
                    pe.wait_ge(ord_.sem, n)
                if G == 0 or (G == QG - 1 and s + 1 < STEPS):
                    pe.wait_ge(mpr.sem, s + 1 + (G > 0))
                for i in range(4):
                    last = pe.transpose(ps[:, 7, i * P:(i + 1) * P], oT[:, i * P:(i + 1) * P], m.ident[:])
                last.then_inc(otd.sem, 1)

            def max_rows(s):
                pe.wait_ge(mcd.sem, s + 1)
                if s >= 1:
                    pe.wait_ge(ord_.sem, QG * s - 1)
                pe.transpose(ps[0:HG * BT, 7, 0:P], mc[:], m.ident[:]).then_inc(mtd.sem, 1)

            def turn_y(g):
                pe.wait_ge(normed.sem, g + 1)
                if g >= 1:
                    pe.wait_ge(yready.sem, g)
                for k in range(KD):
                    for i in range(GT):
                        last = pe.transpose(ps[:, k, i * P:(i + 1) * P], y[:, i, k * P:(k + 1) * P], m.ident[:])
                last.then_inc(tdone.sem, 1)
            turn_y(0)
            for g in range(NG):
                pe.wait_ge(yready.sem, g + 1)
                for n in range(4 * g, 4 * g + 4):
                    w, c = n // 2 % 2, n % 2
                    if n >= 2:
                        pe.wait_ge(evac.sem, n - 1)
                    for k in range(KD):
                        last = pe.matmul(ps[:, 2 + n % 2, :], m.awT[:, w, k, c * P:(c + 1) * P], yT[:, g % 2, k, :],
                                         start=(k == 0), stop=(k == KD - 1))
                    last.then_inc(proj.sem, 1)
                    for piece in early(g, n % 4):
                        max_piece(0, piece)
                if g + 1 < NG:
                    turn_y(g + 1)
                for i in range(GT):
                    t = g * GT + i
                    if t >= 2:
                        pe.wait_ge(vready.sem, t - 1)
                    for k in range(KD):
                        last = pe.matmul(ps[:, 4 + t % 2, 0:D], yT[:, g % 2, k, i * P:(i + 1) * P], m.awT[:, 2, k, :],
                                         start=(k == 0), stop=(k == KD - 1))
                    last.then_inc(vdone.sem, 1)
                    for piece in early(g, 4 + i):
                        max_piece(0, piece)
            max_rows(0)
            pe.wait_ge(yready.sem, NG)
            pe.wait_ge(evac.sem, PU)
            pe.wait_ge(vready.sem, NT)
            for s in range(STEPS):
                pe.wait_ge(mset.sem, 16 * PARTS * (s + 1))
                for u in range(NU):
                    for hh in range(HG):
                        scores(s, u, hh)
                        if s + 1 < STEPS:
                            for n in share[u * HG + hh]:
                                max_piece(s + 1, n)
                        if hh == 1:
                            if u >= 1:
                                weigh(s, u - 1)
                            elif s >= 1:
                                weigh(s - 1, NU - 1)
                        if hh == 3:
                            if u >= 1 and u - 1 in UL[:-1]:
                                turn(s, UL.index(u - 1))
                            if u == 0 and s >= 1:
                                turn(s - 1, QG - 1)
                        if u * HG + hh == ROWS and s + 1 < STEPS:
                            max_rows(s + 1)
            weigh(STEPS - 1, NU - 1)
            turn(STEPS - 1, QG - 1)

        @block.scalar
        def _(act):
            for n in range(PU):
                w, c = n // 2 % 2, n % 2
                act.wait_ge(proj.sem, n + 1)
                if n >= 2:
                    act.wait_ge(restr.sem, n - 1)
                nc.scalar.activation(full[:, n % 2, :], ps[:, 2 + n % 2, :], ACT.Identity,
                                     bias=m.bqkT[:, w, c:c + 1]).then_inc(evac.sem, 1)
                act.wait_ge(evac.sem, n + 1)
                if n >= PR:
                    act.wait_ge(sent[n % PR].sem, 16 * (n // PR))
                nc.scalar.copy(parts[:, n % PR, 0, :], full[:, n % 2, :]).then_inc(high.sem, 1)
            def collect(s, G):
                n = s * QG + G
                act.wait_ge(pv.sem, s * NU + UL[G] + 1)
                if n >= 1:
                    act.wait_ge(otd.sem, n)
                nc.scalar.copy(oT[:], ps[:, 6, :]).then_inc(oev.sem, 1)

            for s in range(STEPS):
                for u, (G, kb) in enumerate(units):
                    j = max(0, kb - 4 * G)
                    if s * NU + u >= 2:
                        act.wait_ge(pv.sem, s * NU + u - 1)
                    for hh in range(HG):
                        n = (s * NU + u) * HG + hh
                        act.wait_ge(st.sem, n + 1)
                        nc.scalar.activation(E[:, (s * NU + u) % 2, hh, j * P:GW], ps[:, SB + n % NSB, j * P:GW],
                                             ACT.Exp, scale=HD ** -0.5).then_inc(ex.sem, 1)
                        if hh == 2:
                            if u >= 1 and u - 1 in UL:
                                collect(s, UL.index(u - 1))
                            if u == 0 and s >= 1:
                                collect(s - 1, QG - 1)
            collect(STEPS - 1, QG - 1)

        @block.vector
        def _(dve):
            link = linker(dve, chain)
            link(nc.vector.memset(mx[:], -3e38))

            def max_piece(s, n):
                hh, i, bk = pieces[n]
                c = s * NP + n
                dve.wait_ge(qk.sem, c + 1)
                nc.vector.tensor_reduce(mx[:, s % 2, hh * BT + i, bk:bk + 1], ps[:, max_bank(c), 0:width(pieces[n])], AX.X,
                                        ALU.max).then_inc(mxd.sem, 1)

            def max_ready(s):
                dve.wait_ge(mxd.sem, NP * (s + 1))
                if s >= 1:
                    dve.wait_ge(mtd.sem, s)
                nc.vector.tensor_reduce(mc[:], mx[:, s % 2], AX.X, ALU.max).then_inc(mcd.sem, 1)

            def max_parts(s):
                dve.wait_ge(mtd.sem, s + 1)
                if s >= 1:
                    dve.wait_ge(mset.sem, 16 * PARTS * s)
                link(nc.vector.tensor_scalar(nm[:, 0, :], ps[0:HG * BT, 7, 0:P], -1.0, None, ALU.mult))
                link(nc.vector.tensor_copy(mp[:, 0, :], nm[:, 0, :]))
                link(nc.vector.tensor_tensor(nm[:, 1, :], nm[:, 0, :], mp[:, 0, :], ALU.subtract))
                link(nc.vector.tensor_copy(mp[:, 1, :], nm[:, 1, :]))
                nc.vector.tensor_tensor(mp[:, 2, :], nm[:, 1, :], mp[:, 1, :], ALU.subtract).then_inc(mpr.sem, 1)

            def outputs(s, G):
                b, gr = divmod(s, NH // HG)
                dve.wait_ge(otd.sem, s * QG + G + 1)
                o = ps[:, 7, :].rearrange("p (i h d) -> p i h d", i=4, h=HG)
                link(nc.vector.reciprocal(rec[:], o[:, :, :, HD]))
                for i in range(4):
                    out = O[:, b * BT + 4 * G + i, gr * HG * HD:(gr + 1) * HG * HD].rearrange("p (h d) -> p h d", h=HG)
                    ins = nc.vector.tensor_tensor(out, o[:, i, :, 0:HD], rec[:, i, :, None].broadcast_to([P, HG, HD]), ALU.mult)
                ins.then_inc(ord_.sem, 1)

            def norm_start(g):
                x = m.x[:, g * GT:(g + 1) * GT, :]
                stats, aggregate, _ = layer_norm_steps(nc, dve, m, link, x, y, GT, 1.0)
                if g >= 1:
                    dve.wait_ge(tdone.sem, g)
                stats()
                aggregate().then_inc(var.sem, 1)

            def norm_end(g):
                x = m.x[:, g * GT:(g + 1) * GT, :]
                _, _, apply = layer_norm_steps(nc, dve, m, link, x, y, GT, 1.0)
                dve.wait_ge(rstd.sem, g + 1)
                apply().then_inc(normed.sem, 1)

            def copy_yT(g):
                dve.wait_ge(tdone.sem, g + 1)
                if g >= 2:
                    dve.wait_ge(vdone.sem, (g - 1) * GT)
                nc.vector.tensor_copy(yT[:, g % 2], ps[:, 0:2, :]).then_inc(yready.sem, 1)
            norm_start(0)
            norm_end(0)
            copy_yT(0)
            for g in range(NG):
                if g + 1 < NG:
                    norm_start(g + 1)
                for n in range(g * 4, g * 4 + 4):
                    if n == g * 4 + 2 and g + 1 < NG:
                        norm_end(g + 1)
                    for piece in early(g, n % 4):
                        max_piece(0, piece)
                    dve.wait_ge(high.sem, n + 1)
                    if n >= 2:
                        dve.wait_ge(low.sem, n - 1)
                    nc.vector.tensor_tensor(rest[:, n % 2, :], full[:, n % 2, :], parts[:, n % PR, 0, :],
                                            ALU.subtract).then_inc(restr.sem, 1)
                    dve.wait_ge(restr.sem, n + 1)
                    nc.vector.tensor_copy(parts[:, n % PR, 1, :], rest[:, n % 2, :]).then_inc(mid.sem, 1)
                if g + 1 < NG:
                    copy_yT(g + 1)
                for i in range(GT):
                    for piece in early(g, 4 + i):
                        max_piece(0, piece)
                    t = g * GT + i
                    dve.wait_ge(vdone.sem, t + 1)
                    nc.vector.tensor_tensor(V[:, t, :, 0:HD], ps[:, 4 + t % 2, 0:D].rearrange("p (h d) -> p h d", h=NH),
                                            m.bvo[:, 0, :].rearrange("p (h d) -> p h d", h=NH), ALU.add).then_inc(vready.sem, 1)
            max_ready(0)
            max_parts(0)
            for s in range(STEPS):
                for u in range(NU):
                    for hh in range(HG):
                        if s + 1 < STEPS:
                            for n in share[u * HG + hh]:
                                max_piece(s + 1, n)
                        if hh == 3:
                            if u >= 1 and u - 1 in UL:
                                outputs(s, UL.index(u - 1))
                            if u == 0 and s >= 1:
                                outputs(s - 1, QG - 1)
                        if u * HG + hh == END and s + 1 < STEPS:
                            max_ready(s + 1)
                        if u * HG + hh == SPLIT and s + 1 < STEPS:
                            max_parts(s + 1)
            outputs(STEPS - 1, QG - 1)

        @block.sync
        def _(sp):
            def load(s):
                b, gr = divmod(s, NH // HG)
                if s >= R:
                    sp.wait_ge(st.sem, NU * HG * (s - R + 1))
                    sp.wait_ge(spread[s % R].sem, 16 * LOADS * (s // R))
                for w, (dst, order) in enumerate(((Qp, Q_PARTS), (Kp, K_PARTS))):
                    for j, part in enumerate(order):
                        src = a["qk_parts"][w, part, gr * HG * HD:(gr + 1) * HG * HD, b * S:(b + 1) * S]
                        sp.dma_start(dst[j * HD:(j + 1) * HD, s % R], src.rearrange("(h d) t -> d h t", d=HD)
                                     ).then_inc(spread[s % R].sem, 16)

            for n in range(PU):
                g, w, c = n // 4, n // 2 % 2, n % 2
                sp.wait_ge(low.sem, n + 1)
                dst = a["qk_parts"][w, :, c * P:(c + 1) * P, g * TW:(g + 1) * TW].rearrange("s c t -> c s t")
                sp.dma_start(dst, parts[:, n % PR]).then_inc(sent[n % PR].sem, 16)
                if n == PU // 2 - 1:
                    for each_sent in sent:
                        sp.wait_ge(each_sent.sem, 16 * PU // 2 // PR)
                    for s in range(R):
                        load(s)
            for s in sent:
                sp.wait_ge(s.sem, 16 * PU // PR)
            for s in range(STEPS):
                sp.wait_ge(mpr.sem, s + 1)
                for p in range(PARTS):
                    dst = Qp[QK + p:QK + p + 1, s % R].rearrange("p h (i t) -> p (h i) t", t=P)
                    sp.dma_start(dst, mp[:, p, :]).then_inc(mset.sem, 16)
                if s >= 1 and s + 2 < STEPS:
                    load(s + 2)
            sp.wait_ge(mset.sem, 16 * PARTS * STEPS)


def out_projection_phase(nc, m, a, sig):
    with ExitStack() as ctx:
        sb = buffers(nc, ctx)
        O = m.over.O
        OT = sb("op_OT", [P, 2, KD, P], F32)
        tdone, tcop, done, added = sig("op_transposed"), sig("op_copied"), sig("op_done"), sig("op_added")
        ps = m.ps
        block = ctx.enter_context(nc.Block())

        @block.tensor
        def _(pe):
            def turn(i):
                if i >= 2:
                    pe.wait_ge(tcop.sem, tcop.at(i - 1))
                for k in range(KD):
                    last = pe.transpose(ps[:, i % 2, k * P:(k + 1) * P], O[:, i, k * P:(k + 1) * P], m.ident[:])
                last.then_inc(tdone.sem, 1)
            turn(0)
            for i in range(NT):
                if i + 1 < NT:
                    turn(i + 1)
                pe.wait_ge(tcop.sem, tcop.at(i + 1))
                if i >= 2:
                    pe.wait_ge(added.sem, added.at(i - 1))
                for k in range(KD):
                    last = pe.matmul(ps[:, 2 + i % 2, 0:D], OT[:, i % 2, k, :], m.awT[:, 3, k, :], start=(k == 0),
                                     stop=(k == KD - 1))
                last.then_inc(done.sem, 1)

        @block.scalar
        def _(act):
            for i in range(NT):
                act.wait_ge(tdone.sem, tdone.at(i + 1))
                if i >= 2:
                    act.wait_ge(done.sem, done.at(i - 1))
                nc.scalar.copy(OT[:, i % 2].rearrange("p k t -> p (k t)"), ps[:, i % 2, 0:D]).then_inc(tcop.sem, 1)

        @block.vector
        def _(dve):
            for i in range(NT):
                dve.wait_ge(done.sem, done.at(i + 1))
                xt = m.x[:, i, :]
                nc.vector.tensor_tensor(xt, ps[:, 2 + i % 2, 0:D], xt, ALU.add).then_inc(added.sem, 1)
        for s in (tdone, tcop, done, added):
            s.phase_over(NT)


NE, HE = 8, 512
KH = HE // P
TOPK = 2
SLOT_TILES = (T * TOPK + NE * (P - 1)) // P
SLOTS = SLOT_TILES * P
W1_COLS, W2_COLS, W3_COLS = KD * HE, KH * HE, KH * D
EXPERT_COLS = 2 * (W1_COLS + W2_COLS + W3_COLS)
WS = 256.0


def expert_views(flat):
    out, at = [], 0
    for cols, n in ((W1_COLS, HE), (W2_COLS, HE), (W3_COLS, D)):
        out.append(flat[:, at:at + 2 * cols].rearrange("p (s k n) -> p s k n", s=2, n=n))
        at += 2 * cols
    return out


def expert_weights_phase(nc, m, a, sig):
    with ExitStack() as ctx:
        sb = buffers(nc, ctx)
        raw = sb("expert_raw", [P, 2, EXPERT_COLS // 2], F32)
        bn = sb("expert_bias_natural", [NE * KH, 2, P], F32)
        zero = sb("zero_rows", [P, 2 * D], F16)
        loaded = [sig("ew_loaded_even"), sig("ew_loaded_odd")]
        biases, hi, lo = sig("ew_biases_loaded"), sig("ew_hi"), sig("ew_lo")
        tdone, zeroed, cleared = sig("ew_bias_transposed"), sig("ew_zeroed"), sig("ew_cleared")
        chain = sig("ew_chain")
        block = ctx.enter_context(nc.Block())
        stages = ((a["L1_ffn_W1"], 0, W1_COLS), (a["L1_ffn_W2"], W1_COLS, W2_COLS), (a["L1_ffn_W3"], W1_COLS + W2_COLS, W3_COLS))

        @block.sync
        def _(sp):
            for e in range(NE):
                if e >= 2:
                    sp.wait_ge(lo.sem, lo.at(3 * (e - 1)))
                for w, at, cols in stages:
                    sp.dma_start(raw[:, e % 2, at:at + cols].rearrange("p (k n) -> p k n", n=w.shape[2]),
                                 w[e].rearrange("(k p) n -> p k n", p=P)).then_inc(loaded[e % 2].sem, 16)
                if e == 0:
                    for n, v in enumerate((a["L1_ffn_b1"], a["L1_ffn_b2"])):
                        sp.dma_start(bn[:, n, :], v.rearrange("e (m p) -> (e m) p", p=P)).then_inc(biases.sem, 16)
                    sp.dma_start(m.wg[:], a["L1_ffn_Wg"].rearrange("(k p) n -> p k n", p=P)).then_inc(biases.sem, 16)
                    sp.dma_start(m.bg[:], a["L1_ffn_bg"].rearrange("(a n) -> a n", a=1).broadcast_to([P, NE])).then_inc(biases.sem, 16)
                    sp.dma_start(m.tri[:], a["c_before"]).then_inc(biases.sem, 16)
                    sp.dma_start(m.eiota[:], a["c_experts"]).then_inc(biases.sem, 16)
                    sp.dma_start(m.starts[:], a["c_tile_starts"]).then_inc(biases.sem, 16)
            sp.wait_ge(biases.sem, biases.at(16 * 7))

        @block.gpsimd
        def _(pool):
            nc.gpsimd.memset(zero[:], 0.0).then_inc(cleared.sem, 1)
            pool.wait_ge(cleared.sem, cleared.at(1))
            for t in range(SLOT_TILES):
                pool.dma_start(a["moe_rows"][t * P:(t + 1) * P, :], zero[:]).then_inc(zeroed.sem, 16)
            pool.wait_ge(zeroed.sem, zeroed.at(16 * SLOT_TILES))

        @block.tensor
        def _(pe):
            pe.wait_ge(biases.sem, biases.at(16 * 7))
            for n in range(2):
                last = pe.transpose(m.ps[:, 0, n * NE * KH:(n + 1) * NE * KH], bn[:, n, :], m.ident[0:NE * KH, 0:NE * KH])
            last.then_inc(tdone.sem, 1)

        @block.scalar
        def _(act):
            for e in range(NE):
                act.wait_ge(loaded[e % 2].sem, loaded[e % 2].at(48 * (e // 2 + 1)))
                views = expert_views(m.we[:, e, :])
                for n, (w, at, cols) in enumerate(stages):
                    src = raw[:, e % 2, at:at + cols].rearrange("p (k n) -> p k n", n=w.shape[2])
                    nc.scalar.mul(views[n][:, 0], src, WS).then_inc(hi.sem, 1)

        @block.vector
        def _(dve):
            dve.wait_ge(tdone.sem, tdone.at(1))
            nc.vector.tensor_copy(m.eb12[:], m.ps[:, 0, 0:2 * NE * KH].rearrange("p (n e c) -> p e n c", n=2, e=NE))
            for e in range(NE):
                dve.wait_ge(loaded[e % 2].sem, loaded[e % 2].at(48 * (e // 2 + 1)))
                views = expert_views(m.we[:, e, :])
                for n, (w, at, cols) in enumerate(stages):
                    src = raw[:, e % 2, at:at + cols].rearrange("p (k n) -> p k n", n=w.shape[2])
                    dve.wait_ge(hi.sem, hi.at(3 * e + n + 1))
                    nc.vector.scalar_tensor_tensor(out=views[n][:, 1], in0=src, scalar=WS, in1=views[n][:, 0],
                                                   op0=ALU.mult, op1=ALU.subtract).then_inc(lo.sem, 1)


def routing_phase(nc, m, a, sig):
    with ExitStack() as ctx:
        sb = buffers(nc, ctx)
        y = sb("rt_y", [P, 2, GT, D], F32)
        yT = sb("rt_yT", [P, 2, KD, GT * P], F32)
        bn = sb("rt_bn_stats", [P, NT, 6], F32)
        mv = sb("rt_bn_mean_var", [P, NT, 2], F32)
        var_, rstd_, work = (sb(f"rt_{n}", [P, NT], F32) for n in ("variance", "root", "newton"))
        HT = NT // 2
        rows = sb("rt_rows", [P, NT, 2 * D], F16)
        big = [sb(f"rt_big{n}", [P, NT, NE], F32) for n in range(8)]
        small = [sb(f"rt_small{n}", [P, NT], F32) for n in range(6)]
        ends = sb("rt_ends", [P, 6, NE], F32)
        te = sb("rt_tile_expert", [1, 2, SLOT_TILES + 1, NE], F32)
        tr = sb("rt_tile_sum", [1, 2, SLOT_TILES + 1], F32)
        one = sb("rt_one", [P, NT], F32)
        var, rstd, normed = sig("rt_var"), sig("rt_rstd"), sig("rt_normed")
        tdone, yready, gated = sig("rt_transposed"), sig("rt_yT_ready"), sig("rt_gated")
        shifted, expd, chosen, counted = sig("rt_shifted"), sig("rt_exp"), sig("rt_chosen"), sig("rt_counted")
        placed, sent, chain, pchain = sig("rt_placed"), sig("rt_rows_sent"), sig("rt_chain"), sig("rt_pool_chain")
        split, low = sig("rt_rows_high"), sig("rt_rows_low")
        ps = m.ps
        logits, prob, h1, h2, eq, cand, both, base = big
        mx, i1, i2, w1, w2, rs = small
        block = ctx.enter_context(nc.Block())

        @block.tensor
        def _(pe):
            def turn(g):
                pe.wait_ge(normed.sem, normed.at(g + 1))
                if g >= 2:
                    pe.wait_ge(yready.sem, yready.at(g - 1))
                for k in range(KD):
                    for i in range(GT):
                        last = pe.transpose(ps[:, 5 * (g % 2) + k, i * P:(i + 1) * P], y[:, g % 2, i, k * P:(k + 1) * P], m.ident[:])
                last.then_inc(tdone.sem, 1)
            turn(0)
            for g in range(NG):
                if g + 1 < NG:
                    turn(g + 1)
                pe.wait_ge(yready.sem, yready.at(g + 1))
                for i in range(GT):
                    t = g * GT + i
                    for k in range(KD):
                        last = pe.matmul(ps[:, 2, t * NE:(t + 1) * NE], yT[:, g % 2, k, i * P:(i + 1) * P], m.wg[:, k, :],
                                         start=(k == 0), stop=(k == KD - 1))
                last.then_inc(gated.sem, 1)
            pe.wait_ge(chosen.sem, chosen.at(1))
            flat = both[:].rearrange("p t e -> p (t e)")
            pe.matmul(ps[:, 3, 0:NT * NE], m.tri[:], flat, start=True, stop=True)
            pe.matmul(ps[:, 4, 0:NT * NE], m.ones[:], flat, start=True, stop=True).then_inc(counted.sem, 1)

        @block.scalar
        def _(act):
            for g in range(NG):
                act.wait_ge(tdone.sem, tdone.at(g + 1))
                if g >= 2:
                    act.wait_ge(gated.sem, gated.at(g - 1))
                at = 5 * (g % 2)
                nc.scalar.copy(yT[:, g % 2], ps[:, at:at + 2, :]).then_inc(yready.sem, 1)
                nc.scalar.copy(rows[:, g * GT:(g + 1) * GT, 0:D], y[:, g % 2]).then_inc(split.sem, 1)
            act.wait_ge(shifted.sem, shifted.at(1))
            nc.scalar.activation(prob[:], logits[:], ACT.Exp).then_inc(expd.sem, 1)

        @block.vector
        def _(dve):
            link = linker(dve, chain)
            v = nc.vector
            link(v.memset(one[:], 1.0))
            for h in range(2):
                half = slice(h * HT, (h + 1) * HT)
                for t in range(h * HT, (h + 1) * HT):
                    ins = v.bn_stats(bn[:, t, :], m.x[:, t, :])
                link(ins)
                for t in range(h * HT, (h + 1) * HT):
                    ins = v.bn_aggr(mv[:, t, :], bn[:, t, :])
                link(ins)
                link(v.tensor_scalar(var_[:, half], mv[:, half, 1], EPS, 1.0 / (YS * YS), ALU.add, ALU.mult))
                guess_root(nc, link, var_[:, half], rstd_[:, half]).then_inc(var.sem, 1)
            for g in range(NG):
                dve.wait_ge(rstd.sem, rstd.at(g // 2 + 1))
                if g >= 2:
                    dve.wait_ge(tdone.sem, tdone.at(g - 1))
                    dve.wait_ge(split.sem, split.at(g - 1))
                    dve.wait_ge(low.sem, low.at(g - 1))
                for i in range(GT):
                    t = g * GT + i
                    ins = v.tensor_scalar(y[:, g % 2, i, :], m.x[:, t, :], mv[:, t, 0:1], rstd_[:, t:t + 1], ALU.subtract, ALU.mult)
                ins.then_inc(normed.sem, 1)

            def over(t, shape=(P, NT, NE)):
                return t[:, :, None].broadcast_to(list(shape))
            dve.wait_ge(gated.sem, gated.at(NG))
            iota = m.eiota[:]
            link(v.scalar_tensor_tensor(out=logits[:], in0=ps[:, 2, 0:NT * NE].rearrange("p (t e) -> p t e", e=NE),
                                        scalar=1.0 / YS, in1=m.bg[:, None, :].broadcast_to([P, NT, NE]),
                                        op0=ALU.mult, op1=ALU.add))
            link(v.tensor_reduce(mx[:], logits[:], AX.X, ALU.max))
            v.tensor_tensor(logits[:], logits[:], over(mx), ALU.subtract).then_inc(shifted.sem, 1)
            dve.wait_ge(expd.sem, expd.at(1))
            link(v.tensor_reduce(rs[:], prob[:], AX.X, ALU.add))
            link(v.reciprocal(rs[:], rs[:]))
            link(v.tensor_tensor(prob[:], prob[:], over(rs), ALU.mult))
            for n, (w, idx, hot) in enumerate(((w1, i1, h1), (w2, i2, h2))):
                link(v.tensor_reduce(w[:], prob[:], AX.X, ALU.max))
                link(v.tensor_tensor(eq[:], prob[:], over(w), ALU.is_equal))
                link(v.scalar_tensor_tensor(out=cand[:], in0=eq[:], scalar=-float(NE), in1=iota, op0=ALU.mult, op1=ALU.add))
                link(v.tensor_reduce(idx[:], cand[:], AX.X, ALU.min))
                link(v.tensor_scalar(idx[:], idx[:], float(NE), None, ALU.add))
                link(v.tensor_tensor(hot[:], iota, over(idx), ALU.is_equal))
                link(v.tensor_scalar(m.weight[:, :, n], w[:], 0.5, None, ALU.mult))
                if n == 0:
                    link(v.scalar_tensor_tensor(out=prob[:], in0=hot[:], scalar=-2.0, in1=prob[:], op0=ALU.mult, op1=ALU.add))
            v.tensor_tensor(both[:], h1[:], h2[:], ALU.add).then_inc(chosen.sem, 1)
            dve.wait_ge(counted.sem, counted.at(1))
            total = cand
            link(v.tensor_copy(total[:], ps[:, 4, 0:NT * NE].rearrange("p (t e) -> p t e", e=NE)))
            for e in range(NE):
                ins = v.tensor_tensor_scan(logits[:, :, e], one[:], total[:, :, e], 0.0, ALU.mult, ALU.add)
            link(ins)
            n_, pad, end, start, up, rem = (ends[:, k, :] for k in range(6))
            link(v.tensor_scalar(up, logits[:, NT - 1, :], float(P - 1), None, ALU.add))
            link(v.tensor_scalar(rem.bitcast(I32), up, 0.0, None, ALU.add))
            link(v.tensor_scalar(rem.bitcast(I32), rem.bitcast(I32), 7, None, ALU.arith_shift_right))
            link(v.tensor_scalar(pad, rem.bitcast(I32), float(P), None, ALU.mult))
            link(v.tensor_tensor_scan(end, one[:, 0:NE], pad, 0.0, ALU.mult, ALU.add))
            link(v.tensor_tensor(start, end, pad, ALU.subtract))
            link(v.tensor_tensor(base[:], logits[:], total[:], ALU.subtract))
            link(v.tensor_tensor(base[:], base[:], start[:, None, :].broadcast_to([P, NT, NE]), ALU.add))
            link(v.tensor_tensor(base[:], ps[:, 3, 0:NT * NE].rearrange("p (t e) -> p t e", e=NE), base[:], ALU.add))
            for n, hot in enumerate((h1, h2)):
                link(v.tensor_tensor(eq[:], hot[:], base[:], ALU.mult))
                link(v.tensor_reduce(mx[:], eq[:], AX.X, ALU.add))
                v.tensor_copy(m.slot[:, :, n], mx[:]).then_inc(placed.sem, 1)
                dve.wait_ge(placed.sem, placed.at(n + 1))
            nt = SLOT_TILES
            link(v.tensor_tensor(te[:, 0, 0:nt, :], end[0:1, None, :].broadcast_to([1, nt, NE]),
                                 m.starts[0:1, :, None].broadcast_to([1, nt, NE]), ALU.is_le))
            link(v.tensor_reduce(tr[:, 0, 0:nt], te[:, 0, 0:nt, :], AX.X, ALU.add))
            link(v.tensor_scalar(m.tile_expert[:], tr[:, 0, 0:nt], float(NE - 1), None, ALU.min))

        @block.gpsimd
        def _(pool):
            link = linker(pool, pchain)
            for h in range(2):
                half = slice(h * HT, (h + 1) * HT)
                pool.wait_ge(var.sem, var.at(h + 1))
                refine_root(nc, link, var_[:, half], rstd_[:, half], work[:, half]).then_inc(rstd.sem, 1)
            for g in range(NG):
                r = rows[:, g * GT:(g + 1) * GT, :]
                pool.wait_ge(split.sem, split.at(g + 1))
                nc.gpsimd.tensor_tensor(r[:, :, D:2 * D], y[:, g % 2], r[:, :, 0:D], ALU.subtract).then_inc(low.sem, 1)
            pool.wait_ge(low.sem, low.at(NG))
            pool.wait_ge(placed.sem, placed.at(2))
            for t in range(NT):
                for n in range(TOPK):
                    pool.indirect_dma_start(out=a["moe_rows"][:, :], out_offset=bass.IndirectOffsetOnAxis(ap=m.slot[:, t, n:n + 1], axis=0),
                                            in_=rows[:, t, :], in_offset=None).then_inc(sent.sem, 16)
            pool.wait_ge(sent.sem, sent.at(16 * NT * TOPK))
        for s, n in ((var, 2), (rstd, 2), (low, NG), (normed, NG), (tdone, NG), (yready, NG), (gated, NG), (shifted, 1), (expd, 1),
                     (chosen, 1), (counted, 1), (placed, 2), (sent, 16 * NT * TOPK), (split, NG),
                     (chain, chain.links), (pchain, pchain.links)):
            s.phase_over(n)


def expert_phase(nc, m, a, sig):
    with ExitStack() as ctx:
        sb = buffers(nc, ctx)
        xt = sb("ex_rows", [P, 2, 2 * D], F16)
        yT = sb("ex_yT", [P, 2, 2, KD, P], F16)
        wr = sb("ex_weights", [P, 2, EXPERT_COLS], F16)
        bb = sb("ex_biases", [P, 2, 2, KH], F32)
        g32 = sb("ex_gelu", [P, 2, KH, P], F32)
        gp = sb("ex_gelu_parts", [P, 2, 2, 2, KH, P], F16)
        eo = sb("ex_out", [P, 2, D], F32)
        b3 = sb("ex_b3", [P, NE, D], F32)
        b3_loaded = sig("ex_b3_loaded")
        loaded = [sig("ex_rows_loaded_even"), sig("ex_rows_loaded_odd")]
        stored = [sig("ex_out_stored_even"), sig("ex_out_stored_odd")]
        tdone, yready, out_ready = sig("ex_transposed"), sig("ex_yT_ready"), sig("ex_out_ready")
        wready = [sig(f"ex_w{n}_ready") for n in (1, 2, 3)]
        layer = [sig(f"ex_layer{n}_done") for n in (1, 2, 3)]
        gelu = [sig(f"ex_gelu{n}_done") for n in (1, 2)]
        hi = [sig(f"ex_hi{n}_ready") for n in (1, 2)]
        lo = [sig(f"ex_lo{n}_ready") for n in (1, 2)]
        ps = m.ps
        views = [expert_views(wr[:, n, :]) for n in range(2)]
        block = ctx.enter_context(nc.Block())
        N = SLOT_TILES
        FIRST = 4
        OUTER = (N - 2 - FIRST) // 2
        AT = (0, 2 * W1_COLS, 2 * (W1_COLS + W2_COLS), EXPERT_COLS)

        def run(eng, body):
            def peeled(i):
                body(i, i % 2, i // 2, lambda o: 0 <= i + o < N)
            for i in range(FIRST):
                peeled(i)
            with eng.Fori(0, OUTER) as j:
                for u in range(2):
                    body(j * 2 + (FIRST + u), u, j + FIRST // 2, lambda o: True)
            for i in range(FIRST + 2 * OUTER, N + 2):
                peeled(i)

        def tile(i):
            return bass.ds(i * P, P)

        @block.sync
        def _(sp):
            for e in range(NE):
                sp.dma_start(b3[:, e, :], a["L1_ffn_b3"][e:e + 1, :].broadcast_to([P, D])).then_inc(b3_loaded.sem, 16)
            for t in range(2):
                sp.dma_start(xt[:, t, :], a["moe_rows"][t * P:(t + 1) * P, :]).then_inc(loaded[t].sem, 16)

            def body(i, par, half, stage):
                if stage(2) and (not isinstance(i, int) or i + 2 < N):
                    sp.wait_ge(tdone.sem, tdone.at(i + 1))
                    sp.dma_start(xt[:, par, :], a["moe_rows"][tile(i + 2), :]).then_inc(loaded[par].sem, 16)
                if stage(-2):
                    if due(i - 1):
                        sp.wait_ge(out_ready.sem, out_ready.at(i - 1))
                    sp.dma_start(a["moe_out"][tile(i - 2), :], eo[:, par, :]).then_inc(stored[par].sem, 16)
            run(sp, body)
            for par in range(2):
                sp.wait_ge(stored[par].sem, stored[par].at(16 * ((N + 1 - par) // 2)))

        @block.tensor
        def _(pe):
            def transposes(i, par, half):
                o = 1 - par
                if due((half + 1 + par) * 16):
                    pe.wait_ge(loaded[o].sem, loaded[o].at((half + 1 + par) * 16))
                if due(i):
                    pe.wait_ge(yready.sem, yready.at(i))
                bank = ps[:, o, :].bitcast(F16)
                for c in range(2 * KD):
                    last = pe.transpose(bank[:, c * P:(c + 1) * P], xt[:, o, c * P:(c + 1) * P], m.ident16[:])
                last.then_inc(tdone.sem, 1)

            def wide(bank, w, act, kn, done):
                for mo in range(KH):
                    for k in range(kn):
                        for n, (pw, pa) in enumerate(((0, 0), (0, 1), (1, 0))):
                            last = pe.matmul(bank[:, mo * P:(mo + 1) * P], w[:, pw, k, mo * P:(mo + 1) * P],
                                             act[:, pa, k, :], start=(k == 0 and n == 0), stop=(k == kn - 1 and n == 2))
                last.then_inc(done.sem, 1)

            def body(i, par, half, stage):
                if stage(0):
                    pe.wait_ge(yready.sem, yready.at(i + 1))
                    pe.wait_ge(wready[0].sem, wready[0].at(i + 1))
                    if due(i - 1):
                        pe.wait_ge(gelu[0].sem, gelu[0].at(i - 1))
                    wide(ps[:, 2 + par, :], views[par][0], yT[:, par], KD, layer[0])
                if stage(1):
                    transposes(i, par, half)
                if stage(-1):
                    if due(i):
                        pe.wait_ge(lo[0].sem, lo[0].at(i))
                    if due(i):
                        pe.wait_ge(wready[1].sem, wready[1].at(i))
                    if due(i - 2):
                        pe.wait_ge(gelu[1].sem, gelu[1].at(i - 2))
                    wide(ps[:, 5 - par, :], views[1 - par][1], gp[:, 0, 1 - par], KH, layer[1])
                if stage(-2):
                    if due(i - 1):
                        pe.wait_ge(lo[1].sem, lo[1].at(i - 1))
                    if due(i - 1):
                        pe.wait_ge(wready[2].sem, wready[2].at(i - 1))
                    if due(i - 3):
                        pe.wait_ge(out_ready.sem, out_ready.at(i - 3))
                    for k in range(KH):
                        for n, (pw, pa) in enumerate(((0, 0), (1, 0), (0, 1))):
                            last = pe.matmul(ps[:, 6 + par, 0:D], gp[:, 1, par, pa, k, :], views[par][2][:, pw, k, :],
                                             start=(k == 0 and n == 0), stop=(k == KH - 1 and n == 2))
                    last.then_inc(layer[2].sem, 1)
            transposes(-1, 1, -1)
            run(pe, body)

        @block.scalar
        def _(act):
            def layer_out(n, t, par, bank, scale, parts_free, freed):
                act.wait_ge(layer[n].sem, layer[n].at(t + 1))
                if due(t):
                    act.wait_ge(lo[n].sem, lo[n].at(t))
                for c in range(KH):
                    last = nc.scalar.activation(g32[:, n, c, :], bank[:, c * P:(c + 1) * P], ACT.Gelu,
                                                bias=bb[:, par, n, c:c + 1], scale=scale)
                last.then_inc(gelu[n].sem, 1)
                act.wait_ge(gelu[n].sem, gelu[n].at(t + 1))
                if due(t - 1):
                    act.wait_ge(parts_free.sem, parts_free.at(t - 1))
                nc.scalar.copy(gp[:, n, par, 0], g32[:, n]).then_inc(hi[n].sem, 1)

            def body(i, par, half, stage):
                if stage(0):
                    layer_out(0, i, par, ps[:, 2 + par, :], 1.0 / (YS * WS), layer[1], None)
                if stage(-1):
                    layer_out(1, i - 1, 1 - par, ps[:, 5 - par, :], 1.0 / WS, layer[2], None)
            run(act, body)

        @block.vector
        def _(dve):
            v = nc.vector

            def expert_of(t):
                if isinstance(t, int):
                    return dve.value_load(m.tile_expert[0:1, t:t + 1], min_val=0, max_val=NE - 1)
                return dve.value_load(m.tile_expert[0:1, bass.ds(t, 1)], min_val=0, max_val=NE - 1)

            def weights(n, t, par):
                e = expert_of(t)
                flat = m.we[:].rearrange("p e c -> p (e c)")
                if due(t - 1):
                    dve.wait_ge(layer[n].sem, layer[n].at(t - 1))
                if n < 2:
                    if due(t - 1):
                        dve.wait_ge(gelu[n].sem, gelu[n].at(t - 1))
                    v.tensor_copy(bb[:, par, n, :], m.eb12[:].rearrange("p e n c -> p (e n c)")[:, bass.ds(e * (2 * KH) + n * KH, KH)])
                c = AT[n + 1] - AT[n]
                v.tensor_copy(wr[:, par, AT[n]:AT[n + 1]], flat[:, bass.ds(e * EXPERT_COLS + AT[n], c)]).then_inc(wready[n].sem, 1)

            def low(n, t, par):
                dve.wait_ge(hi[n].sem, hi[n].at(t + 1))
                v.tensor_tensor(gp[:, n, par, 1], g32[:, n], gp[:, n, par, 0], ALU.subtract).then_inc(lo[n].sem, 1)

            def yT_copy(t, par):
                dve.wait_ge(tdone.sem, tdone.at(t + 1))
                if due(t - 1):
                    dve.wait_ge(layer[0].sem, layer[0].at(t - 1))
                v.tensor_copy(yT[:, par].rearrange("p s k t -> p (s k t)"), ps[:, par, 0:D].bitcast(F16)).then_inc(yready.sem, 1)

            weights(0, 0, 0)
            yT_copy(0, 0)
            dve.wait_ge(b3_loaded.sem, b3_loaded.at(16 * NE))

            def body(i, par, half, stage):
                if stage(1):
                    weights(0, i + 1, 1 - par)
                if stage(0):
                    weights(1, i, par)
                if stage(-1):
                    weights(2, i - 1, 1 - par)
                if stage(1):
                    yT_copy(i + 1, 1 - par)
                if stage(0):
                    low(0, i, par)
                if stage(-1):
                    low(1, i - 1, 1 - par)
                if stage(-2):
                    e = expert_of(i - 2)
                    if due(i - 1):
                        dve.wait_ge(layer[2].sem, layer[2].at(i - 1))
                    if not isinstance(half, int) or half > 1:
                        dve.wait_ge(stored[par].sem, stored[par].at((half - 1) * 16))
                    v.scalar_tensor_tensor(out=eo[:, par, :], in0=ps[:, 6 + par, 0:D], scalar=1.0 / WS,
                                           in1=b3[:].rearrange("p e d -> p (e d)")[:, bass.ds(e * D, D)],
                                           op0=ALU.mult, op1=ALU.add).then_inc(out_ready.sem, 1)
            run(dve, body)
        for s in [tdone, yready, out_ready] + wready + layer + gelu + hi + lo:
            s.phase_over(N)
        b3_loaded.phase_over(16 * NE)
        for par in range(2):
            loaded[par].phase_over(16 * ((N + 1 - par) // 2))
            stored[par].phase_over(16 * ((N + 1 - par) // 2))


def combine_phase(nc, m, a, sig):
    with ExitStack() as ctx:
        sb = buffers(nc, ctx)
        R = 4
        got = sb("co_rows", [P, R, TOPK, D], F32)
        here = [sig(f"co_rows_here{n}") for n in range(R)]
        added = sig("co_added")
        stored = sig("x_loaded")
        out = a["out"].rearrange("b s d -> (b s) d").rearrange("(i p) d -> p i d", p=P)
        block = ctx.enter_context(nc.Block())

        @block.gpsimd
        def _(pool):
            for t in range(NT):
                if t >= R:
                    pool.wait_ge(added.sem, 2 * (t - R + 1))
                for n in range(TOPK):
                    pool.indirect_dma_start(out=got[:, t % R, n, :], out_offset=None, in_=a["moe_out"][:, :],
                                            in_offset=bass.IndirectOffsetOnAxis(ap=m.slot[:, t, n:n + 1], axis=0)
                                            ).then_inc(here[t % R].sem, 16)

        @block.vector
        def _(dve):
            for t in range(NT):
                dve.wait_ge(here[t % R].sem, here[t % R].at(16 * TOPK * (t // R + 1)))
                for n in range(TOPK):
                    nc.vector.scalar_tensor_tensor(out=m.x[:, t, :], in0=got[:, t % R, n, :], scalar=m.weight[:, t, n:n + 1],
                                                   in1=m.x[:, t, :], op0=ALU.mult, op1=ALU.add).then_inc(added.sem, 1)
                    dve.wait_ge(added.sem, 2 * t + n + 1)

        @block.sync
        def _(sp):
            for t in range(0, NT, 2):
                sp.wait_ge(added.sem, TOPK * (t + 2))
                sp.dma_start(out[:, t:t + 2, :], m.x[:, t:t + 2, :]).then_inc(stored.sem, 16)
            sp.wait_ge(stored.sem, stored.at(16 * NT // 2))


def moe_phases(nc, m, a, sig):
    routing_phase(nc, m, a, sig)
    expert_phase(nc, m, a, sig)


def retention_phase(nc, m, a, sig):
    with ExitStack() as ctx:
        sb = buffers(nc, ctx)
        HC = NH // KD
        wqkvg = sb("re_w_qkvg", [P, KD, 4 * D], F32)
        wproj = sb("re_w_proj", [P, KD, D], F32)
        gn = sb("re_gn", [P, 2, D], F32)
        decay = sb("re_decay", [P, NH, P], F32)
        qdec = sb("re_q_decay", [P, KD, P], F32)
        kdec = sb("re_k_decay", [P, D], F32)
        heads = sb("re_head_rows", [P, HC], F32)
        sdec = sb("re_state_decay", [P, KD], F32)
        rot = sb("re_rotation", [P, 2, D], F32)
        y = sb("re_y", [P, 1, D], F32)
        yT = sb("re_yT", [P, KD, P], F32)
        qk = sb("re_qk", [P, 2, D], F32)
        t2 = sb("re_swapped", [P, 2, D], F32)
        V = sb("re_v", [P, 2, NH, HP], F32)
        gate = sb("re_gate", [P, 2, D], F32)
        qT = sb("re_qT", [P, KD, P], F32)
        kT = sb("re_kT", [P, 2, KD, P], F32)
        qdT = sb("re_q_decayed", [P, KD, P], F32)
        kd = sb("re_k_decayed", [P, D], F32)
        qx = sb("re_q_by_head", [P, KD, HC, P], F32)
        pt = sb("re_weights", [P, 2, HC // 2, P], F32)
        state = sb("re_state", [P, KD, HC * HP], F32)
        upd = t2
        oT = sb("re_oT", [P, 4 * P], F32)
        cent = sb("re_centred", [P, NH, HD], F32)
        sq = t2[:, 0, :].rearrange("p (h d) -> p h d", h=NH)
        roots = sb("re_roots", [P, 3, 1 + NH], F32)
        sums = sb("re_sums", [P, NH], F32)
        nT = y[:, 0, :].rearrange("p (k t) -> p k t", k=KD)
        got = sb("re_expert_rows", [P, TOPK, D], F32)
        names = ("loaded rot cleared guessed rooted normed yturned yT qkproj vgproj rotated vready gated qkturned qkT qdT kd qx0 qx1 combined "
                 "scored weighed retained updated stated oT oturned centred mixed nturned nT projected added "
                 "chain pchain heard").split()
        g = {n: sig("re_" + n) for n in names}
        here = [sig(f"co_rows_here{n}") for n in range(TOPK)]
        ps = m.ps
        v, pl = nc.vector, nc.gpsimd
        N = NT

        def rooted(i):
            return slice(0 if i + 1 < N else 1, 1 + NH if 0 <= i - 2 < N else 1)
        block = ctx.enter_context(nc.Block())
        NLOAD = 10

        @block.sync
        def _(sp):
            kp = "(k p) n -> p k n"
            row = lambda w: w.rearrange("(a d) -> a d", a=1).broadcast_to([P, D])
            for dst, src in ((wqkvg[:, :, 0:3 * D], a["L1_attn_w_qkv"].rearrange(kp, p=P)),
                             (wqkvg[:, :, 3 * D:], a["L1_attn_w_g"].rearrange(kp, p=P)), (wproj[:], a["L1_attn_w_proj"].rearrange(kp, p=P)),
                             (gn[:, 0, :], row(a["L1_attn_gn_weight"])), (gn[:, 1, :], row(a["L1_attn_gn_bias"])),
                             (decay[:], a["c_decay"]), (qdec[:], a["c_q_decay"]), (kdec[:], a["c_k_decay"]),
                             (heads[:], a["c_head_rows"]), (sdec[:], a["c_state_decay"])):
                sp.dma_start(dst, src).then_inc(g["loaded"].sem, 16)
            for i in range(N):
                if i > 0:
                    sp.wait_ge(g["rotated"].sem, i)
                sp.dma_start(rot[:], a["c_rotation"][i % BT]).then_inc(g["rot"].sem, 16)
            sp.wait_ge(g["loaded"].sem, 16 * NLOAD)

        @block.tensor
        def _(pe):
            pe.wait_ge(g["loaded"].sem, 16 * NLOAD)
            for i in range(N + 3):
                r, o, q = i - 1, i - 2, i - 3
                if i < N:
                    pe.wait_ge(g["normed"].sem, i + 1)
                    if 0 < q:
                        pe.wait_ge(g["nT"].sem, q)
                    for k in range(KD):
                        last = pe.transpose(ps[:, 0, k * P:(k + 1) * P], y[:, 0, k * P:(k + 1) * P], m.ident[:])
                    last.then_inc(g["yturned"].sem, 1)

                def scores(p):
                    c, n = p // 2, 4 * r + p
                    if p % 2 == 0:
                        pe.wait_ge(g["qx" + str(c)].sem, r + 1)
                    if n >= 2:
                        pe.wait_ge(g["weighed"].sem, n - 1)
                    pe.matmul(ps[:, 4 + p % 2, :], kT[:, r % 2, c, :], qx[:, c, p % 2 * 4:p % 2 * 4 + 4, :],
                              start=True, stop=True).then_inc(g["scored"].sem, 1)

                def retain(p):
                    c, n = p // 2, 4 * r + p
                    pe.wait_ge(g["weighed"].sem, n + 1)
                    if p == 0:
                        if r > 0:
                            pe.wait_ge(g["oT"].sem, r)
                            pe.wait_ge(g["stated"].sem, r)
                        pe.wait_ge(g["qdT"].sem, r + 1)
                        pe.wait_ge(g["vready"].sem, r + 1)
                    pe.matmul(ps[:, 6, p * P:(p + 1) * P], state[:, c, p % 2 * P:(p % 2 + 1) * P], qdT[:, c, :], start=True,
                              stop=False, skip_group_check=True)
                    for h in range(4):
                        last = pe.matmul(ps[h * HP:(h + 1) * HP, 6, p * P:(p + 1) * P], V[:, r % 2, p * 4 + h, :],
                                         pt[:, p % 2, h, :], start=False, stop=True, skip_group_check=True)
                    last.then_inc(g["retained"].sem, 1)

                def project(n, projected):
                    for k in range(KD):
                        last = pe.matmul(ps[:, 1 + n, :], yT[:, k, :], wqkvg[:, k, n * 512:(n + 1) * 512],
                                         start=(k == 0), stop=(k == KD - 1))
                    last.then_inc(projected.sem, 1)

                if 0 <= r < N:
                    scores(0)
                    scores(1)
                if 0 <= o < N:
                    pe.wait_ge(g["oT"].sem, o + 1)
                    pe.wait_ge(g["stated"].sem, o + 1)
                    for n in range(4):
                        last = pe.transpose(ps[:, 7, n * P:(n + 1) * P], oT[:, n * P:(n + 1) * P], m.ident[:])
                    last.then_inc(g["oturned"].sem, 1)
                if 0 <= q:
                    pe.wait_ge(g["mixed"].sem, q + 1)
                    pe.wait_ge(g["yT"].sem, min(N, i + 1))
                    for k in range(KD):
                        last = pe.transpose(ps[:, 0, k * P:(k + 1) * P], cent[:, k * 8:(k + 1) * 8, :].rearrange("p h d -> p (h d)"), m.ident[:])
                    last.then_inc(g["nturned"].sem, 1)
                if i < N:
                    pe.wait_ge(g["yT"].sem, i + 1)
                    if i > 0:
                        pe.wait_ge(g["rotated"].sem, i)
                    project(0, g["qkproj"])
                if 0 <= r < N:
                    retain(0)
                    scores(2)
                if 0 <= q:
                    pe.wait_ge(g["nT"].sem, q + 1)
                    pe.wait_ge(g["qkT"].sem, min(N, i))
                    if q > 0:
                        pe.wait_ge(g["added"].sem, q)
                    for k in range(KD):
                        last = pe.matmul(ps[:, 3, 0:D], nT[:, k, :], wproj[:, k, :], start=(k == 0), stop=(k == KD - 1))
                    last.then_inc(g["projected"].sem, 1)
                if i < N:
                    if i > 0:
                        pe.wait_ge(g["vready"].sem, i)
                        pe.wait_ge(g["gated"].sem, i)
                    project(1, g["vgproj"])
                if 0 <= r < N:
                    retain(1)
                    scores(3)
                if i < N:
                    pe.wait_ge(g["rotated"].sem, i + 1)
                    if q >= 0:
                        pe.wait_ge(g["added"].sem, q + 1)
                    for n in range(4):
                        last = pe.transpose(ps[:, 3, n * P:(n + 1) * P], qk[:, n // 2, (n % 2) * P:(n % 2 + 1) * P], m.ident[:])
                    last.then_inc(g["qkturned"].sem, 1)
                if 0 <= r < N:
                    retain(2)
                if 0 <= r < N:
                    retain(3)
                    pe.wait_ge(g["kd"].sem, r + 1)
                    if r > 0:
                        pe.wait_ge(g["centred"].sem, r)
                    for c in range(KD):
                        last = pe.matmul(ps[:, 7, c * HC * HP:(c + 1) * HC * HP], kd[:, c * P:(c + 1) * P],
                                         V[:, r % 2, c * HC:(c + 1) * HC, :].rearrange("p h d -> p (h d)"), start=True, stop=True)
                    last.then_inc(g["updated"].sem, 1)

        @block.scalar
        def _(act):
            for i in range(N + 3):
                r, q = i - 1, i - 3
                if i < N:
                    act.wait_ge(g["yturned"].sem, i + 1)
                    if i > 0:
                        act.wait_ge(g["vgproj"].sem, i)
                    nc.scalar.copy(yT[:].rearrange("p k t -> p (k t)"), ps[:, 0, 0:D]).then_inc(g["yT"].sem, 1)
                if 0 <= q:
                    act.wait_ge(g["nturned"].sem, q + 1)
                    if q > 0:
                        act.wait_ge(g["projected"].sem, q)
                    nc.scalar.copy(y[:, 0, :], ps[:, 0, 0:D]).then_inc(g["nT"].sem, 1)
                if i < N:
                    act.wait_ge(g["vgproj"].sem, i + 1)
                    if i >= 2:
                        act.wait_ge(g["updated"].sem, i - 1)
                    act.wait_ge(g["cleared"].sem, 2)
                    nc.scalar.copy(V[:, i % 2, :, 0:HD], ps[:, 2, 0:D].rearrange("p (h d) -> p h d", h=NH)).then_inc(g["vready"].sem, 1)
                    act.wait_ge(g["qkturned"].sem, i + 1)
                    if i >= 2:
                        act.wait_ge(g["scored"].sem, 4 * (i - 1))
                    nc.scalar.copy(kT[:, i % 2].rearrange("p k t -> p (k t)"), ps[:, 3, D:2 * D])
                    if i >= 1:
                        act.wait_ge(g["qx0"].sem, i)
                        act.wait_ge(g["qx1"].sem, i)
                        act.wait_ge(g["qdT"].sem, i)
                    nc.scalar.copy(qT[:].rearrange("p k t -> p (k t)"), ps[:, 3, 0:D]).then_inc(g["qkT"].sem, 1)
                if i < N:
                    if i >= 2:
                        act.wait_ge(g["mixed"].sem, i - 1)
                    nc.scalar.activation(gate[:, i % 2, :], ps[:, 2, D:2 * D], ACT.Silu).then_inc(g["gated"].sem, 1)
                if 0 <= r < N:
                    act.wait_ge(g["retained"].sem, 4 * r + 4)
                    if r > 0:
                        act.wait_ge(g["oturned"].sem, r)
                    nc.scalar.copy(oT[:], ps[:, 6, :]).then_inc(g["oT"].sem, 1)

        @block.vector
        def _(dve):
            link = linker(dve, g["chain"])
            v.memset(state[:], 0.0).then_inc(g["cleared"].sem, 1)
            v.memset(V[:], 0.0).then_inc(g["cleared"].sem, 1)
            dve.wait_ge(g["cleared"].sem, 2)
            dve.wait_ge(g["loaded"].sem, 16 * NLOAD)

            def norm_start(t):
                for n in range(TOPK):
                    dve.wait_ge(here[n].sem, here[n].at(16 * (t + 1)))
                    v.scalar_tensor_tensor(out=m.x[:, t, :], in0=got[:, n, :], scalar=m.weight[:, t, n:n + 1],
                                           in1=m.x[:, t, :], op0=ALU.mult, op1=ALU.add).then_inc(g["combined"].sem, 1)
                    dve.wait_ge(g["combined"].sem, TOPK * t + n + 1)
                if t > 0:
                    dve.wait_ge(g["normed"].sem, t)
                link(v.bn_stats(m.bn[:, 0, :], m.x[:, t, :]))
                link(v.bn_aggr(m.mv[:, 0, :], m.bn[:, 0, :]))
                link(v.tensor_scalar(roots[:, 0, 0:1], m.mv[:, 0, 1:2], EPS, None, ALU.add))

            def norm_end(t):
                dve.wait_ge(g["rooted"].sem, t + 1)
                if t > 0:
                    dve.wait_ge(g["yturned"].sem, t)
                v.tensor_scalar(y[:, 0, :], m.x[:, t, :], m.mv[:, 0, 0:1], roots[:, 1, 0:1], ALU.subtract,
                                ALU.mult).then_inc(g["normed"].sem, 1)
            norm_start(0)
            guess_root(nc, link, roots[:, 0, 0:1], roots[:, 1, 0:1]).then_inc(g["guessed"].sem, 1)
            norm_end(0)
            for i in range(N + 3):
                r, o, q = i - 1, i - 2, i - 3

                def weigh(p):
                    n = 4 * r + p
                    dve.wait_ge(g["scored"].sem, n + 1)
                    if n >= 2:
                        dve.wait_ge(g["retained"].sem, n - 1)
                    v.tensor_tensor(pt[:, p % 2], ps[:, 4 + p % 2, :].rearrange("p (h t) -> p h t", t=P),
                                    decay[:, 4 * p:4 * p + 4, :], ALU.mult).then_inc(g["weighed"].sem, 1)
                if 0 <= r < N:
                    weigh(0)
                    weigh(1)
                if i + 1 < N:
                    norm_start(i + 1)
                if 0 <= o < N:
                    dve.wait_ge(g["oturned"].sem, o + 1)
                    if o > 0:
                        dve.wait_ge(g["nturned"].sem, o)
                    ov = ps[:, 7, :].rearrange("p (h d) -> p h d", h=NH)[:, :, 0:HD]
                    link(v.tensor_reduce(sums[:], ov, AX.X, ALU.add))
                    v.scalar_tensor_tensor(out=cent[:], in0=sums[:, :, None].broadcast_to([P, NH, HD]), scalar=-1.0 / HD,
                                           in1=ov, op0=ALU.mult, op1=ALU.add).then_inc(g["centred"].sem, 1)
                    dve.wait_ge(g["centred"].sem, o + 1)
                    link(v.tensor_tensor(sq, cent[:], cent[:], ALU.mult))
                    link(v.tensor_reduce(sums[:], sq, AX.X, ALU.add))
                    link(v.tensor_scalar(roots[:, 0, 1:], sums[:], 1.0 / HD, EPS, ALU.mult, ALU.add))
                if i + 1 < N or 0 <= o < N:
                    guess_root(nc, link, roots[:, 0, rooted(i)], roots[:, 1, rooted(i)]).then_inc(g["guessed"].sem, 1)
                if i < N:
                    rw = rot[:]
                    src = ps[:, 1, :].rearrange("p (n d) -> p n d", n=2)
                    pair = lambda t: t.rearrange("p n (d e) -> p n d e", e=2)
                    sin = rw[:, 1:2, :].rearrange("p n (d e) -> p n d e", e=2)
                    dve.wait_ge(g["qkproj"].sem, i + 1)
                    dve.wait_ge(g["rot"].sem, 16 * (i + 1))
                    if i > 0:
                        dve.wait_ge(g["qkturned"].sem, i)
                        dve.wait_ge(g["kd"].sem, i)
                    v.tensor_tensor(qk[:], src, rw[:, 0:1, :].broadcast_to([P, 2, D]), ALU.mult)
                    for e in range(2):
                        ins = v.tensor_tensor(pair(t2[:])[:, :, :, e], pair(src)[:, :, :, 1 - e],
                                              sin[:, :, :, e].broadcast_to([P, 2, D // 2]), ALU.mult)
                    link(ins)
                    v.tensor_tensor(qk[:], qk[:], t2[:], ALU.add).then_inc(g["rotated"].sem, 1)
                if 0 <= q:
                    dve.wait_ge(g["projected"].sem, q + 1)
                    xt = m.x[:, q, :]
                    v.tensor_tensor(xt, ps[:, 3, 0:D], xt, ALU.add).then_inc(g["added"].sem, 1)
                if 0 <= r < N:
                    weigh(2)
                    weigh(3)
                if i + 1 < N:
                    norm_end(i + 1)
                if i < N:
                    dve.wait_ge(g["qkT"].sem, i + 1)
                    if i > 0:
                        dve.wait_ge(g["scored"].sem, 4 * i - 2)
                    v.tensor_tensor(qx[:, 0], qT[:, 0:1, :].broadcast_to([P, HC, P]),
                                    heads[:, :, None].broadcast_to([P, HC, P]), ALU.mult).then_inc(g["qx0"].sem, 1)
                if 0 <= r < N:
                    dve.wait_ge(g["updated"].sem, r + 1)
                    dve.wait_ge(g["retained"].sem, 4 * r + 4)
                    if r % BT == BT - 1:
                        v.memset(state[:], 0.0).then_inc(g["stated"].sem, 1)
                    else:
                        link(v.tensor_tensor(upd[:].rearrange("p k (h d) -> p k h d", h=HC),
                                             ps[:, 7, :].rearrange("p (k h d) -> p k h d", k=KD, h=HC),
                                             heads[:, None, :, None].broadcast_to([P, KD, HC, HP]), ALU.mult))
                        for c in range(KD):
                            ins = v.scalar_tensor_tensor(out=state[:, c, :], in0=state[:, c, :], scalar=sdec[:, c:c + 1],
                                                         in1=upd[:, c, :], op0=ALU.mult, op1=ALU.add)
                        ins.then_inc(g["stated"].sem, 1)
                    dve.wait_ge(g["stated"].sem, r + 1)
                if i < N:
                    v.tensor_tensor(qdT[:], qT[:], qdec[:], ALU.mult).then_inc(g["qdT"].sem, 1)

        @block.gpsimd
        def _(pool):
            link = linker(pool, g["pchain"])

            def gather(t):
                for n in range(TOPK):
                    if t > 0:
                        pool.wait_ge(g["combined"].sem, TOPK * (t - 1) + n + 1)
                    pool.indirect_dma_start(out=got[:, n, :], out_offset=None, in_=a["moe_out"][:, :],
                                            in_offset=bass.IndirectOffsetOnAxis(ap=m.slot[:, t, n:n + 1], axis=0)
                                            ).then_inc(here[n].sem, 16)
            gather(0)
            gather(1)
            pool.wait_ge(g["loaded"].sem, 16 * NLOAD)
            pool.wait_ge(g["guessed"].sem, 1)
            refine_root(nc, link, *(roots[:, n, 0:1] for n in range(3))).then_inc(g["rooted"].sem, 1)
            for i in range(N + 3):
                r, o = i - 1, i - 2
                if i + 1 < N or 0 <= o < N:
                    pool.wait_ge(g["guessed"].sem, i + 2)
                    refine_root(nc, link, *(roots[:, n, rooted(i)] for n in range(3))).then_inc(g["rooted"].sem, 1)
                    pool.wait_ge(g["rooted"].sem, i + 2)
                if 0 <= o < N:
                    flat = cent[:].rearrange("p h d -> p (h d)")
                    link(pl.tensor_tensor(cent[:], cent[:], roots[:, 1, 1:, None].broadcast_to([P, NH, HD]), ALU.mult))
                    link(pl.tensor_tensor(flat, flat, gn[:, 0, :], ALU.mult))
                    link(pl.tensor_tensor(flat, flat, gn[:, 1, :], ALU.add))
                    pool.wait_ge(g["gated"].sem, o + 1)
                    pl.tensor_tensor(flat, flat, gate[:, o % 2, :], ALU.mult).then_inc(g["mixed"].sem, 1)
                if i + 2 < N:
                    gather(i + 2)
                if i < N:
                    pool.wait_ge(g["rotated"].sem, i + 1)
                    if i > 0:
                        pool.wait_ge(g["scored"].sem, 4 * i)
                    pool.wait_ge(g["qkT"].sem, i + 1)
                    pl.tensor_tensor(qx[:, 1], qT[:, 1:2, :].broadcast_to([P, HC, P]),
                                     heads[:, :, None].broadcast_to([P, HC, P]), ALU.mult).then_inc(g["qx1"].sem, 1)
                    if r >= 0:
                        pool.wait_ge(g["updated"].sem, i)
                    pl.tensor_tensor(kd[:], qk[:, 1, :], kdec[:], ALU.mult).then_inc(g["kd"].sem, 1)
        for s in here:
            s.phase_over(16 * NT)


def macaron(nc, a, stages=6, first=0):
    ctx = ExitStack()
    with ctx:
        sb = buffers(nc, ctx)

        USED.clear()
        sems = {}

        def sig(name):
            if name not in sems:
                sems[name] = Signal(ctx.enter_context(nc.semaphore(name)))
            return sems[name]

        m = Memory()
        m.x = sb("x", [P, NT, D], F32)
        m.ident = sb("ident", [P, P], F32)
        m.ident16 = sb("ident16", [P, P], F16)
        m.ones = sb("ones", [P, P], F32)
        m.bn = sb("bn_stats", [P, GT, 6], F32)
        m.mv = sb("bn_mean_var", [P, GT, 2], F32)
        m.var = sb("variance", [P, GT], F32)
        m.rstd = sb("rstd", [P, GT], F32)
        m.nt = sb("newton", [P, GT], F32)
        m.ps = ctx.enter_context(nc.psum_tensor("ps", [P, 8, 512], F32))
        a["qk_parts"] = nc.dram_tensor("qk_parts", (2, PARTS, D, T), BF16, kind="Internal").ap()
        a["moe_rows"] = nc.dram_tensor("moe_rows", (SLOTS, 2 * D), F16, kind="Internal").ap()
        a["moe_out"] = nc.dram_tensor("moe_out", (SLOTS, D), F32, kind="Internal").ap()
        m.we = sb("expert_weights", [P, NE, EXPERT_COLS], F16)
        m.over = Overlay(m.we)
        m.eb12 = sb("expert_b12", [P, NE, 2, KH], F32)
        m.wg = sb("gate_w", [P, KD, NE], F32)
        m.bg = sb("gate_b", [P, NE], F32)
        m.tri = sb("before", [P, P], F32)
        m.eiota = sb("experts", [P, NT, NE], F32)
        m.starts = sb("tile_starts", [1, SLOT_TILES], F32)
        m.slot = sb("slots", [P, NT, TOPK], I32)
        m.weight = sb("mix_weights", [P, NT, TOPK], F32)
        m.tile_expert = sb("tile_expert", [1, SLOT_TILES], I32)
        with ExitStack() as inner:
            sb = buffers(nc, inner)
            m.b2h = sb("ffn_b2_half", [P, D], F32)
            m.b1T = sb("ffn_b1T", [P, NF], F32)
            m.w1qT = sb("w1qT", [P, KD, F0], F16)
            m.w2qT = sb("w2qT", [P, NF, D], F16)
            with ExitStack() as innermost:
                sb = buffers(nc, innermost)
                m.bqkT = sb("attn_bqkT", [P, 2, KD], F32)
                m.bvo = sb("attn_bvo", [P, 2, D], F32)
                m.awT = sb("attn_wT", [P, 4, KD, D], F32)
                m.mask_loaded = sb("causal_mask_loaded", [P, 2, P], F32)
                m.mask16 = sb("causal_mask", [P, 2, P], BF16)
                m.identb = sb("ident_bf16", [P, P], BF16)
                quantize_phase(nc, m, a, sig)
                if first <= 0 < stages:
                    ffn_phase(nc, m, a, sig)
                if first <= 1 < stages:
                    transpose_weights_phase(nc, m, a, sig)
                    attend_phase(nc, m, a, sig)
                    out_projection_phase(nc, m, a, sig)
            if first <= 2 < stages:
                ffn_phase(nc, m, a, sig, experts=True)
        if stages > 3:
            if first > 2:
                expert_weights_phase(nc, m, a, sig)
            moe_phases(nc, m, a, sig)
            if stages > 4:
                retention_phase(nc, m, a, sig)
            if stages > 5:
                moe_phases(nc, m, a, sig)
            combine_phase(nc, m, a, sig)


def retention_constants():
    c = {}
    f = np.float32
    gamma = 1.0 - 2.0 ** (-5.0 - np.arange(NH, dtype=np.float64))
    i = np.arange(P)
    scale = HD ** -0.5
    late = i[None, None, :] - i[:, None, None]
    c["c_decay"] = np.where(late >= 0, gamma[None, :, None] ** np.maximum(late, 0) * scale, 0).astype(f)
    head = np.arange(D) // HD
    by_channel = gamma[head].reshape(KD, P).T
    c["c_q_decay"] = (by_channel[:, :, None] ** (i + 1)[None, None, :] * scale).astype(f)
    c["c_k_decay"] = (gamma[head][None, :] ** (P - 1 - i)[:, None]).astype(f)
    c["c_state_decay"] = (by_channel ** P).astype(f)
    own = (i[:, None] // HD) == np.arange(NH // KD)[None, :]
    c["c_head_rows"] = own.astype(f)
    pair = np.arange(0, D, 2, dtype=f)
    dim_scale = (pair + f(0.4 * D)) / f(1.4 * D)
    pos = np.arange(S, dtype=f)
    xs = dim_scale[None, :] ** (pos[:, None] / f(512.0))
    inv_freq = f(1.0) / f(10000.0) ** (pair / f(D))
    angle = pos[:, None] * inv_freq[None, :]
    sin, cos = np.sin(angle) * xs, np.cos(angle) * xs
    rotation = np.stack([np.repeat(cos, 2, axis=1), np.stack([-sin, sin], axis=-1).reshape(S, D)], axis=1)
    c["c_rotation"] = np.ascontiguousarray(rotation.reshape(BT, P, 2, D).astype(f))
    return c


def constants():
    c = {}
    c["c_ident"] = np.eye(P, dtype=np.float32)
    q, k = np.arange(P)[:, None], np.arange(P)[None, :]
    c["c_mask"] = np.stack([np.where(k > q, NEG, 0), np.where(q > k, NEG, 0)], axis=1).astype(np.float32)
    c["c_before"] = (q < k).astype(np.float32)
    c["c_experts"] = np.broadcast_to(np.arange(NE, dtype=np.float32), (P, NT, NE)).copy()
    c["c_tile_starts"] = (np.arange(SLOT_TILES, dtype=np.float32) * P)[None]
    c.update(retention_constants())
    return c


_INS = ['L0_attn_h', 'L0_attn_Wq', 'L0_attn_bq', 'L0_attn_Wk', 'L0_attn_bk', 'L0_attn_Wv', 'L0_attn_bv', 'L0_attn_Wo',
        'L0_attn_bo', 'L0_ffn_w1', 'L0_ffn_b1', 'L0_ffn_w2', 'L0_ffn_b2', 'L1_attn_w_qkv', 'L1_attn_w_g',
        'L1_attn_w_proj', 'L1_attn_gn_weight', 'L1_attn_gn_bias', 'L1_ffn_W1', 'L1_ffn_b1', 'L1_ffn_W2', 'L1_ffn_b2',
        'L1_ffn_W3', 'L1_ffn_b3', 'L1_ffn_Wg', 'L1_ffn_bg']


def kernel(**inputs):
    import concourse.bacc as _bacc
    from concourse import mybir as _mybir
    from concourse.bass_utils import run_bass_kernel_spmd as _run

    nc = _bacc.Bacc("TRN2", target_bir_lowering=False, num_devices=1)
    arrays, aps = {}, {}
    given = {name: np.ascontiguousarray(inputs[name]) for name in _INS}
    given.update(constants())
    for name, v in given.items():
        arrays[f"in_{name}"] = v
        aps[name] = nc.dram_tensor(f"in_{name}", v.shape, _mybir.dt.from_np(v.dtype), kind="ExternalInput").ap()
    aps["out"] = nc.dram_tensor("out_x", (B, S, D), F32, kind="ExternalOutput").ap()
    macaron(nc, aps)
    r = _run(nc, [arrays], core_ids=[0])
    return r.results[0]["out_x"]
```

```python
from contextlib import ExitStack

import numpy as np

import concourse.bass as bass
from concourse import mybir

P = 128
F32 = mybir.dt.float32
F16 = mybir.dt.float16
BF16 = mybir.dt.bfloat16
I32 = mybir.dt.int32
ALU = mybir.AluOpType
ACT = mybir.ActivationFunctionType
AX = mybir.AxisListType

B, S, D = 2, 1024, 256
T = B * S
NT = T // P
KD = D // P
F0 = 1024
NF = F0 // P
GT = 4
NG = NT // GT
EPS = 1e-5
YS = 256.0
NH = 16
HD = D // NH
BT = S // P
HP = 32
PARTS = 3
Q_PARTS = (0, 0, 0, 1, 1, 2)
K_PARTS = (0, 1, 2, 0, 1, 0)
QK = HD * len(Q_PARTS)
NEG = -1e30
HG = 4
STEP_BUFFERS = 3


class Signal:

    def __init__(self, sem):
        self.sem, self.past, self.links = sem, 0, 0

    def at(self, n):
        return n + self.past

    def phase_over(self, n):
        self.past += n


def buffers(nc, ctx):
    def sb(name, shape, dt):
        used = sb.used[name] = sb.used.get(name, 0) + 1
        return ctx.enter_context(nc.sbuf_tensor(name if used == 1 else f"{name}_{used}", shape, dt))
    sb.used = USED
    return sb


USED = {}


def due(n):
    return not isinstance(n, int) or n > 0


class Memory:
    pass


class Overlay:

    def __init__(self, whole):
        self.flat, self.at = whole[:].rearrange("p e c -> p (e c)"), 0
        self.V = self.place([NT, NH, HP], F32, "p (t h d) -> p t h d", t=NT, h=NH)
        self.O = self.place([NT, D], F32, "p (t d) -> p t d", t=NT)
        self.Qp = self.place([STEP_BUFFERS, HG, S], BF16, "p (r h t) -> p r h t", r=STEP_BUFFERS, h=HG)
        self.Kp = self.place([STEP_BUFFERS, HG, S], BF16, "p (r h t) -> p r h t", r=STEP_BUFFERS, h=HG)
        self.E = self.place([2, HG, 4 * P], F32, "p (n h t) -> p n h t", n=2, h=HG)
        self.wn = self.place([4, KD, D], F32, "p (n k d) -> p n k d", n=4, k=KD)

    def place(self, shape, dt, pattern=None, **sizes):
        cols = int(np.prod(shape)) * (2 if dt == F32 else 1)
        part = self.flat[:, self.at:self.at + cols]
        self.at += cols
        if dt != F16:
            part = part.bitcast(dt)
        return part.rearrange(pattern, **sizes) if pattern else part


def layer_norm_steps(nc, dve, m, link, x, y, n, scale):
    def stats():
        for i in range(n):
            ins = nc.vector.bn_stats(m.bn[:, i, :], x[:, i, :])
        link(ins)

    def aggregate():
        for i in range(n):
            ins = nc.vector.bn_aggr(m.mv[:, i, :], m.bn[:, i, :])
        link(ins)
        v, r = m.var[:, 0:n], m.rstd[:, 0:n]
        link(nc.vector.tensor_scalar(v, m.mv[:, 0:n, 1], EPS, 1.0 / (scale * scale), ALU.add, ALU.mult))
        return guess_root(nc, link, v, r)

    def apply():
        for i in range(n):
            ins = nc.vector.tensor_scalar(y[:, i, :], x[:, i, :], m.mv[:, i, 0:1], m.rstd[:, i:i + 1],
                                          ALU.subtract, ALU.mult)
        return ins
    return stats, aggregate, apply


def guess_root(nc, link, v, r):
    link(nc.vector.tensor_scalar(r.bitcast(I32), v.bitcast(I32), 1, None, ALU.arith_shift_right))
    return nc.vector.tensor_scalar(r.bitcast(I32), r.bitcast(I32), -1.0, float(0x5f3759df), ALU.mult, ALU.add)


def refine_root(nc, link, v, r, t):
    for step in range(3):
        link(nc.gpsimd.tensor_tensor(t, r, r, ALU.mult))
        link(nc.gpsimd.tensor_tensor(t, t, v, ALU.mult))
        link(nc.gpsimd.tensor_scalar(t, t, -0.5, 1.5, ALU.mult, ALU.add))
        ins = nc.gpsimd.tensor_tensor(r, r, t, ALU.mult)
        if step < 2:
            link(ins)
    return ins


def linker(eng, signal):
    signal.links = 0

    def link(ins):
        signal.links += 1
        ins.then_inc(signal.sem, 1)
        eng.wait_ge(signal.sem, signal.at(signal.links))
    return link


def quantize_phase(nc, m, a, sig):
    with ExitStack() as ctx:
        sb = buffers(nc, ctx)

        w1n = sb("w1_natural", [P, NF, D], F32)
        w2n = sb("w2_natural", [P, KD, F0], F32)
        below = sb("below", [P, NF * D], F16)
        q1 = sb("w1_quantized", [P, NF, D], F16)
        q2 = sb("w2_quantized", [P, KD, F0], F16)
        absw = sb("abs_w", [P, NF * D], F32)
        rows = sb("row_sums", [P, 2], F32)
        thr = sb("threshold", [P, 4], F32)
        loaded, xs, later, cleared = sig("q_loaded"), sig("x_loaded"), sig("aw_loaded"), sig("q_cleared")
        summed, total, chain = sig("q_summed"), sig("q_total"), sig("q_chain")
        quant, tdone, tcopied = sig("q_quantized"), sig("q_transposed"), sig("q_copied")
        var, rstd, pchain = sig("ffn_var_ready"), sig("ffn_rstd_ready"), sig("pr_pool_chain")
        ps = m.ps
        block = ctx.enter_context(nc.Block())

        @block.sync
        def _(sp):
            h = a["L0_attn_h"].rearrange("b s d -> (b s) d").rearrange("(i p) d -> p i d", p=P)
            sp.dma_start(m.x[:, 0:GT, :], h[:, 0:GT, :]).then_inc(xs.sem, 16)
            sp.dma_start(m.ident[:], a["c_ident"]).then_inc(loaded.sem, 16)
            sp.dma_start(w1n[:], a["L0_ffn_w1"].rearrange("(c p) d -> p c d", p=P)).then_inc(loaded.sem, 16)
            sp.dma_start(w2n[:], a["L0_ffn_w2"].rearrange("(c p) f -> p c f", p=P)).then_inc(loaded.sem, 16)
            sp.dma_start(m.b1T[:], a["L0_ffn_b1"].rearrange("(c p) -> p c", p=P), allow_slow_non_contiguous=True).then_inc(loaded.sem, 16)
            sp.dma_start(m.b2h[:], a["L0_ffn_b2"].rearrange("(a d) -> a d", a=1).broadcast_to([P, D])).then_inc(loaded.sem, 16)
            sp.wait_ge(xs.sem, 16)
            sp.dma_start(m.x[:, GT:, :], h[:, GT:, :]).then_inc(xs.sem, 16)
            for n, w in enumerate((a["L0_attn_Wq"], a["L0_attn_Wk"], a["L0_attn_Wv"], a["L0_attn_Wo"])):
                sp.dma_start(m.over.wn[:, n], w.rearrange("(c p) d -> p c d", p=P)).then_inc(later.sem, 16)
            for n, v in enumerate((a["L0_attn_bq"], a["L0_attn_bk"])):
                sp.dma_start(m.bqkT[:, n, :], v.rearrange("(c p) -> p c", p=P), allow_slow_non_contiguous=True).then_inc(later.sem, 16)
            for n, v in enumerate((a["L0_attn_bv"], a["L0_attn_bo"])):
                sp.dma_start(m.bvo[:, n, :], v.rearrange("(a d) -> a d", a=1).broadcast_to([P, D])).then_inc(later.sem, 16)
            sp.dma_start(m.mask_loaded[:], a["c_mask"]).then_inc(later.sem, 16)
            sp.wait_ge(xs.sem, 32)

        @block.gpsimd
        def _(pool):
            nc.gpsimd.memset(m.over.Kp[QK:QK + PARTS], 1.0).then_inc(cleared.sem, 1)
            pool.wait_ge(cleared.sem, 1)
            nc.gpsimd.memset(m.over.V[:, :, :, HD:HP], 0.0).then_inc(cleared.sem, 1)
            pool.wait_ge(cleared.sem, 2)
            nc.gpsimd.memset(m.over.V[:, :, :, HD:HD + 1], 1.0).then_inc(cleared.sem, 1)
            pool.wait_ge(var.sem, 1)
            refine_root(nc, linker(pool, pchain), m.var[:, 0:GT], m.rstd[:, 0:GT], m.nt[:, 0:GT]).then_inc(rstd.sem, 1)

        @block.scalar
        def _(act):
            act.wait_ge(loaded.sem, loaded.at(80))
            nc.scalar.activation(absw[:], w1n[:].rearrange("p c d -> p (c d)"), ACT.Abs,
                                 accum_out=rows[:, 0:1]).then_inc(summed.sem, 1)
            act.wait_ge(summed.sem, summed.at(1))
            nc.scalar.activation(absw[:], w2n[:].rearrange("p c d -> p (c d)"), ACT.Abs,
                                 accum_out=rows[:, 1:2]).then_inc(summed.sem, 1)

        @block.tensor
        def _(pe):
            pe.wait_ge(summed.sem, summed.at(2))
            pe.wait_ge(chain.sem, chain.at(1))
            pe.matmul(ps[:, 0, 0:2], m.ones[:], rows[:], start=True, stop=True).then_inc(total.sem, 1)
            for n in range(4):
                pe.wait_ge(quant.sem, quant.at(n // 2 + 1))
                if n >= 2:
                    pe.wait_ge(tcopied.sem, tcopied.at(n - 1))
                bank = ps[:, 1 + n % 2, :].bitcast(F16)
                for j in range(8):
                    if n < 2:
                        src = q1[:, j, n * P:(n + 1) * P]
                    else:
                        src = q2[:, n - 2, j * P:(j + 1) * P]
                    last = pe.transpose(bank[:, j * P:(j + 1) * P], src, m.ident16[:])
                last.then_inc(tdone.sem, 1)

        @block.vector
        def _(dve):
            link = linker(dve, chain)

            link(nc.vector.memset(m.ones[:], 1.0))
            dve.wait_ge(xs.sem, 16)
            stats, aggregate, _ = layer_norm_steps(nc, dve, m, link, m.x[:, 0:GT, :], None, GT, YS)
            stats()
            aggregate().then_inc(var.sem, 1)
            dve.wait_ge(loaded.sem, loaded.at(80))
            link(nc.vector.tensor_copy(m.ident16[:], m.ident[:]))
            link(nc.vector.tensor_scalar(m.b2h[:], m.b2h[:], 0.5, None, ALU.mult))
            dve.wait_ge(total.sem, total.at(1))
            link(nc.vector.tensor_scalar(thr[:, 0:2], ps[:, 0, 0:2], 1.0 / (F0 * D), 0.7, ALU.mult, ALU.mult))
            link(nc.vector.tensor_scalar(thr[:, 2:4], thr[:, 0:2], -1.0, None, ALU.mult))
            for n, (w, q) in enumerate(((w1n, q1), (w2n, q2))):
                w_, q_ = w[:].rearrange("p c d -> p (c d)"), q[:].rearrange("p c d -> p (c d)")
                link(nc.vector.tensor_scalar(below[:], w_, thr[:, 2 + n:3 + n], None, ALU.is_le))
                ins = nc.vector.scalar_tensor_tensor(out=q_, in0=w_, scalar=thr[:, n:n + 1], in1=below[:],
                                                     op0=ALU.is_ge, op1=ALU.subtract)
                if n == 1:
                    link(ins)
                    ins = nc.vector.tensor_scalar(q_, q_, 0.5, None, ALU.mult)
                ins.then_inc(quant.sem, 1)
                dve.wait_ge(quant.sem, quant.at(n + 1))
            for n in range(4):
                dve.wait_ge(tdone.sem, tdone.at(n + 1))
                bank = ps[:, 1 + n % 2, :].bitcast(F16)
                if n < 2:
                    ins = nc.vector.tensor_copy(m.w1qT[:, n, :], bank)
                else:
                    ins = nc.vector.tensor_copy(m.w2qT[:, :, (n - 2) * P:(n - 1) * P],
                                                bank.rearrange("p (f q) -> p f q", f=NF))
                ins.then_inc(tcopied.sem, 1)
        xs.phase_over(32)
        pchain.phase_over(pchain.links)
        chain.phase_over(chain.links)


def ffn_phase(nc, m, a, sig, experts=False, begun=False):
    with ExitStack() as ctx:
        sb = buffers(nc, ctx)

        GW = GT * P
        y = sb("ffn_y", [P, GT, D], F32)
        yp = sb("ffn_y_parts", [P, 2, GT, D], F16)
        yT = sb("ffn_yT", [P, 2, 2, KD, GW], F16)
        g32 = sb("ffn_g", [P, 2, GW], F32)
        gp = sb("ffn_g_parts", [P, 4, 2, GW], F16)
        split, tdone, tcopied = sig("ffn_y_split"), sig("ffn_transposed"), sig("ffn_yT_ready")
        var, rstd = sig("ffn_var_ready"), sig("ffn_rstd_ready")
        normed, biased = sig("ffn_normed"), sig("ffn_bias_added")
        up, gelu, hi, lo = sig("ffn_up_done"), sig("ffn_gelu_done"), sig("ffn_hi_ready"), sig("ffn_lo_ready")
        down, added, chain = sig("ffn_down_done"), sig("ffn_added"), sig("ffn_chain")
        pchain = sig("ffn_pool_chain")
        ps = m.ps
        TB = 6
        steps = NG * NF
        WC = 1024
        RAW = 4
        if experts:
            raw = sb("ew_raw", [P, RAW, WC], F32)
            bn = sb("ew_bias_natural", [NE * KH, 2, P], F32)
            arrived = [sig(f"ew_arrived{n}") for n in range(RAW)]
            consts, whi, wlo = sig("ew_constants"), sig("ew_hi"), sig("ew_lo")
            bturned = sig("ew_bias_transposed")
            chunks = [(w, e, k, v) for e in range(NE) for w, v, ks in ((a["L1_ffn_W1"], 0, (0,)), (a["L1_ffn_W2"], 1, (0, 2)),
                                                                       (a["L1_ffn_W3"], 2, (0,))) for k in ks]
            assert len(chunks) == steps

            def weights(n):
                w, e, k, v = chunks[n]
                cols = w.shape[2]
                ks = WC // cols
                view = expert_views(m.we[:, e, :])[v]
                return (raw[:, n % RAW, :].rearrange("p (k n) -> p k n", n=cols), view[:, 0, k:k + ks], view[:, 1, k:k + ks],
                        w[e].rearrange("(k p) n -> p k n", p=P)[:, k:k + ks])
        block = ctx.enter_context(nc.Block())

        @block.gpsimd
        def _(pool):
            link = linker(pool, pchain)

            def root(g):
                pool.wait_ge(var.sem, var.at(g + 1))
                refine_root(nc, link, m.var[:, 0:GT], m.rstd[:, 0:GT], m.nt[:, 0:GT]).then_inc(rstd.sem, 1)

            def bias(g):
                pool.wait_ge(normed.sem, normed.at(g + 1))
                xg = m.x[:, g * GT:(g + 1) * GT, :]
                nc.gpsimd.tensor_tensor(xg, xg, m.b2h[:, None, :].broadcast_to([P, GT, D]), ALU.add).then_inc(biased.sem, 1)
            if not begun:
                root(0)
            bias(0)
            for n in range(steps):
                g, f = divmod(n, NF)
                if g + 1 < NG and f == 2:
                    root(g + 1)
                if g + 1 < NG and f == 4:
                    bias(g + 1)
                if experts:
                    pool.wait_ge(hi.sem, hi.at(n + 1))
                    nc.gpsimd.tensor_tensor(gp[:, n % 4, 1, :], g32[:, n % 2, :], gp[:, n % 4, 0, :],
                                            ALU.subtract).then_inc(lo.sem, 1)

        @block.sync
        def _(sp):
            if experts:
                for n in range(steps):
                    if n >= RAW:
                        sp.wait_ge(wlo.sem, n - RAW + 1)
                    sp.dma_start(weights(n)[0], weights(n)[3]).then_inc(arrived[n % RAW].sem, 16)
                    if n == RAW:
                        for i, b in enumerate((a["L1_ffn_b1"], a["L1_ffn_b2"])):
                            sp.dma_start(bn[:, i, :], b.rearrange("e (m p) -> (e m) p", p=P)).then_inc(consts.sem, 16)
                        sp.dma_start(m.wg[:], a["L1_ffn_Wg"].rearrange("(k p) n -> p k n", p=P)).then_inc(consts.sem, 16)
                        sp.dma_start(m.bg[:], a["L1_ffn_bg"].rearrange("(a n) -> a n", a=1).broadcast_to([P, NE])).then_inc(consts.sem, 16)
                        sp.dma_start(m.tri[:], a["c_before"]).then_inc(consts.sem, 16)
                        sp.dma_start(m.eiota[:], a["c_experts"]).then_inc(consts.sem, 16)
                        sp.dma_start(m.starts[:], a["c_tile_starts"]).then_inc(consts.sem, 16)
                sp.wait_ge(consts.sem, 16 * 7)
        @block.tensor
        def _(pe):
            def transposes(g):
                for part in range(2):
                    pe.wait_ge(split.sem, split.at(2 * g + part + 1))
                    if 2 * g + part > 0:
                        pe.wait_ge(tcopied.sem, tcopied.at(2 * g + part))
                    bank = ps[:, TB, :].bitcast(F16)
                    for k in range(KD):
                        for i in range(GT):
                            j = k * GT + i
                            last = pe.transpose(bank[:, j * P:(j + 1) * P], yp[:, part, i, k * P:(k + 1) * P], m.ident16[:])
                    last.then_inc(tdone.sem, 1)

            def up_chunk(n):
                g, f = divmod(n, NF)
                if f == 0:
                    pe.wait_ge(tcopied.sem, tcopied.at(2 * g + 2))
                if n >= 2:
                    pe.wait_ge(gelu.sem, gelu.at(n - 1))
                for k in range(KD):
                    for part in range(2):
                        last = pe.matmul(ps[:, n % 2, :], m.w1qT[:, k, f * P:(f + 1) * P], yT[:, g % 2, part, k, :],
                                         start=(k + part == 0), stop=(k == KD - 1 and part == 1))
                last.then_inc(up.sem, 1)

            def down_chunk(n):
                g, f = divmod(n, NF)
                pe.wait_ge(lo.sem, lo.at(n + 1))
                if f == 0 and g >= 2:
                    pe.wait_ge(added.sem, added.at(g - 1))
                for i in range(GT):
                    acc = ps[:, 2 + 2 * (g % 2) + i // 2, (i % 2) * D:(i % 2 + 1) * D]
                    for part in range(2):
                        last = pe.matmul(acc, gp[:, n % 4, part, i * P:(i + 1) * P], m.w2qT[:, f, :],
                                         start=(f == 0 and part == 0 and i % 2 == 0),
                                         stop=(f == NF - 1 and part == 1), skip_group_check=True)
                last.then_inc(down.sem, 1)

            transposes(0)
            for n in range(steps + 2):
                if n < steps:
                    up_chunk(n)
                    if n % NF == 6 and n // NF + 1 < NG:
                        transposes(n // NF + 1)
                if n >= 2:
                    down_chunk(n - 2)
            if experts:
                pe.wait_ge(consts.sem, 16 * 7)
                for n in range(2):
                    last = pe.transpose(ps[:, 7, n * NE * KH:(n + 1) * NE * KH], bn[:, n, :], m.ident[0:NE * KH, 0:NE * KH])
                last.then_inc(bturned.sem, 1)

        @block.scalar
        def _(act):
            for n in range(steps):
                f = n % NF
                act.wait_ge(up.sem, up.at(n + 1))
                if n >= 2:
                    act.wait_ge(lo.sem, lo.at(n - 1))
                nc.scalar.activation(g32[:, n % 2, :], ps[:, n % 2, :], ACT.Gelu, bias=m.b1T[:, f:f + 1],
                                     scale=1.0 / YS).then_inc(gelu.sem, 1)
                act.wait_ge(gelu.sem, gelu.at(n + 1))
                if n >= 4:
                    act.wait_ge(down.sem, down.at(n - 3))
                nc.scalar.copy(gp[:, n % 4, 0, :], g32[:, n % 2, :]).then_inc(hi.sem, 1)
                if experts:
                    src, high, _, _ = weights(n)
                    act.wait_ge(arrived[n % RAW].sem, 16 * (n // RAW + 1))
                    nc.scalar.mul(high, src, WS).then_inc(whi.sem, 1)

        @block.vector
        def _(dve):
            link = linker(dve, chain)

            def norm(g):
                stats, aggregate, apply = layer_norm_steps(nc, dve, m, link, m.x[:, g * GT:(g + 1) * GT, :], y, GT, YS)

                def first():
                    if g >= 1:
                        dve.wait_ge(normed.sem, normed.at(g))
                    stats()

                def variances():
                    aggregate().then_inc(var.sem, 1)

                def scaled():
                    if g >= 1:
                        dve.wait_ge(split.sem, split.at(2 * g))
                    dve.wait_ge(rstd.sem, rstd.at(g + 1))
                    ins = apply()
                    ins.then_inc(normed.sem, 1)
                    dve.wait_ge(normed.sem, normed.at(g + 1))

                def high():
                    if g >= 1:
                        dve.wait_ge(tdone.sem, tdone.at(2 * g))
                    nc.vector.tensor_copy(yp[:, 0], y[:]).then_inc(split.sem, 1)
                    dve.wait_ge(split.sem, split.at(2 * g + 1))

                def low():
                    nc.vector.tensor_tensor(yp[:, 1], y[:], yp[:, 0], ALU.subtract).then_inc(split.sem, 1)
                return first, variances, scaled, high, low

            def copy_yT(g):
                for part in range(2):
                    dve.wait_ge(tdone.sem, tdone.at(2 * g + part + 1))
                    if g >= 2:
                        dve.wait_ge(up.sem, up.at(NF * (g - 1)))
                    nc.vector.tensor_copy(yT[:, g % 2, part].rearrange("p k t -> p (k t)"),
                                          ps[:, TB, :].bitcast(F16)).then_inc(tcopied.sem, 1)

            def add_out(g):
                dve.wait_ge(down.sem, down.at(NF * (g + 1)))
                dve.wait_ge(biased.sem, biased.at(g + 1))
                for j in range(2):
                    xg = m.x[:, g * GT + 2 * j:g * GT + 2 * j + 2, :]
                    acc = ps[:, 2 + 2 * (g % 2) + j, :].rearrange("p (i d) -> p i d", i=2)
                    ins = nc.vector.tensor_tensor(xg, acc, xg, ALU.add)
                ins.then_inc(added.sem, 1)

            def weights_low(n):
                src, high, low, _ = weights(n)
                dve.wait_ge(whi.sem, n + 1)
                dve.wait_ge(arrived[n % RAW].sem, 16 * (n // RAW + 1))
                nc.vector.scalar_tensor_tensor(out=low, in0=src, scalar=WS, in1=high, op0=ALU.mult,
                                               op1=ALU.subtract).then_inc(wlo.sem, 1)

            AHEAD = (0, 1, 3, 4, 5)

            for step in norm(0)[2 if begun else 0:]:
                step()
            copy_yT(0)
            for n in range(steps):
                g, f = divmod(n, NF)
                if g + 1 < NG:
                    if f == 0:
                        ahead = norm(g + 1)
                    if f in AHEAD:
                        ahead[AHEAD.index(f)]()
                    if f == 6:
                        copy_yT(g + 1)
                if f == 2 and g >= 1:
                    add_out(g - 1)
                if not experts:
                    dve.wait_ge(hi.sem, hi.at(n + 1))
                    nc.vector.tensor_tensor(gp[:, n % 4, 1, :], g32[:, n % 2, :], gp[:, n % 4, 0, :],
                                            ALU.subtract).then_inc(lo.sem, 1)
                if experts and n >= 1:
                    weights_low(n - 1)
            if experts:
                weights_low(steps - 1)
            add_out(NG - 1)
            if experts:
                dve.wait_ge(bturned.sem, 1)
                nc.vector.tensor_copy(m.eb12[:], ps[:, 7, 0:2 * NE * KH].rearrange("p (n e c) -> p e n c", n=2, e=NE))
        for s, n in ((split, 2 * NG), (tdone, 2 * NG), (tcopied, 2 * NG), (normed, NG), (var, NG), (rstd, NG), (biased, NG), (up, steps),
                     (gelu, steps), (hi, steps), (lo, steps), (down, steps), (added, NG), (chain, chain.links), (pchain, pchain.links)):
            s.phase_over(n)


def transpose_weights_phase(nc, m, a, sig):
    with ExitStack() as ctx:
        wn, cm, loaded = m.over.wn, m.mask_loaded, sig("aw_loaded")
        tdone, copied = sig("aw_transposed"), sig("aw_copied")
        block = ctx.enter_context(nc.Block())

        @block.tensor
        def _(pe):
            pe.wait_ge(loaded.sem, loaded.at(16 * 9))
            for n in range(4):
                if n >= 2:
                    pe.wait_ge(copied.sem, copied.at(n - 1))
                for ko in range(KD):
                    for ki in range(KD):
                        last = pe.transpose(m.ps[:, n % 2, (ki * KD + ko) * P:(ki * KD + ko + 1) * P],
                                            wn[:, n, ko, ki * P:(ki + 1) * P], m.ident[:])
                last.then_inc(tdone.sem, 1)

        @block.vector
        def _(dve):
            for n in range(4):
                dve.wait_ge(tdone.sem, tdone.at(n + 1))
                nc.vector.tensor_copy(m.awT[:, n].rearrange("p k d -> p (k d)"), m.ps[:, n % 2, :]).then_inc(copied.sem, 1)
            dve.wait_ge(loaded.sem, loaded.at(16 * 9))
            nc.vector.tensor_copy(m.mask16[:], cm[:])
            nc.vector.tensor_copy(m.identb[:], m.ident[:])


def attend_phase(nc, m, a, sig):
    with ExitStack() as ctx:
        sb = buffers(nc, ctx)
        V, O, Qp, Kp, E = m.over.V, m.over.O, m.over.Qp, m.over.Kp, m.over.E
        TW = GT * P
        PR = 4
        y = sb("pr_y", [P, GT, D], F32)
        yT = sb("pr_yT", [P, 2, KD, TW], F32)
        full = sb("pr_full", [P, 2, TW], F32)
        rest = sb("pr_rest", [P, 2, TW], F32)
        parts = sb("pr_parts", [P, PR, PARTS, TW], BF16)
        var, rstd, normed = sig("pr_var"), sig("pr_rstd"), sig("pr_normed")
        tdone, yready = sig("pr_transposed"), sig("pr_yT_ready")
        proj, evac, high = sig("pr_projected"), sig("pr_full_ready"), sig("pr_high_ready")
        restr, mid, low = sig("pr_rest_ready"), sig("pr_mid_ready"), sig("pr_low_ready")
        sent = [sig(f"pr_parts_sent{n}") for n in range(PR)]
        vdone, vready, pchain = sig("pr_v_done"), sig("pr_v_ready"), sig("pr_pool_chain")
        biased = sig("pr_biased")
        PU = NG * 4
        QG = BT // 4
        GW = 4 * P
        R = STEP_BUFFERS
        STEPS = B * NH // HG
        LOADS = 2 * len(Q_PARTS)
        mx = sb("at_max_pieces", [P, 2, HG * BT, 2], F32)
        mc = sb("at_max", [P, HG * BT], F32)
        nm = sb("at_neg_max", [HG * BT, 2, P], F32)
        mp = sb("at_max_parts", [HG * BT, PARTS, P], BF16)
        oT = sb("at_oT", [P, GW], F32)
        rec = sb("at_rec", [P, 4, HG], F32)
        spread = [sig(f"at_qk_loaded{n}") for n in range(R)]
        qk, mxd, mcd, mtd, mpr = sig("at_qk_done"), sig("at_max_done"), sig("at_max_ready"), sig("at_maxT_done"), sig("at_max_parts")
        mset = sig("at_max_rows")
        st, ex, pv = sig("at_st_done"), sig("at_exp_done"), sig("at_pv_done")
        oev, otd, ord_, chain = sig("at_oT_ready"), sig("at_o_transposed"), sig("at_o_ready"), sig("at_chain")
        ps = m.ps
        SB, NSB = 3, 3
        units = [(G, kb) for G in range(QG) for kb in range(4 * G + 4)]
        NU = len(units)
        UL = [u for u, (G, kb) in enumerate(units) if kb == 4 * G + 3]
        pieces = [(hh, i, bk) for i in range(BT) for bk in range((i + 4) // 4) for hh in range(HG)]
        NP = len(pieces)

        def width(piece):
            _, i, bk = piece
            return min(GW, (i + 1) * P - bk * GW)
        total = sum(width(p) + 60 for p in pieces)
        spans = [GW - max(0, kb - 4 * G) * P + 60 for G, kb in units for _ in range(HG)]
        share, piece, passed, at = [[] for _ in spans], 0, 0, 0
        for n, w in enumerate(spans):
            at += w
            while piece < NP and passed < 1.25 * total * at / sum(spans):
                share[n].append(piece)
                passed += width(pieces[piece]) + 60
                piece += 1
        END = next(n for n, some in enumerate(share) if NP - 1 in some)
        ROWS, SPLIT = END + 2, END + 3
        assert SPLIT < NU * HG and (UL[-2] + 2) * HG <= ROWS

        LATE = 3
        SLOTS0 = NG // 2 * 8
        each = -(-NP // (SLOTS0 - LATE))
        PASS0 = [[p for p in range((n - LATE) * each, (n - LATE + 1) * each) if 0 <= p < NP] for n in range(SLOTS0)]

        def early(g, n):
            return PASS0[(g - NG // 2) * 8 + n] if g >= NG // 2 else []

        def max_bank(c):
            return 6 + c % 2 if c < NP else c % 3
        block = ctx.enter_context(nc.Block())

        @block.gpsimd
        def _(pool):
            link = linker(pool, pchain)

            def root(g):
                pool.wait_ge(var.sem, g + 1)
                refine_root(nc, link, m.var[:, 0:GT], m.rstd[:, 0:GT], m.nt[:, 0:GT]).then_inc(rstd.sem, 1)
            root(0)
            for g in range(NG):
                if g + 1 < NG:
                    root(g + 1)
                for n in range(4 * g, 4 * g + 4):
                    pool.wait_ge(mid.sem, n + 1)
                    nc.gpsimd.tensor_tensor(parts[:, n % PR, 2, :], rest[:, n % 2, :], parts[:, n % PR, 1, :],
                                            ALU.subtract).then_inc(low.sem, 1)
                pool.wait_ge(normed.sem, g + 1)
                xg = m.x[:, g * GT:(g + 1) * GT, :]
                nc.gpsimd.tensor_tensor(xg, xg, m.bvo[:, 1:2, :].broadcast_to([P, GT, D]), ALU.add).then_inc(biased.sem, 1)

        @block.tensor
        def _(pe):
            def max_piece(s, n):
                hh, i, bk = pieces[n]
                c = s * NP + n
                if n == 0:
                    pe.wait_ge(spread[s % R].sem, 16 * LOADS * (s // R + 1))
                if c >= 2:
                    pe.wait_ge(mxd.sem, c - 1 if c < NP + 3 else c - 2)
                w = width(pieces[n])
                diag = bk == i // 4
                last = pe.matmul(ps[:, max_bank(c), 0:w], Qp[0:QK, s % R, hh, i * P:(i + 1) * P],
                                 Kp[0:QK, s % R, hh, bk * GW:bk * GW + w], start=True, stop=not diag)
                if diag:
                    last = pe.matmul(ps[:, max_bank(c), w - P:w], m.identb[:], m.mask16[:, 0, :], start=False, stop=True)
                last.then_inc(qk.sem, 1)

            def scores(s, u, hh):
                G, kb = units[u]
                j = max(0, kb - 4 * G)
                n = (s * NU + u) * HG + hh
                if n >= NSB:
                    pe.wait_ge(ex.sem, n - NSB + 1)
                bank = ps[:, SB + n % NSB, :]
                last = pe.matmul(bank[:, j * P:GW], Kp[0:QK + PARTS, s % R, hh, kb * P:(kb + 1) * P],
                                 Qp[0:QK + PARTS, s % R, hh, G * GW + j * P:(G + 1) * GW], start=True, stop=kb < 4 * G)
                if kb >= 4 * G:
                    last = pe.matmul(bank[:, j * P:(j + 1) * P], m.identb[:], m.mask16[:, 1, :], start=False, stop=True)
                last.then_inc(st.sem, 1)

            def weigh(s, u):
                G, kb = units[u]
                j = max(0, kb - 4 * G)
                pe.wait_ge(ex.sem, (s * NU + u + 1) * HG)
                if kb == 0 and s * QG + G >= 1:
                    pe.wait_ge(oev.sem, s * QG + G)
                b, gr = divmod(s, NH // HG)
                for hh in range(HG):
                    last = pe.matmul(ps[hh * HP:(hh + 1) * HP, 6, j * P:GW], V[:, b * BT + kb, gr * HG + hh, :],
                                     E[:, (s * NU + u) % 2, hh, j * P:GW], start=(kb == 0), stop=(kb == 4 * G + 3),
                                     skip_group_check=True)
                last.then_inc(pv.sem, 1)

            def turn(s, G):
                n = s * QG + G
                pe.wait_ge(oev.sem, n + 1)
                if n >= 1:
                    pe.wait_ge(ord_.sem, n)
                if G == 0 or (G == QG - 1 and s + 1 < STEPS):
                    pe.wait_ge(mpr.sem, s + 1 + (G > 0))
                for i in range(4):
                    last = pe.transpose(ps[:, 7, i * P:(i + 1) * P], oT[:, i * P:(i + 1) * P], m.ident[:])
                last.then_inc(otd.sem, 1)

            def max_rows(s):
                pe.wait_ge(mcd.sem, s + 1)
                if s >= 1:
                    pe.wait_ge(ord_.sem, QG * s - 1)
                pe.transpose(ps[0:HG * BT, 7, 0:P], mc[:], m.ident[:]).then_inc(mtd.sem, 1)

            def turn_y(g):
                pe.wait_ge(normed.sem, g + 1)
                if g >= 1:
                    pe.wait_ge(yready.sem, g)
                for k in range(KD):
                    for i in range(GT):
                        last = pe.transpose(ps[:, k, i * P:(i + 1) * P], y[:, i, k * P:(k + 1) * P], m.ident[:])
                last.then_inc(tdone.sem, 1)
            turn_y(0)
            for g in range(NG):
                pe.wait_ge(yready.sem, g + 1)
                for n in range(4 * g, 4 * g + 4):
                    w, c = n // 2 % 2, n % 2
                    if n >= 2:
                        pe.wait_ge(evac.sem, n - 1)
                    for k in range(KD):
                        last = pe.matmul(ps[:, 2 + n % 2, :], m.awT[:, w, k, c * P:(c + 1) * P], yT[:, g % 2, k, :],
                                         start=(k == 0), stop=(k == KD - 1))
                    last.then_inc(proj.sem, 1)
                    for piece in early(g, n % 4):
                        max_piece(0, piece)
                if g + 1 < NG:
                    turn_y(g + 1)
                for i in range(GT):
                    t = g * GT + i
                    if t >= 2:
                        pe.wait_ge(vready.sem, t - 1)
                    for k in range(KD):
                        last = pe.matmul(ps[:, 4 + t % 2, 0:D], yT[:, g % 2, k, i * P:(i + 1) * P], m.awT[:, 2, k, :],
                                         start=(k == 0), stop=(k == KD - 1))
                    last.then_inc(vdone.sem, 1)
                    for piece in early(g, 4 + i):
                        max_piece(0, piece)
            max_rows(0)
            pe.wait_ge(yready.sem, NG)
            pe.wait_ge(evac.sem, PU)
            pe.wait_ge(vready.sem, NT)
            for s in range(STEPS):
                pe.wait_ge(mset.sem, 16 * PARTS * (s + 1))
                for u in range(NU):
                    for hh in range(HG):
                        scores(s, u, hh)
                        if s + 1 < STEPS:
                            for n in share[u * HG + hh]:
                                max_piece(s + 1, n)
                        if hh == 1:
                            if u >= 1:
                                weigh(s, u - 1)
                            elif s >= 1:
                                weigh(s - 1, NU - 1)
                        if hh == 3:
                            if u >= 1 and u - 1 in UL[:-1]:
                                turn(s, UL.index(u - 1))
                            if u == 0 and s >= 1:
                                turn(s - 1, QG - 1)
                        if u * HG + hh == ROWS and s + 1 < STEPS:
                            max_rows(s + 1)
            weigh(STEPS - 1, NU - 1)
            turn(STEPS - 1, QG - 1)

        @block.scalar
        def _(act):
            for n in range(PU):
                w, c = n // 2 % 2, n % 2
                act.wait_ge(proj.sem, n + 1)
                if n >= 2:
                    act.wait_ge(restr.sem, n - 1)
                nc.scalar.activation(full[:, n % 2, :], ps[:, 2 + n % 2, :], ACT.Identity,
                                     bias=m.bqkT[:, w, c:c + 1]).then_inc(evac.sem, 1)
                act.wait_ge(evac.sem, n + 1)
                if n >= PR:
                    act.wait_ge(sent[n % PR].sem, 16 * (n // PR))
                nc.scalar.copy(parts[:, n % PR, 0, :], full[:, n % 2, :]).then_inc(high.sem, 1)
            def collect(s, G):
                n = s * QG + G
                act.wait_ge(pv.sem, s * NU + UL[G] + 1)
                if n >= 1:
                    act.wait_ge(otd.sem, n)
                nc.scalar.copy(oT[:], ps[:, 6, :]).then_inc(oev.sem, 1)

            for s in range(STEPS):
                for u, (G, kb) in enumerate(units):
                    j = max(0, kb - 4 * G)
                    if s * NU + u >= 2:
                        act.wait_ge(pv.sem, s * NU + u - 1)
                    for hh in range(HG):
                        n = (s * NU + u) * HG + hh
                        act.wait_ge(st.sem, n + 1)
                        nc.scalar.activation(E[:, (s * NU + u) % 2, hh, j * P:GW], ps[:, SB + n % NSB, j * P:GW],
                                             ACT.Exp, scale=HD ** -0.5).then_inc(ex.sem, 1)
                        if hh == 2:
                            if u >= 1 and u - 1 in UL:
                                collect(s, UL.index(u - 1))
                            if u == 0 and s >= 1:
                                collect(s - 1, QG - 1)
            collect(STEPS - 1, QG - 1)

        @block.vector
        def _(dve):
            link = linker(dve, chain)
            link(nc.vector.memset(mx[:], -3e38))

            def max_piece(s, n):
                hh, i, bk = pieces[n]
                c = s * NP + n
                dve.wait_ge(qk.sem, c + 1)
                nc.vector.tensor_reduce(mx[:, s % 2, hh * BT + i, bk:bk + 1], ps[:, max_bank(c), 0:width(pieces[n])], AX.X,
                                        ALU.max).then_inc(mxd.sem, 1)

            def max_ready(s):
                dve.wait_ge(mxd.sem, NP * (s + 1))
                if s >= 1:
                    dve.wait_ge(mtd.sem, s)
                nc.vector.tensor_reduce(mc[:], mx[:, s % 2], AX.X, ALU.max).then_inc(mcd.sem, 1)

            def max_parts(s):
                dve.wait_ge(mtd.sem, s + 1)
                if s >= 1:
                    dve.wait_ge(mset.sem, 16 * PARTS * s)
                link(nc.vector.tensor_scalar(nm[:, 0, :], ps[0:HG * BT, 7, 0:P], -1.0, None, ALU.mult))
                link(nc.vector.tensor_copy(mp[:, 0, :], nm[:, 0, :]))
                link(nc.vector.tensor_tensor(nm[:, 1, :], nm[:, 0, :], mp[:, 0, :], ALU.subtract))
                link(nc.vector.tensor_copy(mp[:, 1, :], nm[:, 1, :]))
                nc.vector.tensor_tensor(mp[:, 2, :], nm[:, 1, :], mp[:, 1, :], ALU.subtract).then_inc(mpr.sem, 1)

            def outputs(s, G):
                b, gr = divmod(s, NH // HG)
                dve.wait_ge(otd.sem, s * QG + G + 1)
                o = ps[:, 7, :].rearrange("p (i h d) -> p i h d", i=4, h=HG)
                link(nc.vector.reciprocal(rec[:], o[:, :, :, HD]))
                for i in range(4):
                    out = O[:, b * BT + 4 * G + i, gr * HG * HD:(gr + 1) * HG * HD].rearrange("p (h d) -> p h d", h=HG)
                    ins = nc.vector.tensor_tensor(out, o[:, i, :, 0:HD], rec[:, i, :, None].broadcast_to([P, HG, HD]), ALU.mult)
                ins.then_inc(ord_.sem, 1)

            def norm_start(g):
                x = m.x[:, g * GT:(g + 1) * GT, :]
                stats, aggregate, _ = layer_norm_steps(nc, dve, m, link, x, y, GT, 1.0)
                if g >= 1:
                    dve.wait_ge(tdone.sem, g)
                stats()
                aggregate().then_inc(var.sem, 1)

            def norm_end(g):
                x = m.x[:, g * GT:(g + 1) * GT, :]
                _, _, apply = layer_norm_steps(nc, dve, m, link, x, y, GT, 1.0)
                dve.wait_ge(rstd.sem, g + 1)
                apply().then_inc(normed.sem, 1)

            def copy_yT(g):
                dve.wait_ge(tdone.sem, g + 1)
                if g >= 2:
                    dve.wait_ge(vdone.sem, (g - 1) * GT)
                nc.vector.tensor_copy(yT[:, g % 2], ps[:, 0:2, :]).then_inc(yready.sem, 1)
            norm_start(0)
            norm_end(0)
            copy_yT(0)
            for g in range(NG):
                if g + 1 < NG:
                    norm_start(g + 1)
                for n in range(g * 4, g * 4 + 4):
                    if n == g * 4 + 2 and g + 1 < NG:
                        norm_end(g + 1)
                    for piece in early(g, n % 4):
                        max_piece(0, piece)
                    dve.wait_ge(high.sem, n + 1)
                    if n >= 2:
                        dve.wait_ge(low.sem, n - 1)
                    nc.vector.tensor_tensor(rest[:, n % 2, :], full[:, n % 2, :], parts[:, n % PR, 0, :],
                                            ALU.subtract).then_inc(restr.sem, 1)
                    dve.wait_ge(restr.sem, n + 1)
                    nc.vector.tensor_copy(parts[:, n % PR, 1, :], rest[:, n % 2, :]).then_inc(mid.sem, 1)
                if g + 1 < NG:
                    copy_yT(g + 1)
                for i in range(GT):
                    for piece in early(g, 4 + i):
                        max_piece(0, piece)
                    t = g * GT + i
                    dve.wait_ge(vdone.sem, t + 1)
                    nc.vector.tensor_tensor(V[:, t, :, 0:HD], ps[:, 4 + t % 2, 0:D].rearrange("p (h d) -> p h d", h=NH),
                                            m.bvo[:, 0, :].rearrange("p (h d) -> p h d", h=NH), ALU.add).then_inc(vready.sem, 1)
            max_ready(0)
            max_parts(0)
            for s in range(STEPS):
                for u in range(NU):
                    for hh in range(HG):
                        if s + 1 < STEPS:
                            for n in share[u * HG + hh]:
                                max_piece(s + 1, n)
                        if hh == 3:
                            if u >= 1 and u - 1 in UL:
                                outputs(s, UL.index(u - 1))
                            if u == 0 and s >= 1:
                                outputs(s - 1, QG - 1)
                        if u * HG + hh == END and s + 1 < STEPS:
                            max_ready(s + 1)
                        if u * HG + hh == SPLIT and s + 1 < STEPS:
                            max_parts(s + 1)
            outputs(STEPS - 1, QG - 1)

        @block.sync
        def _(sp):
            def load(s):
                b, gr = divmod(s, NH // HG)
                if s >= R:
                    sp.wait_ge(st.sem, NU * HG * (s - R + 1))
                    sp.wait_ge(spread[s % R].sem, 16 * LOADS * (s // R))
                for w, (dst, order) in enumerate(((Qp, Q_PARTS), (Kp, K_PARTS))):
                    for j, part in enumerate(order):
                        src = a["qk_parts"][w, part, gr * HG * HD:(gr + 1) * HG * HD, b * S:(b + 1) * S]
                        sp.dma_start(dst[j * HD:(j + 1) * HD, s % R], src.rearrange("(h d) t -> d h t", d=HD)
                                     ).then_inc(spread[s % R].sem, 16)

            for n in range(PU):
                g, w, c = n // 4, n // 2 % 2, n % 2
                sp.wait_ge(low.sem, n + 1)
                dst = a["qk_parts"][w, :, c * P:(c + 1) * P, g * TW:(g + 1) * TW].rearrange("s c t -> c s t")
                sp.dma_start(dst, parts[:, n % PR]).then_inc(sent[n % PR].sem, 16)
                if n == PU // 2 - 1:
                    for each_sent in sent:
                        sp.wait_ge(each_sent.sem, 16 * PU // 2 // PR)
                    for s in range(R):
                        load(s)
            for s in sent:
                sp.wait_ge(s.sem, 16 * PU // PR)
            for s in range(STEPS):
                sp.wait_ge(mpr.sem, s + 1)
                for p in range(PARTS):
                    dst = Qp[QK + p:QK + p + 1, s % R].rearrange("p h (i t) -> p (h i) t", t=P)
                    sp.dma_start(dst, mp[:, p, :]).then_inc(mset.sem, 16)
                if s >= 1 and s + 2 < STEPS:
                    load(s + 2)
            sp.wait_ge(mset.sem, 16 * PARTS * STEPS)
        pchain.phase_over(pchain.links)


def out_projection_phase(nc, m, a, sig):
    with ExitStack() as ctx:
        sb = buffers(nc, ctx)
        O = m.over.O
        OT = sb("op_OT", [P, 2, KD, P], F32)
        tdone, tcop, done, added = sig("op_transposed"), sig("op_copied"), sig("op_done"), sig("op_added")
        var, rstd, chain, pchain = sig("ffn_var_ready"), sig("ffn_rstd_ready"), sig("q_chain"), sig("pr_pool_chain")
        ps = m.ps
        block = ctx.enter_context(nc.Block())

        @block.tensor
        def _(pe):
            def turn(i):
                if i >= 2:
                    pe.wait_ge(tcop.sem, tcop.at(i - 1))
                for k in range(KD):
                    last = pe.transpose(ps[:, i % 2, k * P:(k + 1) * P], O[:, i, k * P:(k + 1) * P], m.ident[:])
                last.then_inc(tdone.sem, 1)
            turn(0)
            for i in range(NT):
                if i + 1 < NT:
                    turn(i + 1)
                pe.wait_ge(tcop.sem, tcop.at(i + 1))
                if i >= 2:
                    pe.wait_ge(added.sem, added.at(i - 1))
                for k in range(KD):
                    last = pe.matmul(ps[:, 2 + i % 2, 0:D], OT[:, i % 2, k, :], m.awT[:, 3, k, :], start=(k == 0),
                                     stop=(k == KD - 1))
                last.then_inc(done.sem, 1)

        @block.scalar
        def _(act):
            for i in range(NT):
                act.wait_ge(tdone.sem, tdone.at(i + 1))
                if i >= 2:
                    act.wait_ge(done.sem, done.at(i - 1))
                nc.scalar.copy(OT[:, i % 2].rearrange("p k t -> p (k t)"), ps[:, i % 2, 0:D]).then_inc(tcop.sem, 1)

        @block.vector
        def _(dve):
            link = linker(dve, chain)
            stats, aggregate, _ = layer_norm_steps(nc, dve, m, link, m.x[:, 0:GT, :], None, GT, YS)
            for i in range(NT):
                if i == GT + 1:
                    dve.wait_ge(added.sem, added.at(GT))
                    stats()
                if i == GT + 3:
                    aggregate().then_inc(var.sem, 1)
                dve.wait_ge(done.sem, done.at(i + 1))
                xt = m.x[:, i, :]
                nc.vector.tensor_tensor(xt, ps[:, 2 + i % 2, 0:D], xt, ALU.add).then_inc(added.sem, 1)

        @block.gpsimd
        def _(pool):
            link = linker(pool, pchain)
            pool.wait_ge(var.sem, var.at(1))
            refine_root(nc, link, m.var[:, 0:GT], m.rstd[:, 0:GT], m.nt[:, 0:GT]).then_inc(rstd.sem, 1)
        for s in (tdone, tcop, done, added):
            s.phase_over(NT)


NE, HE = 8, 512
KH = HE // P
TOPK = 2
SLOT_TILES = (T * TOPK + NE * (P - 1)) // P
SLOTS = SLOT_TILES * P
W1_COLS, W2_COLS, W3_COLS = KD * HE, KH * HE, KH * D
EXPERT_COLS = 2 * (W1_COLS + W2_COLS + W3_COLS)
WS = 256.0


def expert_views(flat):
    out, at = [], 0
    for cols, n in ((W1_COLS, HE), (W2_COLS, HE), (W3_COLS, D)):
        out.append(flat[:, at:at + 2 * cols].rearrange("p (s k n) -> p s k n", s=2, n=n))
        at += 2 * cols
    return out


def routing_phase(nc, m, a, sig):
    with ExitStack() as ctx:
        sb = buffers(nc, ctx)
        y = sb("rt_y", [P, NG, GT, D], F32)
        yT = sb("rt_yT", [P, 2, 2, KD, GT, P], F16)
        wgp = sb("rt_gate_parts", [P, 2, KD, NE], F16)
        bn = sb("rt_bn_stats", [P, NT, 6], F32)
        mv = sb("rt_bn_mean_var", [P, NT, 2], F32)
        var_, rstd_, work = (sb(f"rt_{n}", [P, NT], F32) for n in ("variance", "root", "newton"))
        BATCHES = ((0, GT), (GT, NT))
        rows = sb("rt_rows", [P, NT, 2 * D], F16)
        big = [sb(f"rt_big{n}", [P, NT, NE], F32) for n in range(8)]
        small = [sb(f"rt_small{n}", [P, NT], F32) for n in range(6)]
        ends = sb("rt_ends", [P, 6, NE], F32)
        te = sb("rt_tile_expert", [1, 2, SLOT_TILES + 1, NE], F32)
        tr = sb("rt_tile_sum", [1, 2, SLOT_TILES + 1], F32)
        one = sb("rt_one", [P, NT], F32)
        slot = sb("rt_slot", [P, TOPK, NT], F32)
        tile_of = sb("rt_slot_tile", [P, TOPK, NT], F32)
        row_of = sb("rt_slot_row", [P, TOPK, NT], F32)
        shift = sb("rt_slot_bits", [P, TOPK, NT], I32)
        numbers = sb("rt_numbers", [P, P], F32)
        tokens = sb("rt_tokens", [P, NT], F32)
        spare = sb("rt_spare_rows", [P, SLOT_TILES], F32)
        onrow = y[:].rearrange("p g i d -> p (g i d)").bitcast(F16)[:, 0:TOPK * NT * P].rearrange("p (n t r) -> p n t r", n=TOPK, t=NT)
        ontile = sb("rt_on_tile", [P, TOPK, NT, 2, SLOT_TILES], F16)
        used = sb("rt_used", [P, 3, SLOT_TILES], F32)
        var, rstd, normed = sig("rt_var"), sig("rt_rstd"), sig("rt_normed")
        tdone, gated = sig("rt_transposed"), sig("rt_gated")
        yready = [sig("rt_yT_high_ready"), sig("rt_yT_low_ready")]
        shifted, chosen, counted = sig("rt_shifted"), sig("rt_chosen"), sig("rt_counted")
        sent, chain, pchain = sig("rt_rows_sent"), sig("rt_chain"), sig("rt_pool_chain")
        constants, inverted, turned = sig("rt_constants"), sig("rt_inverted"), sig("rt_marked")
        split, low = sig("rt_rows_high_then_exp"), [sig("rt_rows_low_even"), sig("rt_rows_low_odd")]
        ps = m.ps
        logits, prob, h1, h2, eq, cand, both, base = big
        mx, i1, i2, w1, w2, rs = small
        block = ctx.enter_context(nc.Block())

        @block.sync
        def _(sp):
            for dst, src in ((numbers[:], a["c_numbers"]), (tokens[:], a["c_tokens"]), (spare[:], a["c_spare_rows"])):
                sp.dma_start(dst, src).then_inc(constants.sem, 16)
            for g in range(NG):
                sp.wait_ge(split.sem, split.at(g + 1))
                sp.wait_ge(low[g % 2].sem, low[g % 2].at(g // 2 + 1))
                dst = a["moe_rows"][g * GT * P:(g + 1) * GT * P, :].rearrange("(i p) d -> p i d", p=P)
                sp.dma_start(dst, rows[:, g * GT:(g + 1) * GT, :]).then_inc(sent.sem, 16)
            sp.wait_ge(sent.sem, sent.at(16 * NG))

        @block.tensor
        def _(pe):
            def turn(g):
                pe.wait_ge(split.sem, split.at(g + 1))
                pe.wait_ge(low[g % 2].sem, low[g % 2].at(g // 2 + 1))
                if g >= 2:
                    for part in range(2):
                        pe.wait_ge(yready[part].sem, yready[part].at(g - 1))
                for part in range(2):
                    bank = ps[:, 5 * (g % 2) + part, :].bitcast(F16)
                    for n in range(KD * GT):
                        k, i = divmod(n, GT)
                        at = part * D + k * P
                        last = pe.transpose(bank[:, n * P:(n + 1) * P], rows[:, g * GT + i, at:at + P], m.ident16[:])
                last.then_inc(tdone.sem, 1)
            turn(0)
            for g in range(NG):
                if g + 1 < NG:
                    turn(g + 1)
                for part in range(2):
                    pe.wait_ge(yready[part].sem, yready[part].at(g + 1))
                for i in range(GT):
                    t = g * GT + i
                    products = [(k, pw, py) for k in range(KD) for pw, py in ((0, 0), (0, 1), (1, 0))]
                    for j, (k, pw, py) in enumerate(products):
                        last = pe.matmul(ps[:, 2, t * NE:(t + 1) * NE], yT[:, g % 2, py, k, i, :], wgp[:, pw, k, :],
                                         start=(j == 0), stop=(j == len(products) - 1))
                last.then_inc(gated.sem, 1)
            pe.wait_ge(chosen.sem, chosen.at(1))
            flat = both[:].rearrange("p t e -> p (t e)")
            pe.matmul(ps[:, 3, 0:NT * NE], m.tri[:], flat, start=True, stop=True)
            pe.matmul(ps[:, 4, 0:NT * NE], m.ones[:], flat, start=True, stop=True).then_inc(counted.sem, 1)
            for n in range(TOPK):
                pe.wait_ge(turned.sem, turned.at(n + 1))
                for t in range(NT):
                    last = pe.matmul(ps[:, 7, 0:2 * SLOT_TILES], onrow[:, n, t, :], ontile[:, n, t].rearrange("p a s -> p (a s)"),
                                     start=(n == 0 and t == 0), stop=(n == TOPK - 1 and t == NT - 1))
            last.then_inc(inverted.sem, 1)

        @block.scalar
        def _(act):
            def high(g):
                act.wait_ge(normed.sem, normed.at(g + 1))
                nc.scalar.copy(rows[:, g * GT:(g + 1) * GT, 0:D], y[:, g]).then_inc(split.sem, 1)
            high(0)
            high(1)
            for g in range(NG):
                if g + 2 < NG:
                    high(g + 2)
                act.wait_ge(tdone.sem, tdone.at(g + 1))
                if g >= 2:
                    act.wait_ge(gated.sem, gated.at(g - 1))
                nc.scalar.copy(yT[:, g % 2, 0].rearrange("p k i t -> p (k i t)"),
                               ps[:, 5 * (g % 2), :].bitcast(F16)).then_inc(yready[0].sem, 1)
            act.wait_ge(shifted.sem, shifted.at(1))
            nc.scalar.activation(prob[:], logits[:], ACT.Exp).then_inc(split.sem, 1)

        @block.vector
        def _(dve):
            link = linker(dve, chain)
            v = nc.vector
            link(v.memset(one[:], 1.0))
            for first, end in BATCHES:
                for t in range(first, end):
                    ins = v.bn_stats(bn[:, t, :], m.x[:, t, :])
                link(ins)
                for t in range(first, end):
                    ins = v.bn_aggr(mv[:, t, :], bn[:, t, :])
                link(ins)
                link(v.tensor_scalar(var_[:, first:end], mv[:, first:end, 1], EPS, 1.0 / (YS * YS), ALU.add, ALU.mult))
                guess_root(nc, link, var_[:, first:end], rstd_[:, first:end]).then_inc(var.sem, 1)
            link(v.tensor_scalar(wgp[:, 0], m.wg[:], WS, None, ALU.mult))
            link(v.scalar_tensor_tensor(out=wgp[:, 1], in0=m.wg[:], scalar=WS, in1=wgp[:, 0], op0=ALU.mult, op1=ALU.subtract))
            def apply(g):
                dve.wait_ge(rstd.sem, rstd.at(1 if g == 0 else 2))
                for i in range(GT):
                    t = g * GT + i
                    ins = v.tensor_scalar(y[:, g, i, :], m.x[:, t, :], mv[:, t, 0:1], rstd_[:, t:t + 1], ALU.subtract, ALU.mult)
                ins.then_inc(normed.sem, 1)

            def low_part(g):
                r = rows[:, g * GT:(g + 1) * GT, :]
                dve.wait_ge(split.sem, split.at(g + 1))
                v.tensor_tensor(r[:, :, D:2 * D], y[:, g], r[:, :, 0:D], ALU.subtract).then_inc(low[0].sem, 1)

            def copy_low(g):
                dve.wait_ge(tdone.sem, tdone.at(g + 1))
                if g >= 2:
                    dve.wait_ge(gated.sem, gated.at(g - 1))
                v.tensor_copy(yT[:, g % 2, 1].rearrange("p k i t -> p (k i t)"),
                              ps[:, 5 * (g % 2) + 1, :].bitcast(F16)).then_inc(yready[1].sem, 1)
            apply(0)
            low_part(0)
            for g in range(1, NG):
                apply(g)
            copy_low(0)
            low_part(2)
            for g in range(1, NG):
                copy_low(g)

            def over(t, shape=(P, NT, NE)):
                return t[:, :, None].broadcast_to(list(shape))
            dve.wait_ge(gated.sem, gated.at(NG))
            iota = m.eiota[:, None, :].broadcast_to([P, NT, NE])
            link(v.scalar_tensor_tensor(out=logits[:], in0=ps[:, 2, 0:NT * NE].rearrange("p (t e) -> p t e", e=NE),
                                        scalar=1.0 / (YS * WS), in1=m.bg[:, None, :].broadcast_to([P, NT, NE]),
                                        op0=ALU.mult, op1=ALU.add))
            link(v.tensor_reduce(mx[:], logits[:], AX.X, ALU.max))
            v.tensor_tensor(logits[:], logits[:], over(mx), ALU.subtract).then_inc(shifted.sem, 1)
            dve.wait_ge(split.sem, split.at(NG + 1))
            link(v.tensor_reduce(rs[:], prob[:], AX.X, ALU.add))
            link(v.reciprocal(rs[:], rs[:]))
            link(v.tensor_tensor(prob[:], prob[:], over(rs), ALU.mult))
            for n, (w, idx, hot) in enumerate(((w1, i1, h1), (w2, i2, h2))):
                link(v.tensor_reduce(w[:], prob[:], AX.X, ALU.max))
                link(v.tensor_tensor(eq[:], prob[:], over(w), ALU.is_equal))
                link(v.scalar_tensor_tensor(out=cand[:], in0=eq[:], scalar=-float(NE), in1=iota, op0=ALU.mult, op1=ALU.add))
                link(v.tensor_reduce(idx[:], cand[:], AX.X, ALU.min))
                link(v.tensor_scalar(idx[:], idx[:], float(NE), None, ALU.add))
                link(v.tensor_tensor(hot[:], iota, over(idx), ALU.is_equal))
                link(v.tensor_scalar(m.weight[:, :, n], w[:], 0.5, None, ALU.mult))
                if n == 0:
                    link(v.scalar_tensor_tensor(out=prob[:], in0=hot[:], scalar=-2.0, in1=prob[:], op0=ALU.mult, op1=ALU.add))
            v.tensor_tensor(both[:], h1[:], h2[:], ALU.add).then_inc(chosen.sem, 1)
            dve.wait_ge(counted.sem, counted.at(1))
            total = cand
            link(v.tensor_copy(total[:], ps[:, 4, 0:NT * NE].rearrange("p (t e) -> p t e", e=NE)))
            for e in range(NE):
                ins = v.tensor_tensor_scan(logits[:, :, e], one[:], total[:, :, e], 0.0, ALU.mult, ALU.add)
            link(ins)
            n_, pad, end, start, up, rem = (ends[:, k, :] for k in range(6))
            link(v.tensor_scalar(up, logits[:, NT - 1, :], float(P - 1), None, ALU.add))
            link(v.tensor_scalar(rem.bitcast(I32), up, 0.0, None, ALU.add))
            link(v.tensor_scalar(rem.bitcast(I32), rem.bitcast(I32), 7, None, ALU.arith_shift_right))
            link(v.tensor_scalar(pad, rem.bitcast(I32), float(P), None, ALU.mult))
            link(v.tensor_tensor_scan(end, one[:, 0:NE], pad, 0.0, ALU.mult, ALU.add))
            link(v.tensor_tensor(start, end, pad, ALU.subtract))
            link(v.tensor_tensor(base[:], logits[:], total[:], ALU.subtract))
            link(v.tensor_tensor(base[:], base[:], start[:, None, :].broadcast_to([P, NT, NE]), ALU.add))
            link(v.tensor_tensor(base[:], ps[:, 3, 0:NT * NE].rearrange("p (t e) -> p t e", e=NE), base[:], ALU.add))
            for n, hot in enumerate((h1, h2)):
                link(v.tensor_tensor(eq[:], hot[:], base[:], ALU.mult))
                link(v.tensor_reduce(slot[:, n, :], eq[:], AX.X, ALU.add))
            nt = SLOT_TILES
            link(v.tensor_copy(shift[:], slot[:]))
            link(v.tensor_scalar(shift[:], shift[:], 7, None, ALU.arith_shift_right))
            link(v.tensor_copy(tile_of[:], shift[:]))
            link(v.scalar_tensor_tensor(out=row_of[:], in0=tile_of[:], scalar=-float(P), in1=slot[:], op0=ALU.mult, op1=ALU.add))
            dve.wait_ge(constants.sem, constants.at(16 * 3))
            dve.wait_ge(split.sem, split.at(NG))
            dve.wait_ge(low[0].sem, low[0].at(NG // 2))
            dve.wait_ge(low[1].sem, low[1].at(NG // 2))
            for n in range(TOPK):
                ids, marks = ontile[:, n, :, 0, :], ontile[:, n, :, 1, :]
                v.tensor_tensor(onrow[:, n], numbers[:, None, :].broadcast_to([P, NT, P]),
                                row_of[:, n, :, None].broadcast_to([P, NT, P]), ALU.is_equal)
                link(v.tensor_tensor(marks, numbers[:, None, 0:nt].broadcast_to([P, NT, nt]),
                                     tile_of[:, n, :, None].broadcast_to([P, NT, nt]), ALU.is_equal))
                link(v.tensor_tensor(ids, marks, tokens[:, :, None].broadcast_to([P, NT, nt]), ALU.mult))
                v.tensor_scalar(marks, marks, 1.0 + n, None, ALU.mult).then_inc(turned.sem, 1)
            link(v.tensor_tensor(te[:, 0, 0:nt, :], end[0:1, None, :].broadcast_to([1, nt, NE]),
                                 m.starts[0:1, :, None].broadcast_to([1, nt, NE]), ALU.is_le))
            link(v.tensor_reduce(tr[:, 0, 0:nt], te[:, 0, 0:nt, :], AX.X, ALU.add))
            link(v.tensor_scalar(m.tile_expert[:], tr[:, 0, 0:nt], float(NE - 1), None, ALU.min))
            dve.wait_ge(inverted.sem, inverted.at(1))
            token, which = ps[:, 7, 0:nt], ps[:, 7, nt:2 * nt]
            v.tensor_copy(m.slot_token[:], token)
            link(v.tensor_scalar(used[:, 0, :], token, -float(T), None, ALU.add))
            link(v.scalar_tensor_tensor(out=used[:, 0, :], in0=which, scalar=float(T), in1=used[:, 0, :], op0=ALU.mult, op1=ALU.add))
            link(v.tensor_scalar(used[:, 1, :], which, 0.0, None, ALU.is_equal))
            link(v.tensor_tensor(used[:, 1, :], used[:, 1, :], spare[:], ALU.mult))
            v.tensor_tensor(m.slot_out[:], used[:, 0, :], used[:, 1, :], ALU.add)

        @block.gpsimd
        def _(pool):
            link = linker(pool, pchain)
            for n, (first, end) in enumerate(BATCHES):
                pool.wait_ge(var.sem, var.at(n + 1))
                refine_root(nc, link, var_[:, first:end], rstd_[:, first:end], work[:, first:end]).then_inc(rstd.sem, 1)
            for g in range(1, NG, 2):
                r = rows[:, g * GT:(g + 1) * GT, :]
                pool.wait_ge(split.sem, split.at(g + 1))
                nc.gpsimd.tensor_tensor(r[:, :, D:2 * D], y[:, g], r[:, :, 0:D], ALU.subtract).then_inc(low[1].sem, 1)
        for s, n in ((var, 2), (rstd, 2), (low[0], NG // 2), (low[1], NG // 2), (normed, NG), (tdone, NG), (yready[0], NG), (yready[1], NG),
                     (gated, NG), (shifted, 1),
                     (chosen, 1), (counted, 1), (constants, 48), (turned, 2), (inverted, 1), (sent, 16 * NG), (split, NG + 1),
                     (chain, chain.links), (pchain, pchain.links)):
            s.phase_over(n)


def expert_phase(nc, m, a, sig):
    with ExitStack() as ctx:
        sb = buffers(nc, ctx)
        xt = sb("ex_rows", [P, 2, 2 * D], F16)
        yT = sb("ex_yT", [P, 2, 2, KD, P], F16)
        wr = sb("ex_weights", [P, 2, EXPERT_COLS], F16)
        bb = sb("ex_biases", [P, 2, 2, KH], F32)
        g32 = sb("ex_gelu", [P, 2, KH, P], F32)
        gp = sb("ex_gelu_parts", [P, 2, 2, 2, KH, P], F16)
        eo = sb("ex_out", [P, 2, D], F32)
        b3 = sb("ex_b3", [P, NE, D], F32)
        b3_loaded = sig("ex_b3_loaded")
        loaded = [sig("ex_rows_loaded_even"), sig("ex_rows_loaded_odd")]
        stored = [sig("ex_out_stored_even"), sig("ex_out_stored_odd")]
        tdone, yready, out_ready = sig("ex_transposed"), sig("ex_yT_ready"), sig("ex_out_ready")
        wready = [sig(f"ex_w{n}_ready") for n in (1, 2, 3)]
        layer = [sig(f"ex_layer{n}_done") for n in (1, 2, 3)]
        gelu = [sig(f"ex_gelu{n}_done") for n in (1, 2)]
        hi = [sig(f"ex_hi{n}_ready") for n in (1, 2)]
        lo = [sig(f"ex_lo{n}_ready") for n in (1, 2)]
        ps = m.ps
        views = [expert_views(wr[:, n, :]) for n in range(2)]
        block = ctx.enter_context(nc.Block())
        N = SLOT_TILES
        FIRST, UNROLL = 4, 4
        OUTER = (N - 2 - FIRST) // UNROLL
        AT = (0, 2 * W1_COLS, 2 * (W1_COLS + W2_COLS), EXPERT_COLS)

        def run(eng, body):
            def peeled(i):
                body(i, i % 2, i // 2, lambda o: 0 <= i + o < N)
            for i in range(FIRST):
                peeled(i)
            with eng.Fori(0, OUTER) as j:
                for u in range(UNROLL):
                    body(j * UNROLL + (FIRST + u), u % 2, j * (UNROLL // 2) + (FIRST + u) // 2, lambda o: True)
            for i in range(FIRST + UNROLL * OUTER, N + 2):
                peeled(i)

        @block.sync
        def _(sp):
            for e in range(NE):
                sp.dma_start(b3[:, e, :], a["L1_ffn_b3"][e:e + 1, :].broadcast_to([P, D])).then_inc(b3_loaded.sem, 16)

        @block.gpsimd
        def _(pool):
            for i in range(-2, N + 2):
                if i + 2 < N:
                    if i >= 0:
                        pool.wait_ge(tdone.sem, tdone.at(i + 1))
                    pool.indirect_dma_start(out=xt[:, i % 2, :], out_offset=None, in_=a["moe_rows"][:, :],
                                            in_offset=bass.IndirectOffsetOnAxis(ap=m.slot_token[:, i + 2:i + 3], axis=0)
                                            ).then_inc(loaded[i % 2].sem, 16)
                if i >= 2:
                    pool.wait_ge(out_ready.sem, out_ready.at(i - 1))
                    pool.indirect_dma_start(out=a["moe_out"][:, :],
                                            out_offset=bass.IndirectOffsetOnAxis(ap=m.slot_out[:, i - 2:i - 1], axis=0),
                                            in_=eo[:, i % 2, :], in_offset=None).then_inc(stored[i % 2].sem, 16)
            for par in range(2):
                pool.wait_ge(stored[par].sem, stored[par].at(16 * ((N + 1 - par) // 2)))

        @block.tensor
        def _(pe):
            def transposes(i, par, half):
                o = 1 - par
                if due((half + 1 + par) * 16):
                    pe.wait_ge(loaded[o].sem, loaded[o].at((half + 1 + par) * 16))
                if due(i):
                    pe.wait_ge(yready.sem, yready.at(i))
                bank = ps[:, o, :].bitcast(F16)
                for c in range(2 * KD):
                    last = pe.transpose(bank[:, c * P:(c + 1) * P], xt[:, o, c * P:(c + 1) * P], m.ident16[:])
                last.then_inc(tdone.sem, 1)

            def wide(bank, w, act, kn, done):
                for mo in range(KH):
                    for k in range(kn):
                        for n, (pw, pa) in enumerate(((0, 0), (0, 1), (1, 0))):
                            last = pe.matmul(bank[:, mo * P:(mo + 1) * P], w[:, pw, k, mo * P:(mo + 1) * P],
                                             act[:, pa, k, :], start=(k == 0 and n == 0), stop=(k == kn - 1 and n == 2))
                last.then_inc(done.sem, 1)

            def body(i, par, half, stage):
                if stage(0):
                    pe.wait_ge(yready.sem, yready.at(i + 1))
                    pe.wait_ge(wready[0].sem, wready[0].at(i + 1))
                    if due(i - 1):
                        pe.wait_ge(gelu[0].sem, gelu[0].at(i - 1))
                    wide(ps[:, 2 + par, :], views[par][0], yT[:, par], KD, layer[0])
                if stage(1):
                    transposes(i, par, half)
                if stage(-1):
                    if due(i):
                        pe.wait_ge(lo[0].sem, lo[0].at(i))
                    if due(i):
                        pe.wait_ge(wready[1].sem, wready[1].at(i))
                    if due(i - 2):
                        pe.wait_ge(gelu[1].sem, gelu[1].at(i - 2))
                    wide(ps[:, 5 - par, :], views[1 - par][1], gp[:, 0, 1 - par], KH, layer[1])
                if stage(-2):
                    if due(i - 1):
                        pe.wait_ge(lo[1].sem, lo[1].at(i - 1))
                    if due(i - 1):
                        pe.wait_ge(wready[2].sem, wready[2].at(i - 1))
                    if due(i - 3):
                        pe.wait_ge(out_ready.sem, out_ready.at(i - 3))
                    for k in range(KH):
                        for n, (pw, pa) in enumerate(((0, 0), (1, 0), (0, 1))):
                            last = pe.matmul(ps[:, 6 + par, 0:D], gp[:, 1, par, pa, k, :], views[par][2][:, pw, k, :],
                                             start=(k == 0 and n == 0), stop=(k == KH - 1 and n == 2))
                    last.then_inc(layer[2].sem, 1)
            transposes(-1, 1, -1)
            run(pe, body)

        @block.scalar
        def _(act):
            def layer_out(n, t, par, bank, scale, parts_free):
                act.wait_ge(layer[n].sem, layer[n].at(t + 1))
                if due(t):
                    act.wait_ge(lo[n].sem, lo[n].at(t))
                for c in range(KH):
                    last = nc.scalar.activation(g32[:, n, c, :], bank[:, c * P:(c + 1) * P], ACT.Gelu,
                                                bias=bb[:, par, n, c:c + 1], scale=scale)
                last.then_inc(gelu[n].sem, 1)
                act.wait_ge(gelu[n].sem, gelu[n].at(t + 1))
                if due(t - 1):
                    act.wait_ge(parts_free.sem, parts_free.at(t - 1))
                nc.scalar.copy(gp[:, n, par, 0], g32[:, n]).then_inc(hi[n].sem, 1)

            def body(i, par, half, stage):
                if stage(0):
                    layer_out(0, i, par, ps[:, 2 + par, :], 1.0 / (YS * WS), layer[1])
                if stage(-1):
                    layer_out(1, i - 1, 1 - par, ps[:, 5 - par, :], 1.0 / WS, layer[2])
            run(act, body)

        @block.vector
        def _(dve):
            v = nc.vector

            def expert_of(t):
                if isinstance(t, int):
                    return dve.value_load(m.tile_expert[0:1, t:t + 1], min_val=0, max_val=NE - 1)
                return dve.value_load(m.tile_expert[0:1, bass.ds(t, 1)], min_val=0, max_val=NE - 1)

            def weights(n, t, par):
                e = expert_of(t)
                flat = m.we[:].rearrange("p e c -> p (e c)")
                if due(t - 1):
                    dve.wait_ge(layer[n].sem, layer[n].at(t - 1))
                if n < 2:
                    if due(t - 1):
                        dve.wait_ge(gelu[n].sem, gelu[n].at(t - 1))
                    v.tensor_copy(bb[:, par, n, :], m.eb12[:].rearrange("p e n c -> p (e n c)")[:, bass.ds(e * (2 * KH) + n * KH, KH)])
                c = AT[n + 1] - AT[n]
                v.tensor_copy(wr[:, par, AT[n]:AT[n + 1]], flat[:, bass.ds(e * EXPERT_COLS + AT[n], c)]).then_inc(wready[n].sem, 1)

            def low(n, t, par):
                dve.wait_ge(hi[n].sem, hi[n].at(t + 1))
                v.tensor_tensor(gp[:, n, par, 1], g32[:, n], gp[:, n, par, 0], ALU.subtract).then_inc(lo[n].sem, 1)

            def yT_copy(t, par):
                dve.wait_ge(tdone.sem, tdone.at(t + 1))
                if due(t - 1):
                    dve.wait_ge(layer[0].sem, layer[0].at(t - 1))
                v.tensor_copy(yT[:, par].rearrange("p s k t -> p (s k t)"), ps[:, par, 0:D].bitcast(F16)).then_inc(yready.sem, 1)

            weights(0, 0, 0)
            yT_copy(0, 0)
            dve.wait_ge(b3_loaded.sem, b3_loaded.at(16 * NE))

            def body(i, par, half, stage):
                if stage(1):
                    weights(0, i + 1, 1 - par)
                if stage(0):
                    weights(1, i, par)
                if stage(-1):
                    weights(2, i - 1, 1 - par)
                if stage(1):
                    yT_copy(i + 1, 1 - par)
                if stage(0):
                    low(0, i, par)
                if stage(-1):
                    low(1, i - 1, 1 - par)
                if stage(-2):
                    e = expert_of(i - 2)
                    if due(i - 1):
                        dve.wait_ge(layer[2].sem, layer[2].at(i - 1))
                    if not isinstance(half, int) or half > 1:
                        dve.wait_ge(stored[par].sem, stored[par].at((half - 1) * 16))
                    v.scalar_tensor_tensor(out=eo[:, par, :], in0=ps[:, 6 + par, 0:D], scalar=1.0 / WS,
                                           in1=b3[:].rearrange("p e d -> p (e d)")[:, bass.ds(e * D, D)],
                                           op0=ALU.mult, op1=ALU.add).then_inc(out_ready.sem, 1)
            run(dve, body)
        for s in [tdone, yready, out_ready] + wready + layer + gelu + hi + lo:
            s.phase_over(N)
        b3_loaded.phase_over(16 * NE)
        for par in range(2):
            loaded[par].phase_over(16 * ((N + 1 - par) // 2))
            stored[par].phase_over(16 * ((N + 1 - par) // 2))


def combine_phase(nc, m, a, sig):
    with ExitStack() as ctx:
        sb = buffers(nc, ctx)
        R, W = 4, 2
        got = sb("co_rows", [P, R, TOPK, W, D], F32)
        here = [sig(f"co_rows_here{n}") for n in range(R)]
        added = sig("co_added")
        stored = sig("x_loaded")
        out = a["out"].rearrange("b s d -> (b s) d").rearrange("(i p) d -> p i d", p=P)
        rows = a["moe_out"][0:TOPK * T, :].rearrange("(n i p) d -> p n i d", n=TOPK, p=P)
        block = ctx.enter_context(nc.Block())

        @block.sync
        def _(sp):
            for u in range(NT // W):
                if u >= R:
                    sp.wait_ge(added.sem, TOPK * W * (u - R + 1))
                for n in range(TOPK):
                    sp.dma_start(got[:, u % R, n], rows[:, n, u * W:(u + 1) * W, :]).then_inc(here[u % R].sem, 16)

        @block.scalar
        def _(act):
            for u in range(NT // W):
                act.wait_ge(added.sem, TOPK * W * (u + 1))
                act.dma_start(out[:, u * W:(u + 1) * W, :], m.x[:, u * W:(u + 1) * W, :]).then_inc(stored.sem, 16)
            act.wait_ge(stored.sem, stored.at(16 * NT // W))

        @block.vector
        def _(dve):
            for u in range(NT // W):
                dve.wait_ge(here[u % R].sem, here[u % R].at(16 * TOPK * (u // R + 1)))
                for n in range(TOPK):
                    for t in range(u * W, (u + 1) * W):
                        nc.vector.scalar_tensor_tensor(out=m.x[:, t, :], in0=got[:, u % R, n, t - u * W, :],
                                                       scalar=m.weight[:, t, n:n + 1], in1=m.x[:, t, :],
                                                       op0=ALU.mult, op1=ALU.add).then_inc(added.sem, 1)
                    dve.wait_ge(added.sem, TOPK * W * u + (n + 1) * W)


def moe_phases(nc, m, a, sig):
    routing_phase(nc, m, a, sig)
    expert_phase(nc, m, a, sig)


def retention_phase(nc, m, a, sig):
    with ExitStack() as ctx:
        sb = buffers(nc, ctx)
        HC = NH // KD
        wqkvg = sb("re_w_qkvg", [P, 2, KD, 4 * D], F16)
        wproj = sb("re_w_proj", [P, KD, D], F32)
        gn = sb("re_gn", [P, 2, D], F32)
        decay = sb("re_decay", [P, NH, P], F32)
        qdec = sb("re_q_decay", [P, KD, P], F32)
        kdec = sb("re_k_decay", [P, D], F32)
        heads = sb("re_head_rows", [P, HC], F32)
        sdec = sb("re_state_decay", [P, KD], F32)
        rot = sb("re_rotation", [P, 2, D], F32)
        y = sb("re_y", [P, 1, D], F32)
        yp = y[:, 0, :].bitcast(F16).rearrange("p (s d) -> p s d", s=2)
        yT = sb("re_yT", [P, 2, KD, P], F16)
        qk = sb("re_qk", [P, 2, D], F32)
        t2 = sb("re_swapped", [P, 2, D], F32)
        V = sb("re_v", [P, 2, NH, HP], F32)
        gate = sb("re_gate", [P, 2, D], F32)
        qT = sb("re_qT", [P, KD, P], F32)
        kT = sb("re_kT", [P, 2, KD, P], F32)
        qdT = sb("re_q_decayed", [P, KD, P], F32)
        kd = sb("re_k_decayed", [P, D], F32)
        qx = sb("re_q_by_head", [P, KD, HC, P], F32)
        raw = qx[:].rearrange("p k h t -> p (k h t)").rearrange("p (k n) -> p k n", k=KD)
        pt = sb("re_weights", [P, 2, HC // 2, P], F32)
        state = sb("re_state", [P, KD, HC * HP], F32)
        upd = t2
        oT = sb("re_oT", [P, 4 * P], F32)
        cent = sb("re_centred", [P, NH, HD], F32)
        sq = t2[:, 0, :].rearrange("p (h d) -> p h d", h=NH)
        roots = sb("re_roots", [P, 3, 1 + NH], F32)
        sums = sb("re_sums", [P, NH], F32)
        nT = y[:, 0, :].rearrange("p (k t) -> p k t", k=KD)
        got = sb("re_expert_rows", [P, TOPK, D], F32)
        names = ("loaded wloaded whigh wsplit rot cleared combined guessed rooted normed yturned yT qkproj vgproj rotated "
                 "vready gated qkturned qkT qdT kd qx0 qx1 scored weighed retained updated stated oT oturned centred "
                 "mixed nturned nT projected added chain pchain").split()
        g = {n: sig("re_" + n) for n in names}
        here = sig("co_rows_here0")
        ps = m.ps
        v, pl = nc.vector, nc.gpsimd
        N = NT

        def rooted(i):
            return slice(0 if i + 1 < N else 1, 1 + NH if 0 <= i - 2 < N else 1)
        block = ctx.enter_context(nc.Block())
        NLOAD = 8

        @block.sync
        def _(sp):
            kp = "(k p) n -> p k n"
            row = lambda w: w.rearrange("(a d) -> a d", a=1).broadcast_to([P, D])
            expert_rows = a["moe_out"][0:TOPK * T, :].rearrange("(n i p) d -> i p n d", n=TOPK, p=P)
            sp.dma_start(got[:], expert_rows[0]).then_inc(here.sem, 16)
            for dst, src in ((raw[:, :, 0:3 * D], a["L1_attn_w_qkv"]), (raw[:, :, 3 * D:], a["L1_attn_w_g"])):
                sp.dma_start(dst, src.rearrange(kp, p=P)).then_inc(g["wloaded"].sem, 16)
            for dst, src in ((wproj[:], a["L1_attn_w_proj"].rearrange(kp, p=P)),
                             (gn[:, 0, :], row(a["L1_attn_gn_weight"])), (gn[:, 1, :], row(a["L1_attn_gn_bias"])),
                             (decay[:], a["c_decay"]), (qdec[:], a["c_q_decay"]), (kdec[:], a["c_k_decay"]),
                             (heads[:], a["c_head_rows"]), (sdec[:], a["c_state_decay"])):
                sp.dma_start(dst, src).then_inc(g["loaded"].sem, 16)
            for i in range(N):
                if i + 1 < N:
                    sp.wait_ge(g["combined"].sem, i + 1)
                    sp.dma_start(got[:], expert_rows[i + 1]).then_inc(here.sem, 16)
                if i > 0:
                    sp.wait_ge(g["rotated"].sem, i)
                sp.dma_start(rot[:], a["c_rotation"][i % BT]).then_inc(g["rot"].sem, 16)
            sp.wait_ge(g["loaded"].sem, 16 * NLOAD)

        @block.tensor
        def _(pe):
            pe.wait_ge(g["loaded"].sem, 16 * NLOAD)
            pe.wait_ge(g["wsplit"].sem, 1)
            for i in range(N + 3):
                r, o, q = i - 1, i - 2, i - 3
                if i < N:
                    pe.wait_ge(g["normed"].sem, i + 1)
                    if 0 < q:
                        pe.wait_ge(g["nT"].sem, q)
                    for n in range(2 * KD):
                        last = pe.transpose(ps[:, 0, :].bitcast(F16)[:, n * P:(n + 1) * P], yp[:, n // KD, n % KD * P:(n % KD + 1) * P],
                                            m.ident16[:])
                    last.then_inc(g["yturned"].sem, 1)

                def scores(p):
                    c, n = p // 2, 4 * r + p
                    if p % 2 == 0:
                        pe.wait_ge(g["qx" + str(c)].sem, r + 1)
                    if n >= 2:
                        pe.wait_ge(g["weighed"].sem, n - 1)
                    pe.matmul(ps[:, 4 + p % 2, :], kT[:, r % 2, c, :], qx[:, c, p % 2 * 4:p % 2 * 4 + 4, :],
                              start=True, stop=True).then_inc(g["scored"].sem, 1)

                def retain(p):
                    c, n = p // 2, 4 * r + p
                    pe.wait_ge(g["weighed"].sem, n + 1)
                    if p == 0:
                        if r > 0:
                            pe.wait_ge(g["oT"].sem, r)
                            pe.wait_ge(g["stated"].sem, r)
                        pe.wait_ge(g["qdT"].sem, r + 1)
                        pe.wait_ge(g["vready"].sem, r + 1)
                    pe.matmul(ps[:, 6, p * P:(p + 1) * P], state[:, c, p % 2 * P:(p % 2 + 1) * P], qdT[:, c, :], start=True,
                              stop=False, skip_group_check=True)
                    for h in range(4):
                        last = pe.matmul(ps[h * HP:(h + 1) * HP, 6, p * P:(p + 1) * P], V[:, r % 2, p * 4 + h, :],
                                         pt[:, p % 2, h, :], start=False, stop=True, skip_group_check=True)
                    last.then_inc(g["retained"].sem, 1)

                def project(n, projected):
                    products = [(k, pw, py) for k in range(KD) for pw, py in ((0, 0), (0, 1), (1, 0))]
                    for j, (k, pw, py) in enumerate(products):
                        last = pe.matmul(ps[:, 1 + n, :], yT[:, py, k, :], wqkvg[:, pw, k, n * 512:(n + 1) * 512],
                                         start=(j == 0), stop=(j == len(products) - 1))
                    last.then_inc(projected.sem, 1)

                if 0 <= r < N:
                    scores(0)
                    scores(1)
                if 0 <= o < N:
                    pe.wait_ge(g["oT"].sem, o + 1)
                    pe.wait_ge(g["stated"].sem, o + 1)
                    for n in range(4):
                        last = pe.transpose(ps[:, 7, n * P:(n + 1) * P], oT[:, n * P:(n + 1) * P], m.ident[:])
                    last.then_inc(g["oturned"].sem, 1)
                if 0 <= q:
                    pe.wait_ge(g["mixed"].sem, q + 1)
                    pe.wait_ge(g["yT"].sem, min(N, i + 1))
                    for k in range(KD):
                        last = pe.transpose(ps[:, 0, k * P:(k + 1) * P], cent[:, k * 8:(k + 1) * 8, :].rearrange("p h d -> p (h d)"), m.ident[:])
                    last.then_inc(g["nturned"].sem, 1)
                if i < N:
                    pe.wait_ge(g["yT"].sem, i + 1)
                    if i > 0:
                        pe.wait_ge(g["rotated"].sem, i)
                    project(0, g["qkproj"])
                if 0 <= r < N:
                    retain(0)
                    scores(2)
                if 0 <= q:
                    pe.wait_ge(g["nT"].sem, q + 1)
                    pe.wait_ge(g["qkT"].sem, min(N, i))
                    if q > 0:
                        pe.wait_ge(g["added"].sem, q)
                    for k in range(KD):
                        last = pe.matmul(ps[:, 3, 0:D], nT[:, k, :], wproj[:, k, :], start=(k == 0), stop=(k == KD - 1))
                    last.then_inc(g["projected"].sem, 1)
                if i < N:
                    if i > 0:
                        pe.wait_ge(g["vready"].sem, i)
                        pe.wait_ge(g["gated"].sem, i)
                    project(1, g["vgproj"])
                if 0 <= r < N:
                    retain(1)
                    scores(3)
                if i < N:
                    pe.wait_ge(g["rotated"].sem, i + 1)
                    if q >= 0:
                        pe.wait_ge(g["added"].sem, q + 1)
                    for n in range(4):
                        last = pe.transpose(ps[:, 3, n * P:(n + 1) * P], qk[:, n // 2, (n % 2) * P:(n % 2 + 1) * P], m.ident[:])
                    last.then_inc(g["qkturned"].sem, 1)
                if 0 <= r < N:
                    retain(2)
                if 0 <= r < N:
                    retain(3)
                    pe.wait_ge(g["kd"].sem, r + 1)
                    if r > 0:
                        pe.wait_ge(g["centred"].sem, r)
                    for c in range(KD):
                        last = pe.matmul(ps[:, 7, c * HC * HP:(c + 1) * HC * HP], kd[:, c * P:(c + 1) * P],
                                         V[:, r % 2, c * HC:(c + 1) * HC, :].rearrange("p h d -> p (h d)"), start=True, stop=True)
                    last.then_inc(g["updated"].sem, 1)

        @block.scalar
        def _(act):
            act.wait_ge(g["wloaded"].sem, 32)
            nc.scalar.mul(wqkvg[:, 0], raw, WS).then_inc(g["whigh"].sem, 1)
            act.wait_ge(g["loaded"].sem, 16 * NLOAD)
            for i in range(N + 3):
                r, q = i - 1, i - 3
                if i < N:
                    act.wait_ge(g["yturned"].sem, i + 1)
                    if i > 0:
                        act.wait_ge(g["vgproj"].sem, i)
                    nc.scalar.copy(yT[:].rearrange("p s k t -> p (s k t)"), ps[:, 0, :].bitcast(F16)[:, 0:2 * D]).then_inc(g["yT"].sem, 1)
                if 0 <= q:
                    act.wait_ge(g["nturned"].sem, q + 1)
                    if q > 0:
                        act.wait_ge(g["projected"].sem, q)
                    nc.scalar.copy(y[:, 0, :], ps[:, 0, 0:D]).then_inc(g["nT"].sem, 1)
                if i < N:
                    act.wait_ge(g["vgproj"].sem, i + 1)
                    if i >= 2:
                        act.wait_ge(g["updated"].sem, i - 1)
                    act.wait_ge(g["cleared"].sem, 2)
                    nc.scalar.mul(V[:, i % 2, :, 0:HD], ps[:, 2, 0:D].rearrange("p (h d) -> p h d", h=NH), 1.0 / (YS * WS)).then_inc(g["vready"].sem, 1)
                    act.wait_ge(g["qkturned"].sem, i + 1)
                    if i >= 2:
                        act.wait_ge(g["scored"].sem, 4 * (i - 1))
                    nc.scalar.copy(kT[:, i % 2].rearrange("p k t -> p (k t)"), ps[:, 3, D:2 * D])
                    if i >= 1:
                        act.wait_ge(g["qx0"].sem, i)
                        act.wait_ge(g["qx1"].sem, i)
                        act.wait_ge(g["qdT"].sem, i)
                    nc.scalar.copy(qT[:].rearrange("p k t -> p (k t)"), ps[:, 3, 0:D]).then_inc(g["qkT"].sem, 1)
                if i < N:
                    if i >= 2:
                        act.wait_ge(g["mixed"].sem, i - 1)
                    nc.scalar.activation(gate[:, i % 2, :], ps[:, 2, D:2 * D], ACT.Silu,
                                         scale=1.0 / (YS * WS)).then_inc(g["gated"].sem, 1)
                if 0 <= r < N:
                    act.wait_ge(g["retained"].sem, 4 * r + 4)
                    if r > 0:
                        act.wait_ge(g["oturned"].sem, r)
                    nc.scalar.copy(oT[:], ps[:, 6, :]).then_inc(g["oT"].sem, 1)

        @block.vector
        def _(dve):
            link = linker(dve, g["chain"])
            v.memset(state[:], 0.0).then_inc(g["cleared"].sem, 1)
            v.memset(V[:], 0.0).then_inc(g["cleared"].sem, 1)
            dve.wait_ge(g["cleared"].sem, 2)

            def norm_step(t, step, alone):
                if step < TOPK:
                    if step == 0:
                        dve.wait_ge(here.sem, here.at(16 * (t + 1)))
                    return v.scalar_tensor_tensor(out=m.x[:, t, :], in0=got[:, step, :], scalar=m.weight[:, t, step:step + 1],
                                                  in1=m.x[:, t, :], op0=ALU.mult, op1=ALU.add)
                if step == 2:
                    if t > 0:
                        dve.wait_ge(g["normed"].sem, t)
                    v.bn_stats(m.bn[:, 0, :], m.x[:, t, :]).then_inc(g["combined"].sem, 1)
                    if alone:
                        dve.wait_ge(g["combined"].sem, t + 1)
                    return None
                if step == 3:
                    return v.bn_aggr(m.mv[:, 0, :], m.bn[:, 0, :])
                return v.tensor_scalar(roots[:, 0, 0:1], m.mv[:, 0, 1:2], EPS, 1.0 / (YS * YS), ALU.add, ALU.mult)

            def head_step(o, step):
                if step == 0:
                    dve.wait_ge(g["oturned"].sem, o + 1)
                    if o > 0:
                        dve.wait_ge(g["nturned"].sem, o)
                    return v.tensor_reduce(sums[:], heads_out, AX.X, ALU.add)
                if step == 1:
                    v.scalar_tensor_tensor(out=cent[:], in0=sums[:, :, None].broadcast_to([P, NH, HD]), scalar=-1.0 / HD,
                                           in1=heads_out, op0=ALU.mult, op1=ALU.add).then_inc(g["centred"].sem, 1)
                    dve.wait_ge(g["centred"].sem, o + 1)
                    return None
                if step == 2:
                    return v.tensor_tensor(sq, cent[:], cent[:], ALU.mult)
                if step == 3:
                    return v.tensor_reduce(sums[:], sq, AX.X, ALU.add)
                return v.tensor_scalar(roots[:, 0, 1:], sums[:], 1.0 / HD, EPS, ALU.mult, ALU.add)

            heads_out = ps[:, 7, :].rearrange("p (h d) -> p h d", h=NH)[:, :, 0:HD]

            def norm_end(t):
                dve.wait_ge(g["rooted"].sem, t + 1)
                if t > 0:
                    dve.wait_ge(g["yturned"].sem, t)
                if t > 0:
                    dve.wait_ge(g["rotated"].sem, t)
                whole = t2[:, 0, :]
                link(v.tensor_scalar(whole, m.x[:, t, :], m.mv[:, 0, 0:1], roots[:, 1, 0:1], ALU.subtract, ALU.mult))
                link(v.tensor_copy(yp[:, 0], whole))
                v.tensor_tensor(yp[:, 1], whole, yp[:, 0], ALU.subtract).then_inc(g["normed"].sem, 1)
            for step in range(5):
                last = norm_step(0, step, alone=True)
                if last is not None:
                    link(last)
            guess_root(nc, link, roots[:, 0, 0:1], roots[:, 1, 0:1]).then_inc(g["guessed"].sem, 1)
            norm_end(0)
            dve.wait_ge(g["wloaded"].sem, 32)
            dve.wait_ge(g["whigh"].sem, 1)
            v.scalar_tensor_tensor(out=wqkvg[:, 1], in0=raw, scalar=WS, in1=wqkvg[:, 0], op0=ALU.mult,
                                   op1=ALU.subtract).then_inc(g["wsplit"].sem, 1)
            dve.wait_ge(g["loaded"].sem, 16 * NLOAD)
            for i in range(N + 3):
                r, o, q = i - 1, i - 2, i - 3

                def weigh(p):
                    n = 4 * r + p
                    dve.wait_ge(g["scored"].sem, n + 1)
                    if n >= 2:
                        dve.wait_ge(g["retained"].sem, n - 1)
                    v.tensor_tensor(pt[:, p % 2], ps[:, 4 + p % 2, :].rearrange("p (h t) -> p h t", t=P),
                                    decay[:, 4 * p:4 * p + 4, :], ALU.mult).then_inc(g["weighed"].sem, 1)
                if 0 <= r < N:
                    weigh(0)
                    weigh(1)
                for step in range(5):
                    last = None
                    if i + 1 < N:
                        last = norm_step(i + 1, step, alone=not 0 <= o < N)
                    if 0 <= o < N:
                        last = head_step(o, step)
                    if last is not None:
                        link(last)
                if i + 1 < N or 0 <= o < N:
                    guess_root(nc, link, roots[:, 0, rooted(i)], roots[:, 1, rooted(i)]).then_inc(g["guessed"].sem, 1)
                if i < N:
                    rw = rot[:]
                    src = ps[:, 1, :].rearrange("p (n d) -> p n d", n=2)
                    pair = lambda t: t.rearrange("p n (d e) -> p n d e", e=2)
                    sin = rw[:, 1:2, :].rearrange("p n (d e) -> p n d e", e=2)
                    dve.wait_ge(g["qkproj"].sem, i + 1)
                    dve.wait_ge(g["rot"].sem, 16 * (i + 1))
                    if i > 0:
                        dve.wait_ge(g["qkturned"].sem, i)
                        dve.wait_ge(g["kd"].sem, i)
                    v.tensor_tensor(qk[:], src, rw[:, 0:1, :].broadcast_to([P, 2, D]), ALU.mult)
                    for e in range(2):
                        ins = v.tensor_tensor(pair(t2[:])[:, :, :, e], pair(src)[:, :, :, 1 - e],
                                              sin[:, :, :, e].broadcast_to([P, 2, D // 2]), ALU.mult)
                    link(ins)
                    v.tensor_tensor(qk[:], qk[:], t2[:], ALU.add).then_inc(g["rotated"].sem, 1)
                if 0 <= q:
                    dve.wait_ge(g["projected"].sem, q + 1)
                    xt = m.x[:, q, :]
                    v.tensor_tensor(xt, ps[:, 3, 0:D], xt, ALU.add).then_inc(g["added"].sem, 1)
                if 0 <= r < N:
                    weigh(2)
                    weigh(3)
                if i + 1 < N:
                    norm_end(i + 1)
                if i < N:
                    dve.wait_ge(g["qkT"].sem, i + 1)
                    if i > 0:
                        dve.wait_ge(g["scored"].sem, 4 * i - 2)
                    v.tensor_tensor(qx[:, 0], qT[:, 0:1, :].broadcast_to([P, HC, P]),
                                    heads[:, :, None].broadcast_to([P, HC, P]), ALU.mult).then_inc(g["qx0"].sem, 1)
                if 0 <= r < N:
                    dve.wait_ge(g["updated"].sem, r + 1)
                    dve.wait_ge(g["retained"].sem, 4 * r + 4)
                    if r % BT == BT - 1:
                        v.memset(state[:], 0.0).then_inc(g["stated"].sem, 1)
                    else:
                        if i + 1 < N:
                            dve.wait_ge(g["normed"].sem, i + 2)
                        link(v.tensor_tensor(upd[:].rearrange("p k (h d) -> p k h d", h=HC),
                                             ps[:, 7, :].rearrange("p (k h d) -> p k h d", k=KD, h=HC),
                                             heads[:, None, :, None].broadcast_to([P, KD, HC, HP]), ALU.mult))
                        for c in range(KD):
                            ins = v.scalar_tensor_tensor(out=state[:, c, :], in0=state[:, c, :], scalar=sdec[:, c:c + 1],
                                                         in1=upd[:, c, :], op0=ALU.mult, op1=ALU.add)
                        ins.then_inc(g["stated"].sem, 1)
                    dve.wait_ge(g["stated"].sem, r + 1)

        @block.gpsimd
        def _(pool):
            link = linker(pool, g["pchain"])
            pool.wait_ge(g["guessed"].sem, 1)
            refine_root(nc, link, *(roots[:, n, 0:1] for n in range(3))).then_inc(g["rooted"].sem, 1)
            pool.wait_ge(g["loaded"].sem, 16 * NLOAD)
            for i in range(N + 3):
                r, o = i - 1, i - 2
                if i + 1 < N or 0 <= o < N:
                    pool.wait_ge(g["guessed"].sem, i + 2)
                    refine_root(nc, link, *(roots[:, n, rooted(i)] for n in range(3))).then_inc(g["rooted"].sem, 1)
                    pool.wait_ge(g["rooted"].sem, i + 2)
                if 0 <= o < N:
                    flat = cent[:].rearrange("p h d -> p (h d)")
                    link(pl.tensor_tensor(cent[:], cent[:], roots[:, 1, 1:, None].broadcast_to([P, NH, HD]), ALU.mult))
                    link(pl.tensor_tensor(flat, flat, gn[:, 0, :], ALU.mult))
                    link(pl.tensor_tensor(flat, flat, gn[:, 1, :], ALU.add))
                    pool.wait_ge(g["gated"].sem, o + 1)
                    pl.tensor_tensor(flat, flat, gate[:, o % 2, :], ALU.mult).then_inc(g["mixed"].sem, 1)
                if i < N:
                    pool.wait_ge(g["rotated"].sem, i + 1)
                    if i > 0:
                        pool.wait_ge(g["scored"].sem, 4 * i)
                    pool.wait_ge(g["qkT"].sem, i + 1)
                    pl.tensor_tensor(qx[:, 1], qT[:, 1:2, :].broadcast_to([P, HC, P]),
                                     heads[:, :, None].broadcast_to([P, HC, P]), ALU.mult).then_inc(g["qx1"].sem, 1)
                    if r >= 0:
                        pool.wait_ge(g["updated"].sem, i)
                    pl.tensor_tensor(kd[:], qk[:, 1, :], kdec[:], ALU.mult).then_inc(g["kd"].sem, 1)
                    pl.tensor_tensor(qdT[:], qT[:], qdec[:], ALU.mult).then_inc(g["qdT"].sem, 1)
        here.phase_over(16 * NT)


def macaron(nc, a, stages=6, first=0):
    ctx = ExitStack()
    with ctx:
        sb = buffers(nc, ctx)

        USED.clear()
        sems = {}

        def sig(name):
            if name not in sems:
                sems[name] = Signal(ctx.enter_context(nc.semaphore(name)))
            return sems[name]

        m = Memory()
        m.x = sb("x", [P, NT, D], F32)
        m.ident = sb("ident", [P, P], F32)
        m.ident16 = sb("ident16", [P, P], F16)
        m.ones = sb("ones", [P, P], F32)
        m.bn = sb("bn_stats", [P, GT, 6], F32)
        m.mv = sb("bn_mean_var", [P, GT, 2], F32)
        m.var = sb("variance", [P, GT], F32)
        m.rstd = sb("rstd", [P, GT], F32)
        m.nt = sb("newton", [P, GT], F32)
        m.ps = ctx.enter_context(nc.psum_tensor("ps", [P, 8, 512], F32))
        a["qk_parts"] = nc.dram_tensor("qk_parts", (2, PARTS, D, T), BF16, kind="Internal").ap()
        a["moe_rows"] = nc.dram_tensor("moe_rows", (T, 2 * D), F16, kind="Internal").ap()
        a["moe_out"] = nc.dram_tensor("moe_out", (TOPK * T + SLOTS, D), F32, kind="Internal").ap()
        m.we = sb("expert_weights", [P, NE, EXPERT_COLS], F16)
        m.over = Overlay(m.we)
        m.eb12 = sb("expert_b12", [P, NE, 2, KH], F32)
        m.wg = sb("gate_w", [P, KD, NE], F32)
        m.bg = sb("gate_b", [P, NE], F32)
        m.tri = sb("before", [P, P], F32)
        m.eiota = sb("experts", [P, NE], F32)
        m.starts = sb("tile_starts", [1, SLOT_TILES], F32)
        m.slot_token = sb("slot_tokens", [P, SLOT_TILES], I32)
        m.slot_out = sb("slot_outputs", [P, SLOT_TILES], I32)
        m.weight = sb("mix_weights", [P, NT, TOPK], F32)
        m.tile_expert = sb("tile_expert", [1, SLOT_TILES], I32)
        with ExitStack() as inner:
            sb = buffers(nc, inner)
            m.b2h = sb("ffn_b2_half", [P, D], F32)
            m.b1T = sb("ffn_b1T", [P, NF], F32)
            m.w1qT = sb("w1qT", [P, KD, F0], F16)
            m.w2qT = sb("w2qT", [P, NF, D], F16)
            with ExitStack() as innermost:
                sb = buffers(nc, innermost)
                m.bqkT = sb("attn_bqkT", [P, 2, KD], F32)
                m.bvo = sb("attn_bvo", [P, 2, D], F32)
                m.awT = sb("attn_wT", [P, 4, KD, D], F32)
                m.mask_loaded = sb("causal_mask_loaded", [P, 2, P], F32)
                m.mask16 = sb("causal_mask", [P, 2, P], BF16)
                m.identb = sb("ident_bf16", [P, P], BF16)
                quantize_phase(nc, m, a, sig)
                if first <= 0 < stages:
                    ffn_phase(nc, m, a, sig, begun=True)
                if first <= 1 < stages:
                    transpose_weights_phase(nc, m, a, sig)
                    attend_phase(nc, m, a, sig)
                    out_projection_phase(nc, m, a, sig)
            if first <= 2 < stages:
                ffn_phase(nc, m, a, sig, experts=True, begun=True)
        if stages > 3:
            moe_phases(nc, m, a, sig)
            if stages > 4:
                retention_phase(nc, m, a, sig)
            if stages > 5:
                moe_phases(nc, m, a, sig)
            combine_phase(nc, m, a, sig)


def retention_constants():
    c = {}
    f = np.float32
    gamma = 1.0 - 2.0 ** (-5.0 - np.arange(NH, dtype=np.float64))
    i = np.arange(P)
    scale = HD ** -0.5
    late = i[None, None, :] - i[:, None, None]
    c["c_decay"] = np.where(late >= 0, gamma[None, :, None] ** np.maximum(late, 0) * scale, 0).astype(f)
    head = np.arange(D) // HD
    by_channel = gamma[head].reshape(KD, P).T
    c["c_q_decay"] = (by_channel[:, :, None] ** (i + 1)[None, None, :] * scale).astype(f)
    c["c_k_decay"] = (gamma[head][None, :] ** (P - 1 - i)[:, None]).astype(f)
    c["c_state_decay"] = (by_channel ** P).astype(f)
    own = (i[:, None] // HD) == np.arange(NH // KD)[None, :]
    c["c_head_rows"] = own.astype(f)
    pair = np.arange(0, D, 2, dtype=f)
    dim_scale = (pair + f(0.4 * D)) / f(1.4 * D)
    pos = np.arange(S, dtype=f)
    xs = dim_scale[None, :] ** (pos[:, None] / f(512.0))
    inv_freq = f(1.0) / f(10000.0) ** (pair / f(D))
    angle = pos[:, None] * inv_freq[None, :]
    sin, cos = np.sin(angle) * xs, np.cos(angle) * xs
    rotation = np.stack([np.repeat(cos, 2, axis=1), np.stack([-sin, sin], axis=-1).reshape(S, D)], axis=1)
    rotation = rotation / f(YS * WS)
    c["c_rotation"] = np.ascontiguousarray(rotation.reshape(BT, P, 2, D).astype(f))
    return c


def constants():
    c = {}
    c["c_ident"] = np.eye(P, dtype=np.float32)
    q, k = np.arange(P)[:, None], np.arange(P)[None, :]
    c["c_mask"] = np.stack([np.where(k > q, NEG, 0), np.where(q > k, NEG, 0)], axis=1).astype(np.float32)
    c["c_before"] = (q < k).astype(np.float32)
    c["c_experts"] = np.broadcast_to(np.arange(NE, dtype=np.float32), (P, NE)).copy()
    c["c_numbers"] = np.broadcast_to(np.arange(P, dtype=np.float32), (P, P)).copy()
    c["c_tokens"] = np.arange(T, dtype=np.float32).reshape(NT, P).T.copy()
    c["c_spare_rows"] = (np.arange(SLOTS, dtype=np.float32).reshape(SLOT_TILES, P).T + (TOPK + 1) * T).copy()
    c["c_tile_starts"] = (np.arange(SLOT_TILES, dtype=np.float32) * P)[None]
    c.update(retention_constants())
    return c


_INS = ['L0_attn_h', 'L0_attn_Wq', 'L0_attn_bq', 'L0_attn_Wk', 'L0_attn_bk', 'L0_attn_Wv', 'L0_attn_bv', 'L0_attn_Wo',
        'L0_attn_bo', 'L0_ffn_w1', 'L0_ffn_b1', 'L0_ffn_w2', 'L0_ffn_b2', 'L1_attn_w_qkv', 'L1_attn_w_g',
        'L1_attn_w_proj', 'L1_attn_gn_weight', 'L1_attn_gn_bias', 'L1_ffn_W1', 'L1_ffn_b1', 'L1_ffn_W2', 'L1_ffn_b2',
        'L1_ffn_W3', 'L1_ffn_b3', 'L1_ffn_Wg', 'L1_ffn_bg']


def kernel(**inputs):
    import concourse.bacc as _bacc
    from concourse import mybir as _mybir
    from concourse.bass_utils import run_bass_kernel_spmd as _run

    nc = _bacc.Bacc("TRN2", target_bir_lowering=False, num_devices=1)
    arrays, aps = {}, {}
    given = {name: np.ascontiguousarray(inputs[name]) for name in _INS}
    given.update(constants())
    for name, v in given.items():
        arrays[f"in_{name}"] = v
        aps[name] = nc.dram_tensor(f"in_{name}", v.shape, _mybir.dt.from_np(v.dtype), kind="ExternalInput").ap()
    aps["out"] = nc.dram_tensor("out_x", (B, S, D), F32, kind="ExternalOutput").ap()
    macaron(nc, aps)
    r = _run(nc, [arrays], core_ids=[0])
    return r.results[0]["out_x"]
```
